# Optimizing a Trainium2 kernel written in Bass

```python
import numpy as np
import jax
import jax.numpy as jnp

def _softmax(x, axis=-1):
    return jax.nn.softmax(x, axis=axis)

def _gelu(x):
    return jax.nn.gelu(x, approximate=True)

def _silu(x):
    return jax.nn.silu(x)

def _sigmoid(x):
    return jax.nn.sigmoid(x)

def _layernorm(x, axis=-1, eps=1e-05):
    m = jnp.mean(x, axis=axis, keepdims=True)
    v = jnp.var(x, axis=axis, keepdims=True)
    return (x - m) / jnp.sqrt(v + eps)

def _scatter_add(tgt, idx, src, axis=0):
    return tgt.at[idx].add(src)

def _segment_sum(src, seg, n):
    return jax.ops.segment_sum(src, seg, n)
kernel_name = 'mk_decoder_preln_d1_seqx_r4_ea9b0a'

def setup_inputs(seed: int=0):
    np.random.seed(seed)
    _w = jnp.asarray

    def _rec_inputs():
        import jax
        import jax.numpy as jnp
        _rk = jax.random.key(seed)
        x = -0.000125 + 0.9999 * jax.random.normal(jax.random.fold_in(_rk, 1), (4, 512, 512), jnp.float32)
        _lenS = 512 - jax.random.randint(jax.random.fold_in(_rk, 7), (4,), 0, max(1, 512 // 4) + 1, jnp.int32)
        _lenS2 = 512 - jax.random.randint(jax.random.fold_in(_rk, 8), (4,), 0, max(1, 512 // 4) + 1, jnp.int32)
        fside_BxS2xS2_0 = -3.05549e-07 + 0.0199987 * jax.random.normal(jax.random.fold_in(_rk, 11), (4, 512, 512), jnp.float32)
        _ctx_1024P = jax.random.normal(jax.random.fold_in(_rk, 12), (4, 16, 256), jnp.float32)
        _ctx_1024c = jax.random.dirichlet(jax.random.fold_in(_rk, 512), 0.3 * jnp.ones((16,), jnp.float32), (4, 512))
        _ctx_1024t = jnp.einsum('bsk,bkd->bsd', _ctx_1024c, _ctx_1024P)
        _ctx_1024t = _ctx_1024t * jax.lax.rsqrt(jnp.mean(jnp.square(_ctx_1024t)) + 1e-12) * 0.953939
        ctx_1024 = 6.82029e-06 + 0.0200006 * (_ctx_1024t + 0.3 * jax.random.normal(jax.random.fold_in(_rk, 612), (4, 512, 256), jnp.float32))
        return (x, fside_BxS2xS2_0, ctx_1024)
    x, fside_BxS2xS2_0, ctx_1024 = _rec_inputs()

    def _L0_attn_setup():
        import jax, jax.numpy as jnp
        import numpy as np
        D_MODEL = 512
        N_HEADS = 16
        HEAD_DIM = D_MODEL // N_HEADS

        def _alibi_slopes(n_heads: int) -> jnp.ndarray:
            start = 2.0 ** (-8.0 / n_heads)
            return jnp.asarray([start * start ** i for i in range(n_heads)], dtype=jnp.float32)
        key = jax.random.key(seed)
        ks = jax.random.split(key, 9)
        B, S, D = (2, 512, D_MODEL)
        scale = 1.0 / np.sqrt(D)
        return {'x': jax.random.normal(ks[0], (B, S, D), dtype=jnp.float32), 'wq': jax.random.normal(ks[1], (D, D), dtype=jnp.float32) * scale, 'bq': jnp.zeros((D,), dtype=jnp.float32), 'wk': jax.random.normal(ks[2], (D, D), dtype=jnp.float32) * scale, 'bk': jnp.zeros((D,), dtype=jnp.float32), 'wv': jax.random.normal(ks[3], (D, D), dtype=jnp.float32) * scale, 'bv': jnp.zeros((D,), dtype=jnp.float32), 'wo': jax.random.normal(ks[4], (D, D), dtype=jnp.float32) * scale, 'bo': jnp.zeros((D,), dtype=jnp.float32)}
    _L0_attn_all = _L0_attn_setup()
    _L0_attn_in = {k: v for k, v in _L0_attn_all.items() if k in ('wq', 'bq', 'wk', 'bk', 'wv', 'bv', 'wo', 'bo')}
    del _L0_attn_all

    def _L0_xattn_setup():
        import jax, jax.numpy as jnp
        import numpy as np
        EPS = 1e-06
        QMAX = 127.0

        def _smooth_quant_linear(x, w):
            amax_x = jnp.max(jnp.abs(x), axis=0)
            amax_w = jnp.max(jnp.abs(w), axis=0)
            s = jnp.sqrt(jnp.maximum(amax_x, EPS) / jnp.maximum(amax_w, EPS))
            s = jnp.maximum(s, EPS)
            xs = x / s
            ws = w * s
            x_scale = jnp.maximum(jnp.max(jnp.abs(xs), axis=-1, keepdims=True), EPS) / QMAX
            w_scale = jnp.maximum(jnp.max(jnp.abs(ws), axis=-1, keepdims=True), EPS) / QMAX
            x_q = jnp.clip(jnp.round(xs / x_scale), -QMAX, QMAX)
            w_q = jnp.clip(jnp.round(ws / w_scale), -QMAX, QMAX)
            return x_q @ w_q.T * x_scale * w_scale.T

        def _expert_forward(xe, guw, dw):
            h = _smooth_quant_linear(xe, guw)
            gate, up = jnp.split(h, 2, axis=-1)
            a = jax.nn.silu(gate) * up
            return _smooth_quant_linear(a, dw)
        key = jax.random.key(seed)
        k1, k2, k3 = jax.random.split(key, 3)
        E, T, D, I = (8, 512, 512, 256)
        x = jax.random.normal(k1, (E, T, D), dtype=jnp.float32)
        gate_up_weight = jax.random.normal(k2, (E, 2 * I, D), dtype=jnp.float32) * 0.02
        down_weight = jax.random.normal(k3, (E, D, I), dtype=jnp.float32) * 0.02
        return {'x': x, 'gate_up_weight': gate_up_weight, 'down_weight': down_weight}
    _L0_xattn_all = _L0_xattn_setup()
    _L0_xattn_in = {k: v for k, v in _L0_xattn_all.items() if k in ()}
    del _L0_xattn_all

    def _L0_ffn_setup():
        import jax, jax.numpy as jnp
        import numpy as np
        E = 32
        K = 8
        H = 512
        F = 192
        B, S = (1, 256)

        def _moe(x, wg, w1, v1, w2):
            T = x.shape[0]
            logits = x @ wg.T
            scores = jax.nn.softmax(logits, axis=-1)
            weights, idx = jax.lax.top_k(scores, K)
            weights = weights / jnp.sum(weights, axis=-1, keepdims=True)
            flat_e = idx.reshape(-1)
            flat_t = jnp.repeat(jnp.arange(T), K)
            flat_w = weights.reshape(-1)
            order = jnp.argsort(flat_e)
            e_s = flat_e[order]
            t_s = flat_t[order]
            w_s = flat_w[order]
            group_sizes = jnp.bincount(e_s, length=E).astype(jnp.int32)
            xs = x[t_s]
            g = jax.lax.ragged_dot(xs, w1, group_sizes)
            u = jax.lax.ragged_dot(xs, v1, group_sizes)
            h = jax.nn.silu(g) * u
            ys = jax.lax.ragged_dot(h, w2, group_sizes)
            out = jnp.zeros((T, x.shape[1]), x.dtype).at[t_s].add(ys * w_s[:, None])
            return out
        key = jax.random.key(seed)
        k0, k1, k2, k3, k4 = jax.random.split(key, 5)
        scale = 0.02
        return {'hidden_states': jax.random.normal(k0, (B, S, H), jnp.float32), 'wg': jax.random.normal(k1, (E, H), jnp.float32) * scale, 'w1': jax.random.normal(k2, (E, H, F), jnp.float32) * scale, 'v1': jax.random.normal(k3, (E, H, F), jnp.float32) * scale, 'w2': jax.random.normal(k4, (E, F, H), jnp.float32) * scale}
    _L0_ffn_all = _L0_ffn_setup()
    _L0_ffn_in = {k: v for k, v in _L0_ffn_all.items() if k in ('wg', 'w1', 'v1', 'w2')}
    del _L0_ffn_all
    return {'x': x, 'fside_BxS2xS2_0': fside_BxS2xS2_0, 'ctx_1024': ctx_1024, 'L0_attn_wq': _L0_attn_in['wq'], 'L0_attn_bq': _L0_attn_in['bq'], 'L0_attn_wk': _L0_attn_in['wk'], 'L0_attn_bk': _L0_attn_in['bk'], 'L0_attn_wv': _L0_attn_in['wv'], 'L0_attn_bv': _L0_attn_in['bv'], 'L0_attn_wo': _L0_attn_in['wo'], 'L0_attn_bo': _L0_attn_in['bo'], 'L0_ffn_wg': _L0_ffn_in['wg'], 'L0_ffn_w1': _L0_ffn_in['w1'], 'L0_ffn_v1': _L0_ffn_in['v1'], 'L0_ffn_w2': _L0_ffn_in['w2']}

def reference(x, fside_BxS2xS2_0, ctx_1024, L0_attn_wq, L0_attn_bq, L0_attn_wk, L0_attn_bk, L0_attn_wv, L0_attn_bv, L0_attn_wo, L0_attn_bo, L0_ffn_wg, L0_ffn_w1, L0_ffn_v1, L0_ffn_w2):
    import jax
    import jax.numpy as jnp

    def _L0_attn_ref(x, wq, bq, wk, bk, wv, bv, wo, bo):
        import jax, jax.numpy as jnp
        import numpy as np
        D_MODEL = 512
        N_HEADS = 16
        HEAD_DIM = D_MODEL // N_HEADS

        def _alibi_slopes(n_heads: int) -> jnp.ndarray:
            start = 2.0 ** (-8.0 / n_heads)
            return jnp.asarray([start * start ** i for i in range(n_heads)], dtype=jnp.float32)
        B, S, D = x.shape
        H, hd = (N_HEADS, HEAD_DIM)

        def heads(y):
            return y.reshape(B, S, H, hd).transpose(0, 2, 1, 3)
        q = heads(x @ wq + bq)
        k = heads(x @ wk + bk)
        v = heads(x @ wv + bv)
        scores = jnp.einsum('bhqd,bhkd->bhqk', q, k) / jnp.sqrt(jnp.float32(hd))
        pos = jnp.arange(S)
        rel = pos[None, :] - pos[:, None]
        slopes = _alibi_slopes(H)
        bias = slopes[:, None, None] * rel.astype(jnp.float32)
        causal = jnp.where(rel > 0, -jnp.inf, 0.0).astype(jnp.float32)
        scores = scores + (bias + causal)[None]
        attn = jax.nn.softmax(scores, axis=-1)
        out = jnp.einsum('bhqk,bhkd->bhqd', attn, v)
        out = out.transpose(0, 2, 1, 3).reshape(B, S, D)
        return out @ wo + bo

    def _L0_xattn_ref(x, gate_up_weight, down_weight):
        import jax, jax.numpy as jnp
        import numpy as np
        EPS = 1e-06
        QMAX = 127.0

        def _smooth_quant_linear(x, w):
            amax_x = jnp.max(jnp.abs(x), axis=0)
            amax_w = jnp.max(jnp.abs(w), axis=0)
            s = jnp.sqrt(jnp.maximum(amax_x, EPS) / jnp.maximum(amax_w, EPS))
            s = jnp.maximum(s, EPS)
            xs = x / s
            ws = w * s
            x_scale = jnp.maximum(jnp.max(jnp.abs(xs), axis=-1, keepdims=True), EPS) / QMAX
            w_scale = jnp.maximum(jnp.max(jnp.abs(ws), axis=-1, keepdims=True), EPS) / QMAX
            x_q = jnp.clip(jnp.round(xs / x_scale), -QMAX, QMAX)
            w_q = jnp.clip(jnp.round(ws / w_scale), -QMAX, QMAX)
            return x_q @ w_q.T * x_scale * w_scale.T

        def _expert_forward(xe, guw, dw):
            h = _smooth_quant_linear(xe, guw)
            gate, up = jnp.split(h, 2, axis=-1)
            a = jax.nn.silu(gate) * up
            return _smooth_quant_linear(a, dw)
        return jax.vmap(_expert_forward)(x, gate_up_weight, down_weight)

    def _L0_ffn_ref(hidden_states, wg, w1, v1, w2):
        import jax, jax.numpy as jnp
        import numpy as np
        E = 32
        K = 8
        H = 512
        F = 192
        B, S = (1, 256)

        def _moe(x, wg, w1, v1, w2):
            T = x.shape[0]
            logits = x @ wg.T
            scores = jax.nn.softmax(logits, axis=-1)
            weights, idx = jax.lax.top_k(scores, K)
            weights = weights / jnp.sum(weights, axis=-1, keepdims=True)
            flat_e = idx.reshape(-1)
            flat_t = jnp.repeat(jnp.arange(T), K)
            flat_w = weights.reshape(-1)
            order = jnp.argsort(flat_e)
            e_s = flat_e[order]
            t_s = flat_t[order]
            w_s = flat_w[order]
            group_sizes = jnp.bincount(e_s, length=E).astype(jnp.int32)
            xs = x[t_s]
            g = jax.lax.ragged_dot(xs, w1, group_sizes)
            u = jax.lax.ragged_dot(xs, v1, group_sizes)
            h = jax.nn.silu(g) * u
            ys = jax.lax.ragged_dot(h, w2, group_sizes)
            out = jnp.zeros((T, x.shape[1]), x.dtype).at[t_s].add(ys * w_s[:, None])
            return out
        Bb, Ss, Hh = hidden_states.shape
        x = hidden_states.reshape(Bb * Ss, Hh)
        out = _moe(x, wg, w1, v1, w2)
        return out.reshape(Bb, Ss, Hh)
    x = x + _L0_attn_ref(_layernorm(x, axis=-1), L0_attn_wq, L0_attn_bq, L0_attn_wk, L0_attn_bk, L0_attn_wv, L0_attn_bv, L0_attn_wo, L0_attn_bo)
    x = x + _L0_xattn_ref(_layernorm(x, axis=-1), fside_BxS2xS2_0, ctx_1024)
    x = x + _L0_ffn_ref(_layernorm(x, axis=-1), L0_ffn_wg, L0_ffn_w1, L0_ffn_v1, L0_ffn_w2)
    return x

_drawn_inputs = setup_inputs


def setup_inputs(seed=0):
    import zlib

    import numpy as np

    out = dict(_drawn_inputs(seed))
    spreads = {'L0_attn_bq': (0.0, 0.351),
     'L0_attn_bk': (0.0, 0.8),
     'L0_attn_bv': (0.0, 0.1),
     'L0_attn_bo': (0.0, 0.1)}
    factors = {'L0_ffn_wg': 6.115, 'L0_ffn_w1': 5.377, 'L0_ffn_v1': 5.255, 'L0_ffn_w2': 5.255}
    for name, (base, spread) in spreads.items():
        noise = np.random.default_rng([zlib.crc32(name.encode()), seed]).standard_normal(out[name].shape)
        drawn = base * np.exp(spread * noise) if base else spread * noise
        out[name] = jnp.asarray(drawn.astype(out[name].dtype))
    for name, factor in factors.items():
        out[name] = (out[name] * factor).astype(out[name].dtype)
    return out
```

```python
from contextlib import ExitStack

import numpy as np
import concourse.bass as bass
from concourse import mybir

F32, F16, BF16, I32 = mybir.dt.float32, mybir.dt.float16, mybir.dt.bfloat16, mybir.dt.int32
ALU, ACT, AX = mybir.AluOpType, mybir.ActivationFunctionType, mybir.AxisListType

P = 128
B, S, D = 4, 512, 512
NT, KD = S // P, D // P
H, HD = 16, 32
HG = P // HD
PAIRS = H // 2
QI = 256
E, TOPK, F = 32, 8, 192
EB = E // B
LN_EPS, Q_EPS, QMAX = 1e-5, 1e-6, 127.0
MAGIC = 1.5 * 2.0 ** 23
SCALE = 1.0 / np.sqrt(np.float32(HD))
KB = 3 * HD + 16
KM = KB + 1
WC = KD * 2 * 2 * F
W2C = 3 * D
TOK = B * S
REGION = TOK
BLOCKS = REGION // P
TILES = TOK * TOPK // P + E
TABLE = E * BLOCKS + TILES
KT = TOPK * NT
POFF = {0: 0, 1: 512, 3: 896, 2: 1024}
PCOLS = 1280


def shape_constants():
    def parts(x, n):
        out = []
        for _ in range(n):
            h = x.astype(np.float16)
            out.append(h)
            x = x - h.astype(np.float64)
        return out

    eye = np.eye(P, dtype=np.float32)
    i = np.arange(P)
    bf = lambda a: (np.ascontiguousarray(a, np.float32).view(np.uint32) >> 16).astype(np.uint16)
    later = np.where(i[None, :] > i[:, None], np.float32(-1e30), np.float32(0))
    start = np.float32(2.0 ** (-8.0 / H))
    slope = np.array([2.0 ** (-8.0 / H) * (2.0 ** (-8.0 / H)) ** h for h in range(H)], np.float32)
    c = slope.astype(np.float64) * np.sqrt(HD)
    pos = np.arange(S)
    k_rows = np.zeros((32, S), np.float16)
    q_rows = np.zeros((32, H, S), np.float16)
    for n, part in enumerate(parts(c, 3)):
        k_rows[n] = pos % P
        q_rows[n] = part[:, None]
    for j in range(NT):
        for n, part in enumerate(parts(c[:, None] * (P * j - pos)[None, :], 3)):
            k_rows[3 + 3 * j + n] = (pos // P == j)
            q_rows[3 + 3 * j + n] = part
    k_rows[16] = 1
    return {
        "c_eye32": eye, "c_eye16": eye.astype(np.float16), "c_eyeb": bf(eye),
        "c_mask_qk": bf(later), "c_mask_kq": bf(later.T),
        "c_k_rows": k_rows, "c_q_rows": q_rows,
        "c_before": bf(i[:, None] < i[None, :]),
        "c_pads": np.stack([TOK + np.arange(TABLE * P, dtype=np.int32) % P, np.zeros(TABLE * P, np.int32)], 1),
        "c_tok": (np.arange(NT)[None, :] * P + i[:, None]).astype(np.float32),
        "c_keep": np.tile((np.arange(NT * E) % E != 0).astype(np.float32), (P, 1)),
        "c_base": np.tile((np.arange(NT * E) % E * REGION).astype(np.float32), (P, 1)),
        "c_rank": np.tile(np.repeat(np.arange(1, TOPK + 1), NT * E).astype(np.float32), (P, 1)),
        "c_pad_pos": (E * REGION + np.arange(KT)[None, :] * P + i[:, None]).astype(np.int32),
        "c_pad_pay": np.tile(np.stack([TOK + i, 0 * i], 1)[:, None, :], (1, KT, 1)).astype(np.int32),
        "c_tile": np.stack([i, i + P], 1).astype(np.float32),
    }


class Signal:

    def __init__(self, sem, per, each=1, start=0):
        self.sem, self.per, self.each, self.start = sem, per, each, start

    def at(self, b, n):
        if isinstance(b, int):
            return self.start + self.each * (b * self.per + n)
        return b * (self.each * self.per) + (self.start + self.each * n)


def decoder_kernel(nc, x_in, fside, ctx_w, wq, bq, wk, bk, wv, bv, wo, bo, wg, w1, v1, w2,
                   eye32_c, eye16_c, eyeb_c, mask_qk_c, mask_kq_c, k_rows_c, q_rows_c,
                   before_c, pads_c, tok_c, keep_c, base_c, rank_c, pad_pos_c, pad_pay_c, tile_c, out):
    with nc.sbuf_tensor("counts", [P, E], F32) as counts:
        split_w = nc.dram_tensor("split_w", [E, P, WC + W2C], F16, kind="Internal").ap()
        x3_rows = nc.dram_tensor("x3_rows", [TOK + P, 2 * D], F16, kind="Internal").ap()
        table = nc.dram_tensor("table", [TABLE * P, 2], I32, kind="Internal").ap()
        dense_part(nc, x_in, fside, ctx_w, wq, bq, wk, bk, wv, bv, wo, bo, wg, w1, v1, w2,
                   eye32_c, eye16_c, eyeb_c, mask_qk_c, mask_kq_c, k_rows_c, q_rows_c,
                   before_c, pads_c, tok_c, keep_c, base_c, rank_c, pad_pos_c, pad_pay_c,
                   counts, split_w, x3_rows, table, out)
        expert_part(nc, eye32_c, eye16_c, tile_c, counts, split_w, x3_rows, table, out)


def dense_part(nc, x_in, fside, ctx_w, wq, bq, wk, bk, wv, bv, wo, bo, wg, w1, v1, w2,
               eye32_c, eye16_c, eyeb_c, mask_qk_c, mask_kq_c, k_rows_c, q_rows_c,
               before_c, pads_c, tok_c, keep_c, base_c, rank_c, pad_pos_c, pad_pay_c,
               counts, split_w, x3_rows, table, out):
    ctx = ExitStack()
    with ctx:
        def sb(name, shape, dt):
            return ctx.enter_context(nc.sbuf_tensor(name, shape, dt))

        started = []

        def sig(name, per=1, each=1, start=0):
            s = Signal(ctx.enter_context(nc.semaphore(name)), per, each, start)
            if start:
                started.append(s)
            return s

        ps = ctx.enter_context(nc.psum_tensor("ps", [P, 8, 512], F32))
        psb = ps[:, :, :].bitcast(BF16)

        eye32, eye16, eyeb = sb("eye32", [P, P], F32), sb("eye16", [P, P], F16), sb("eyeb", [P, P], BF16)
        mask_qk, mask_kq = sb("mask_qk", [P, P], BF16), sb("mask_kq", [P, P], BF16)
        ones32 = sb("ones32", [P, P], F32)
        eps, neg_half, half = sb("eps", [P, 4], F32), sb("neg_half", [P, 4], F32), sb("half", [P, 4], F32)
        w_hi = sb("w_hi", [P, 4, KD, D], F16)
        w_lo = sb("w_lo", [P, 4, KD, D], F16)
        b_qk = sb("b_qk", [P, 2 * KD], F32)
        b_v, b_o = sb("b_v", [P, D], F32), sb("b_o", [P, D], F32)
        x = sb("x", [P, NT, D], F32)
        x1 = sb("x1", [P, NT, D], F32)
        xn = sb("xn", [P, NT, D], F32)
        t_hi, t_lo = sb("t_hi", [P, KD, S], F16), sb("t_lo", [P, KD, S], F16)
        qk_hi, qk_lo = sb("qk_hi", [P, 8, S], F16), sb("qk_lo", [P, 8, S], F16)
        qop, kop = sb("qop", [P, H, S], F16), sb("kop", [P, H, S], F16)
        v_hi = sb("v_hi", [P, NT, H, HD + 1], F16)
        v_lo = sb("v_lo", [P, NT, H, HD], F16)
        mx = sb("mx", [P, NT, H], F32)
        m_row = sb("m_row", [H // 2, 2, S], F16)
        p32, p_hi, p_lo = sb("p32", [P, 2, PCOLS], F32), sb("p_hi", [P, 2, PCOLS], F16), sb("p_lo", [P, 2, PCOLS], F16)
        rden = sb("rden", [P, 2, NT], F32)
        o32 = sb("o32", [P, NT, D], F32)
        stats, mv, ve, rstd = sb("stats", [P, NT, 6], F32), sb("mv", [P, NT, 2], F32), sb("ve", [P, NT], F32), sb("rstd", [P, NT], F32)
        fw = sb("fw", [P, KD, D], F32)
        cw = sb("cw", [P, KD, QI], F32)
        act = sb("act", [P, NT, QI], F32)
        th = p32[:, :, :].rearrange("p a c -> p (a c)")[:, 0:NT * QI].rearrange("p (t c) -> p t c", t=NT)
        amax, sq = sb("amax", [P, 2, KD], F32), sb("sq", [P, 6, KD], F32)
        dg = sb("dg", [P, 2, KD, P], F32)
        rowmax, rscale, rinv = sb("rowmax", [P, 2, 4], F32), sb("rscale", [P, 2, 4], F32), sb("rinv", [P, 2, 4], F32)
        xq = qk_hi[:, 0:4, :].bitcast(BF16)
        wqz = qk_hi[:, 4:8, :].bitcast(BF16)
        xqT = qk_lo[:, 0:4, :].bitcast(BF16)
        wqT = qk_lo[:, 4:8, :].bitcast(BF16)
        wscb = sb("wscb", [P, D], F32)

        s_const = sig("s_const", 1, 16)
        s_wld = [sig(f"s_wld{n}", 1, 16) for n in range(5)]
        s_whi, s_wlo = sig("s_whi"), sig("s_wlo")
        s_one, s_mg = sig("s_one"), sig("s_mg")
        x_ld = sig("x_ld", 1, 16)
        fw_ld, cw_ld = sig("fw_ld", 1, 16), sig("cw_ld", 1, 16)
        ln_st, ln_mv, ln_rs = sig("ln_st", 3), sig("ln_mv", 3), sig("ln_rs", 3)
        pl_ve = sig("pl_ve", 3)
        xn_ok = sig("xn_ok", 12)
        t_mm = sig("t_mm", 12)
        t_hi_ok, t_lo_ok = sig("t_hi_ok", 12), sig("t_lo_ok", 12)
        qk_mm, qk_hi_ok, qk_lo_ok = sig("qk_mm", 8), sig("qk_hi_ok", 8), sig("qk_lo_ok", 8)
        op_ld = sig("op_ld", 24, 16)
        v_mm, v32_ok, v_hi_ok, v_lo_ok = sig("v_mm", 4), sig("v32_ok", 4), sig("v_hi_ok", 4), sig("v_lo_ok", 4)
        s_mm, s_max = sig("s_mm", 3 * PAIRS), sig("s_max", 3 * PAIRS)
        m_mm, m_row_ok, m_ld = sig("m_mm", 2), sig("m_row_ok", 2), sig("m_ld", 2, 16)
        st_mm, e32_ok, ehi_ok, elo_ok = sig("st_mm", H), sig("e32_ok", H), sig("ehi_ok", H), sig("elo_ok", H)
        pv_mm, rec_ok, norm_ok = sig("pv_mm", H), sig("rec_ok", H), sig("norm_ok", H)
        xbo_ok = sig("xbo_ok", 4)
        wo_mm, x1_ok = sig("wo_mm", 4), sig("x1_ok", 4, start=1)
        am_mm, am_ok = sig("am_mm", 12), sig("am_ok", 12)
        qs_link = sig("qs_link", 12)
        qs_rat, qs_pow = sig("qs_rat", 2), sig("qs_pow", 2)
        dg_ok, bc_mm = sig("dg_ok", 4), sig("bc_mm", 4)
        sc_ok, rm_ok, ri_ok = sig("sc_ok", 16), sig("rm_ok", 4), sig("ri_ok", 4)
        q1_ok, q2_ok, q3_ok = sig("q1_ok", 16), sig("q2_ok", 16), sig("q3_ok", 16, start=1)
        qt_mm, qt_ok = sig("qt_mm", 6), sig("qt_ok", 6)
        wsb_ok = sig("wsb_ok", 2)
        l_mm, l_ok = sig("l_mm", 8), sig("l_ok", 8)
        th_ok, a1_ok, a_ok = sig("th_ok", 4), sig("a1_ok", 4), sig("a_ok", 4)
        x2_ok = sig("x2_ok", 4)
        out_st = sig("out_st", 1, 16, start=1)
        wd_ok, wd_mm = sig("wd_ok", 2), sig("wd_mm", 2)
        lg_mm, lg_ok = sig("lg_mm"), sig("lg_ok")
        magic, idle, idle_p = sb("magic", [P, 2], F32), sb("idle", [P, 1], F32), sb("idle_p", [P, 1], F32)
        g_hi, g_lo = sb("g_hi", [P, KD, E], F16), sb("g_lo", [P, KD, E], F16)
        primer = sb("primer", [P, 8], F32)
        before, onesb = sb("before", [P, P], BF16), sb("onesb", [P, P], BF16)
        keep, base, tokf = sb("keep", [P, NT * E], F32), sb("base", [P, NT * E], F32), sb("tokf", [P, NT], F32)
        rank = sb("rank", [P, TOPK, NT * E], F32)
        lg, sm, rep = sb("lg", [P, NT, E], F32), sb("sm", [P, NT, E], F32), sb("rep", [P, NT, E], F32)
        top, r4 = sb("top", [P, NT, TOPK], F32), sb("r4", [P, 4, NT], F32)
        chosen, chosenb = sb("chosen", [P, NT, E], F32), sb("chosenb", [P, NT, E], BF16)
        nth, slot, gate = sb("nth", [P, NT * E], F32), sb("slot", [P, NT, E], F32), sb("gate", [P, NT, E], F32)
        hit = o32[:, 0:2, :].rearrange("p a (k c) -> p (a k) c", c=NT * E)
        hit2 = o32[:, 2:4, :].rearrange("p a (k c) -> p (a k) c", c=NT * E)
        posf, pos = sb("posf", [P, KT], F32), sb("pos", [P, KT], I32)
        gatek = sb("gatek", [P, KT], F32)
        pay = sb("pay", [P, KT, 2], I32)
        x3 = qk_hi[:, :, :].rearrange("p (t a) d -> p t (a d)", a=2)
        zeros = sb("zeros", [P, D], F32)
        wst = sb("wst", [P, WC + W2C], F16)
        wst13 = wst[:, 0:WC].rearrange("p (k s f) -> p k s f", k=KD, s=2)
        wst2 = wst[:, WC:WC + W2C].rearrange("p (a d) -> p a d", a=3)
        w13f = fw[:, 0:3, :].rearrange("p a c -> p (a c)").rearrange("p (k f) -> p k f", k=KD)
        w2f = act[:, :, :].rearrange("p a c -> p (a c)").rearrange("p (a d) -> p a d", a=2)
        ew_ld, ew_hi, ew_st = sig("ew_ld", 5 * EB, 16), sig("ew_hi", EB), sig("ew_st", EB, 16, start=1)
        ew_lo13, ew_lo2 = sig("ew_lo13", EB, start=1), sig("ew_lo2", EB, start=1)
        r_link, r_rep, r_ex, r_exp = sig("r_link", 15), sig("r_rep"), sig("r_ex"), sig("r_exp")
        r_mask, rk_mm, r_pos, r_tok = sig("r_mask"), sig("rk_mm"), sig("r_pos", start=1), sig("r_tok")
        x3_hi, x3_lo, x3_st = sig("x3_hi", 4), sig("x3_lo"), sig("x3_st", 1, 16, start=1)
        tb_st = sig("tb_st", KT, 16)
        init_st = sig("init_st", 1, 16)

        N_CONST = 17 + H
        bank = [ps[:, i, :] for i in range(8)]
        x_dram = x_in.rearrange("b (t p) d -> b p t d", p=P)
        o_dram = out[0:B * S, :].rearrange("(b t p) d -> b p t d", p=P, t=NT)
        x3_dram = x3_rows[0:TOK, :].rearrange("(b t p) d -> b p t d", p=P, t=NT)
        fw_dram = fside.rearrange("b (t p) d -> b p t d", p=P)
        cw_dram = ctx_w.rearrange("b (t p) d -> b p t d", p=P)
        QKV = {"q": 0, "k": 1, "v": 2, "o": 3}

        block = ctx.enter_context(nc.Block())

        @block.sync
        def _(sp):
            for dst, src in ((keep, keep_c), (base, base_c), (tokf, tok_c), (before, before_c), (pos, pad_pos_c), (eye32, eye32_c), (eye16, eye16_c), (eyeb, eyeb_c), (mask_qk, mask_qk_c),
                             (mask_kq, mask_kq_c), (b_v, bv), (b_o, bo), (b_qk[:, 0:KD], bq), (b_qk[:, KD:2 * KD], bk)):
                sp.dma_start(dst[:, :].bitcast(src.dtype), src).then_inc(s_const.sem, 16)
            sp.dma_start(rank[:, :, :], rank_c.rearrange("p (k c) -> p k c", k=TOPK)).then_inc(s_const.sem, 16)
            sp.dma_start(pay[:, :, :], pad_pay_c).then_inc(s_const.sem, 16)
            sp.dma_start(qop[3 * HD:4 * HD, :, :], q_rows_c).then_inc(s_const.sem, 16)
            for h in range(H):
                sp.dma_start(kop[3 * HD:4 * HD, h, :], k_rows_c).then_inc(s_const.sem, 16)
            for n, w in enumerate((wq, wk, wv, wo)):
                if n >= 2:
                    sp.wait_ge(s_wlo.sem, n - 1)
                sp.dma_start((x, x1)[n % 2][:, :, :], w.rearrange("(k p) n -> p k n", p=P)).then_inc(s_wld[n].sem, 16)
            sp.dma_start(fw[:, :, 0:E], wg.rearrange("(k p) n -> p k n", p=P)).then_inc(s_wld[4].sem, 16)
            sp.dma_start(table, pads_c).then_inc(init_st.sem, 16)
            sp.wait_ge(s_one.sem, 7)
            sp.dma_start(out[TOK:TOK + P, :], zeros[:, :]).then_inc(init_st.sem, 16)
            sp.dma_start(x3_rows[TOK:TOK + P, :], zeros[:, :].bitcast(F16)).then_inc(init_st.sem, 16)
            sp.wait_ge(s_wlo.sem, 5)
            with sp.Fori(0, B) as b:
                sp.wait_ge(x1_ok.sem, x1_ok.at(b, 0))
                sp.dma_start(x[:, :, :], x_dram[b]).then_inc(x_ld.sem, 16)
                sp.wait_ge(q3_ok.sem, q3_ok.at(b, 0))
                sp.dma_start(cw[:, :, :], cw_dram[b]).then_inc(cw_ld.sem, 16)
                for which, dst, (hi_rows, lo_row) in ((0, qop, ((0, 32), 64)), (1, kop, ((0, 64), 32))):
                    sp.wait_ge(qk_hi_ok.sem, qk_hi_ok.at(b, 4 * which + 4))
                    for r in hi_rows:
                        for i in range(HG):
                            sp.dma_start(dst[r:r + HD, i::HG, :], qk_hi[HD * i:HD * i + HD, 4 * which:4 * which + 4, :]).then_inc(op_ld.sem, 16)
                    sp.wait_ge(qk_lo_ok.sem, qk_lo_ok.at(b, 4 * which + 4))
                    for i in range(HG):
                        sp.dma_start(dst[lo_row:lo_row + HD, i::HG, :], qk_lo[HD * i:HD * i + HD, 4 * which:4 * which + 4, :]).then_inc(op_ld.sem, 16)
                for g in range(2):
                    sp.wait_ge(m_row_ok.sem, m_row_ok.at(b, g + 1))
                    sp.dma_start(qop[KB:KB + 1, 8 * g:8 * g + 8, :], m_row[:, g, :]).then_inc(m_ld.sem, 16)
                with sp.Fori(0, EB) as n:
                    e = b * EB + n
                    sp.wait_ge(ew_lo13.sem, ew_lo13.at(b, 0) + n)
                    sp.wait_ge(ew_lo2.sem, ew_lo2.at(b, 0) + n)
                    sp.dma_start(w13f[:, :, 0:F], w1.rearrange("e (k p) f -> e p k f", p=P)[e]).then_inc(ew_ld.sem, 16)
                    sp.dma_start(w13f[:, :, F:2 * F], v1.rearrange("e (k p) f -> e p k f", p=P)[e]).then_inc(ew_ld.sem, 16)
                    sp.dma_start(w2f[:, 0, :], w2[:, 0:P, :][e]).then_inc(ew_ld.sem, 16)
                    for side in range(2):
                        sp.dma_start(w2f[64 * side:64 * side + 64, 1, :], w2[:, P:F, :][e]).then_inc(ew_ld.sem, 16)
                    sp.wait_ge(ew_lo13.sem, ew_lo13.at(b, 1) + n)
                    sp.wait_ge(ew_lo2.sem, ew_lo2.at(b, 1) + n)
                    sp.dma_start(split_w[e], wst[:, :]).then_inc(ew_st.sem, 16)
                sp.dma_start(fw[:, :, :], fw_dram[b]).then_inc(fw_ld.sem, 16)
            sp.wait_ge(ew_st.sem, ew_st.at(B, 0))
            sp.wait_ge(out_st.sem, out_st.at(B, 0))
            sp.wait_ge(x3_st.sem, x3_st.at(B, 0))
            sp.wait_ge(init_st.sem, 16 * 3)
            sp.wait_ge(tb_st.sem, 16 * KT * (B + 1))

        @block.gpsimd
        def _(pool):
            nc.gpsimd.memset(ones32[:, :], 1.0).then_inc(s_one.sem, 1)
            nc.gpsimd.memset(neg_half[:, :], -0.5).then_inc(s_one.sem, 1)
            nc.gpsimd.memset(half[:, :], 0.5).then_inc(s_one.sem, 1)
            nc.gpsimd.memset(eps[:, :], LN_EPS).then_inc(s_one.sem, 1)
            nc.gpsimd.memset(v_hi[:, :, :, :], 1.0).then_inc(s_one.sem, 1)
            nc.gpsimd.memset(onesb[:, :], 1.0).then_inc(s_one.sem, 1)
            nc.gpsimd.memset(zeros[:, :], 0.0).then_inc(s_one.sem, 1)
            for n, s in enumerate(started):
                nc.gpsimd.memset(primer[:, n:n + 1], 0.0).then_inc(s.sem, 1)
            pool.wait_ge(s_one.sem, 7)
            pool.wait_ge(s_const.sem, N_CONST * 16)

            def ln_scale(b, n):
                pool.wait_ge(ln_mv.sem, ln_mv.at(b, n + 1))
                nc.gpsimd.tensor_tensor(ve[:, :], mv[:, :, 1], eps[:, :], ALU.add).then_inc(pl_ve.sem, 1)
                pool.wait_ge(pl_ve.sem, pl_ve.at(b, n + 1))
                nc.gpsimd.tensor_tensor(rstd[:, :], ve[:, :], neg_half[:, :], ALU.pow).then_inc(ln_rs.sem, 1)

            def smooth(b, lin):
                n = (KD, 2)[lin]
                pool.wait_ge(qs_rat.sem, qs_rat.at(b, lin + 1))
                nc.gpsimd.tensor_tensor(sq[:, 3, 0:n], sq[:, 2, 0:n], half[:, 0:n], ALU.pow).then_inc(qs_pow.sem, 1)

            def scatter_choices(b):
                pool.wait_ge(r_pos.sem, r_pos.at(b, 0))
                nc.gpsimd.tensor_tensor(idle_p[:, :], eps[:, 0:1], eps[:, 0:1], ALU.add)
                for c in range(KT):
                    nc.gpsimd.indirect_dma_start(table, bass.IndirectOffsetOnAxis(ap=pos[:, c:c + 1], axis=0),
                                                 pay[:, c, :], None).then_inc(tb_st.sem, 16)

            pool.wait_ge(init_st.sem, 48)
            with pool.Fori(0, B) as b:
                ln_scale(b, 0)
                pool.wait_ge(xn_ok.sem, xn_ok.at(b, 4))
                for t in range(NT):
                    nc.gpsimd.tensor_tensor(x[:, t, :], x[:, t, :], b_o[:, :], ALU.add).then_inc(xbo_ok.sem, 1)
                scatter_choices(b)

                def remainders(b, hp, first):
                    for i in range(2):
                        if not first:
                            pool.wait_ge(pv_mm.sem, pv_mm.at(b, i - 1) + 2 * hp)
                        pool.wait_ge(ehi_ok.sem, ehi_ok.at(b, i + 1) + 2 * hp)
                        nc.gpsimd.tensor_tensor(p_lo[:, i, :], p32[:, i, :], p_hi[:, i, :], ALU.subtract).then_inc(elo_ok.sem, 1)
                    pool.wait_ge(ew_hi.sem, ew_hi.at(b, 1) + hp)
                    nc.gpsimd.tensor_tensor(wst13[:, :, 1, :], w13f[:, :, :], wst13[:, :, 0, :], ALU.subtract).then_inc(ew_lo13.sem, 1)
                remainders(b, 0, True)
                with pool.Fori(1, PAIRS) as hp:
                    remainders(b, hp, False)
                ln_scale(b, 1)
                smooth(b, 0)
                smooth(b, 1)
                ln_scale(b, 2)
                pool.wait_ge(x3_hi.sem, x3_hi.at(b, 4))
                nc.gpsimd.tensor_tensor(x3[:, :, D:2 * D], xn[:, :, :], x3[:, :, 0:D], ALU.subtract).then_inc(x3_lo.sem, 1)
            scatter_choices(B)

        @block.scalar
        def _(act_e):
            act_e.wait_ge(s_mg.sem, 2)
            for n in range(4):
                act_e.wait_ge(s_wld[n].sem, 16)
                nc.scalar.copy(w_hi[:, n, :, :], (x, x1)[n % 2][:, :, :]).then_inc(s_whi.sem, 1)
            act_e.wait_ge(s_wld[4].sem, 16)
            nc.scalar.copy(g_hi[:, :, :], fw[:, :, 0:E]).then_inc(s_whi.sem, 1)

            def halves_hi(b, first):
                for k in range(KD):
                    act_e.wait_ge(t_mm.sem, t_mm.at(b, first + k + 1))
                    nc.scalar.copy(t_hi[:, k, :], bank[(0, 0, 4)[first // 4] + k]).then_inc(t_hi_ok.sem, 1)

            def quantise(b, lin):
                w = (D, QI)[lin]
                for side, src, dst in ((1, (fw, cw)[lin], wqz), (0, (xn, act)[lin], xq)):
                    n = 8 * lin + 4 * (1 - side)
                    act_e.wait_ge(ri_ok.sem, ri_ok.at(b, 2 * lin + 2 - side))
                    for t in range(4):
                        nc.scalar.activation(src[:, t, 0:w], src[:, t, 0:w], ACT.Identity, bias=magic[:, 0:1],
                                             scale=rinv[:, side, t:t + 1]).then_inc(q1_ok.sem, 1)
                    for t in range(4):
                        act_e.wait_ge(q2_ok.sem, q2_ok.at(b, n + t + 1))
                        nc.scalar.activation(dst[:, t, 0:w], src[:, t, 0:w], ACT.Identity, bias=magic[:, 1:2],
                                             scale=1.0).then_inc(q3_ok.sem, 1)

            def quantT_out(b, lin, side):
                if lin == 0:
                    for half_ in range(2):
                        act_e.wait_ge(qt_mm.sem, qt_mm.at(b, 2 * (1 - side) + half_ + 1))
                        nc.scalar.copy((xqT, wqT)[side][:, 2 * half_:2 * half_ + 2, :],
                                       psb[:, (2, 4)[side] + half_, :].rearrange("p (k c) -> p k c", k=2)).then_inc(qt_ok.sem, 1)
                else:
                    act_e.wait_ge(qt_mm.sem, qt_mm.at(b, 4 + (1 - side) + 1))
                    nc.scalar.copy((xqT, wqT)[side][:, 0:2, :],
                                   psb[:, (6, 7)[side], :].rearrange("p (k c) -> p k c", k=2)).then_inc(qt_ok.sem, 1)

            with act_e.Fori(0, B) as b:
                halves_hi(b, 0)
                act_e.wait_ge(x3_st.sem, x3_st.at(b, 0))
                for i in range(8):
                    act_e.wait_ge(qk_mm.sem, qk_mm.at(b, i + 1))
                    nc.scalar.activation(qk_hi[:, i, :], bank[(4 + i) % 8], ACT.Identity, bias=b_qk[:, i:i + 1], scale=1.0).then_inc(qk_hi_ok.sem, 1)
                for t in range(NT):
                    act_e.wait_ge(v32_ok.sem, v32_ok.at(b, t + 1))
                    nc.scalar.copy(v_hi[:, t, :, 0:HD], o32[:, t, :].rearrange("p (h d) -> p h d", h=H)).then_inc(v_hi_ok.sem, 1)
                for g in range(2):
                    act_e.wait_ge(m_mm.sem, m_mm.at(b, g + 1))
                    nc.scalar.mul(m_row[:, g, :], ps[0:H // 2, 6, :], -1.0).then_inc(m_row_ok.sem, 1)
                def exponentials(b, hp, first):
                    for i in range(2):
                        if not first:
                            act_e.wait_ge(pv_mm.sem, pv_mm.at(b, i - 1) + 2 * hp)
                            act_e.wait_ge(elo_ok.sem, elo_ok.at(b, i - 1) + 2 * hp)
                        act_e.wait_ge(st_mm.sem, st_mm.at(b, i + 1) + 2 * hp)
                        src = ps[:, 3 * i:3 * i + 3, :].rearrange("p a c -> p (a c)")[:, 0:PCOLS]
                        nc.scalar.activation(p32[:, i, :], src, ACT.Exp, scale=float(SCALE)).then_inc(e32_ok.sem, 1)
                        nc.scalar.activation(p_hi[:, i, :], src, ACT.Exp, scale=float(SCALE)).then_inc(ehi_ok.sem, 1)
                    act_e.wait_ge(ew_ld.sem, ew_ld.at(b, 5) + 80 * hp)
                    act_e.wait_ge(ew_st.sem, ew_st.at(b, 0) + 16 * hp)
                    nc.scalar.copy(wst13[:, :, 0, :], w13f[:, :, :])
                    nc.scalar.copy(wst2[:, 0::2, :], w2f[:, :, :]).then_inc(ew_hi.sem, 1)
                exponentials(b, 0, True)
                with act_e.Fori(1, PAIRS) as hp:
                    exponentials(b, hp, False)
                halves_hi(b, 4)
                quantise(b, 0)
                quantT_out(b, 0, 1)
                quantT_out(b, 0, 0)
                for t in range(NT):
                    act_e.wait_ge(l_ok.sem, l_ok.at(b, t + 1))
                    nc.scalar.activation(th[:, t, :], o32[:, t, 0:QI], ACT.Tanh, scale=0.5).then_inc(th_ok.sem, 1)
                quantise(b, 1)
                quantT_out(b, 1, 1)
                quantT_out(b, 1, 0)
                act_e.wait_ge(x2_ok.sem, x2_ok.at(b, 4))
                act_e.dma_start(o_dram[b], x1[:, :, :]).then_inc(out_st.sem, 16)
                for t in range(NT):
                    act_e.wait_ge(xn_ok.sem, xn_ok.at(b, 8 + t + 1))
                    nc.scalar.copy(x3[:, t, 0:D], xn[:, t, :]).then_inc(x3_hi.sem, 1)
                halves_hi(b, 8)
                act_e.wait_ge(r_ex.sem, r_ex.at(b, 1))
                nc.scalar.activation(sm[:, :, :], lg[:, :, :], ACT.Exp).then_inc(r_exp.sem, 1)
                act_e.wait_ge(x3_lo.sem, x3_lo.at(b, 1))
                act_e.dma_start(x3_dram[b], x3[:, :, :]).then_inc(x3_st.sem, 16)

        @block.vector
        def _(dve):
            nc.vector.memset(magic[:, 0:1], MAGIC).then_inc(s_mg.sem, 1)
            nc.vector.memset(magic[:, 1:2], -MAGIC).then_inc(s_mg.sem, 1)
            dve.wait_ge(s_one.sem, 7)
            for n in range(4):
                dve.wait_ge(s_whi.sem, n + 1)
                nc.vector.tensor_tensor(w_lo[:, n, :, :], (x, x1)[n % 2][:, :, :], w_hi[:, n, :, :], ALU.subtract).then_inc(s_wlo.sem, 1)
            dve.wait_ge(s_whi.sem, 5)
            nc.vector.tensor_tensor(g_lo[:, :, :], fw[:, :, 0:E], g_hi[:, :, :], ALU.subtract).then_inc(s_wlo.sem, 1)

            def layer_norm(b, n, src):
                for t in range(NT):
                    i = nc.vector.bn_stats(stats[:, t, :], src[:, t, :])
                i.then_inc(ln_st.sem, 1)
                dve.wait_ge(ln_st.sem, ln_st.at(b, n + 1))
                nc.vector.memset(idle[:, :], 0.0)
                for t in range(NT):
                    i = nc.vector.bn_aggr(mv[:, t, :], stats[:, t, :])
                i.then_inc(ln_mv.sem, 1)
                dve.wait_ge(ln_rs.sem, ln_rs.at(b, n + 1))
                for t in range(NT):
                    nc.vector.tensor_scalar(xn[:, t, :], src[:, t, :], mv[:, t, 0:1], rstd[:, t:t + 1],
                                            ALU.subtract, ALU.mult).then_inc(xn_ok.sem, 1)

            def halves_lo(b, first):
                for k in range(KD):
                    dve.wait_ge(t_hi_ok.sem, t_hi_ok.at(b, first + k + 1))
                    nc.vector.tensor_tensor(t_lo[:, k, :], bank[(0, 0, 4)[first // 4] + k], t_hi[:, k, :],
                                            ALU.subtract).then_inc(t_lo_ok.sem, 1)

            def scales(b, lin):
                n = (KD, 2)[lin]
                step = [6 * lin]

                def link(i):
                    step[0] += 1
                    i.then_inc(qs_link.sem, 1)
                    dve.wait_ge(qs_link.sem, qs_link.at(b, step[0]))

                for side in range(2):
                    for k in range(n):
                        m = 8 * lin + n * side + k
                        dve.wait_ge(am_mm.sem, am_mm.at(b, m + 1))
                        nc.vector.tensor_reduce(amax[:, side, k:k + 1], bank[(4 * side, 4 + 2 * side)[lin] + k], AX.X, ALU.max,
                                                apply_absolute_value=True).then_inc(am_ok.sem, 1)
                dve.wait_ge(am_ok.sem, am_ok.at(b, 8 + 4 * lin))
                link(nc.vector.tensor_scalar(sq[:, 0:2, 0:n], amax[:, :, 0:n], Q_EPS, None, ALU.max))
                link(nc.vector.reciprocal(sq[:, 1, 0:n], sq[:, 1, 0:n]))
                nc.vector.tensor_tensor(sq[:, 2, 0:n], sq[:, 0, 0:n], sq[:, 1, 0:n], ALU.mult).then_inc(qs_rat.sem, 1)
                dve.wait_ge(qs_pow.sem, qs_pow.at(b, lin + 1))
                link(nc.vector.tensor_scalar(sq[:, 4, 0:n], sq[:, 3, 0:n], Q_EPS, None, ALU.max))
                link(nc.vector.reciprocal(sq[:, 5, 0:n], sq[:, 4, 0:n]))
                for side in (1, 0):
                    for k in range(n):
                        i = nc.vector.tensor_scalar(dg[:, side, k, :], eye32[:, :], sq[:, (5, 4)[side], k:k + 1], None, ALU.mult)
                    i.then_inc(dg_ok.sem, 1)

            def scaled_rows(b, lin, side):
                w = (D, QI)[lin]
                src = ((xn, act), (fw, cw))[side][lin]
                m = 2 * lin + (1 - side)
                dve.wait_ge(bc_mm.sem, bc_mm.at(b, m + 1))
                if side == 1:
                    ld = (fw_ld, cw_ld)[lin]
                    dve.wait_ge(ld.sem, ld.at(b, 1))
                for t in range(4):
                    nc.vector.tensor_tensor(src[:, t, 0:w], src[:, t, 0:w], bank[(0, 4)[lin] + side][:, 0:w], ALU.mult).then_inc(sc_ok.sem, 1)
                for t in range(4):
                    dve.wait_ge(sc_ok.sem, sc_ok.at(b, 4 * m + t + 1))
                    i = nc.vector.tensor_reduce(rowmax[:, side, t:t + 1], src[:, t, 0:w], AX.X, ALU.max, apply_absolute_value=True)
                i.then_inc(rm_ok.sem, 1)
                dve.wait_ge(rm_ok.sem, rm_ok.at(b, m + 1))
                i = nc.vector.tensor_scalar(rscale[:, side, :], rowmax[:, side, :], Q_EPS, 1.0 / QMAX, ALU.max, ALU.mult)
                i.then_inc(qs_link.sem, 1)
                dve.wait_ge(qs_link.sem, qs_link.at(b, 6 * lin + 4 + (1 - side) + 1))
                nc.vector.reciprocal(rinv[:, side, :], rscale[:, side, :]).then_inc(ri_ok.sem, 1)

            def clip(b, lin, side):
                w = (D, QI)[lin]
                src = ((xn, act), (fw, cw))[side][lin]
                for t in range(4):
                    dve.wait_ge(q1_ok.sem, q1_ok.at(b, 8 * lin + 4 * (1 - side) + t + 1))
                    nc.vector.tensor_scalar(src[:, t, 0:w], src[:, t, 0:w], MAGIC - QMAX, MAGIC + QMAX, ALU.max, ALU.min).then_inc(q2_ok.sem, 1)

            def weight_steps(b, lin):
                for t in range(4):
                    i = nc.vector.tensor_scalar(dg[:, 1, t, :], eye32[:, :], rscale[:, 1, t:t + 1], None, ALU.mult)
                i.then_inc(wd_ok.sem, 1)

            def weight_steps_out(b, lin):
                dve.wait_ge(wd_mm.sem, wd_mm.at(b, lin + 1))
                nc.vector.tensor_copy(wscb[:, :], bank[(6, 4)[lin]]).then_inc(wsb_ok.sem, 1)
                dve.wait_ge(wsb_ok.sem, wsb_ok.at(b, lin + 1))

            def route(b):
                step = [0]

                def link(i):
                    step[0] += 1
                    i.then_inc(r_link.sem, 1)
                    dve.wait_ge(r_link.sem, r_link.at(b, step[0]))

                spread = lambda a: a.unsqueeze(2).to_broadcast([P, NT, E])
                flat = lambda a: a[:, :, :].rearrange("p t e -> p (t e)")
                raw = bank[0][:, 0:NT * E].rearrange("p (t e) -> p t e", t=NT)
                link(nc.vector.tensor_reduce(r4[:, 0, :], raw, AX.X, ALU.max))
                nc.vector.tensor_tensor(lg[:, :, :], raw, spread(r4[:, 0, :]), ALU.subtract).then_inc(r_ex.sem, 1)
                dve.wait_ge(r_exp.sem, r_exp.at(b, 1))
                link(nc.vector.tensor_reduce(r4[:, 1, :], sm[:, :, :], AX.X, ALU.add))
                link(nc.vector.reciprocal(r4[:, 1, :], r4[:, 1, :]))
                nc.vector.tensor_tensor(sm[:, :, :], sm[:, :, :], spread(r4[:, 1, :]), ALU.mult).then_inc(r_rep.sem, 1)
                dve.wait_ge(r_rep.sem, r_rep.at(b, 1))
                nc.vector.memset(idle[:, :], 0.0)
                for t in range(NT):
                    i = nc.vector.max(out=top[:, t, :], in_=sm[:, t, :])
                i.then_inc(r_link.sem, 1)
                step[0] += 1
                dve.wait_ge(r_link.sem, r_link.at(b, step[0]))
                nc.vector.memset(idle[:, :], 0.0)
                for t in range(NT):
                    i = nc.vector.match_replace(out=rep[:, t, :], in_to_replace=top[:, t, :], in_values=sm[:, t, :], imm_value=-1.0)
                link(i)
                nc.vector.tensor_scalar(chosenb[:, :, :], rep[:, :, :], 0.0, None, ALU.is_lt).then_inc(r_mask.sem, 1)
                link(nc.vector.tensor_scalar(chosen[:, :, :], rep[:, :, :], 0.0, None, ALU.is_lt))
                nc.vector.tensor_tensor_scan(nth[:, :], keep[:, :], flat(chosen), 0.0, ALU.mult, ALU.add)
                link(nc.vector.tensor_tensor(gate[:, :, :], sm[:, :, :], chosen[:, :, :], ALU.mult))
                nc.vector.tensor_tensor(nth[:, :], nth[:, :], flat(chosen), ALU.mult)
                link(nc.vector.tensor_reduce(r4[:, 2, :], gate[:, :, :], AX.X, ALU.add))
                link(nc.vector.reciprocal(r4[:, 2, :], r4[:, 2, :]))
                nc.vector.tensor_tensor(gate[:, :, :], gate[:, :, :], spread(r4[:, 2, :]), ALU.mult)
                dve.wait_ge(rk_mm.sem, rk_mm.at(b, 1))
                nc.vector.tensor_tensor(flat(slot), bank[0][:, 128:128 + NT * E], base[:, :], ALU.add).then_inc(r_link.sem, 1)
                step[0] += 1
                link(nc.vector.tensor_tensor(hit[:, :, :], nth[:, :].unsqueeze(1).to_broadcast([P, TOPK, NT * E]), rank[:, :, :], ALU.is_equal))
                link(nc.vector.tensor_tensor(slot[:, :, :], slot[:, :, :], counts[:, :].unsqueeze(1).to_broadcast([P, NT, E]), ALU.add))
                nc.vector.tensor_tensor(counts[:, :], counts[:, :], bank[1][:, 0:E], ALU.add)
                link(nc.vector.tensor_tensor(hit2[:, :, :], hit[:, :, :], flat(slot).unsqueeze(1).to_broadcast([P, TOPK, NT * E]), ALU.mult))
                nc.vector.tensor_reduce(posf[:, :], hit2[:, :, :].rearrange("p k (t e) -> p (k t) e", e=E), AX.X, ALU.add)
                link(nc.vector.tensor_tensor(hit[:, :, :], hit[:, :, :], flat(gate).unsqueeze(1).to_broadcast([P, TOPK, NT * E]), ALU.mult))
                link(nc.vector.tensor_reduce(gatek[:, :], hit[:, :, :].rearrange("p k (t e) -> p (k t) e", e=E), AX.X, ALU.add))
                dve.wait_ge(tb_st.sem, tb_st.at(b, KT))
                nc.vector.tensor_copy(pos[:, :], posf[:, :])
                nc.vector.tensor_copy(pay[:, :, 1].bitcast(F32), gatek[:, :])
                for k in range(TOPK):
                    i = nc.vector.tensor_copy(pay[:, k * NT:(k + 1) * NT, 0], tokf[:, :])
                i.then_inc(r_pos.sem, 1)
                dve.wait_ge(r_pos.sem, r_pos.at(b, 1))
                nc.vector.tensor_scalar(tokf[:, :], tokf[:, :], float(S), None, ALU.add).then_inc(r_tok.sem, 1)

            dve.wait_ge(s_const.sem, N_CONST * 16)
            nc.vector.memset(counts[:, :], 0.0).then_inc(s_mg.sem, 1)
            with dve.Fori(0, B) as b:
                dve.wait_ge(x_ld.sem, x_ld.at(b, 1))
                layer_norm(b, 0, x)
                halves_lo(b, 0)
                for i in range(8):
                    dve.wait_ge(qk_hi_ok.sem, qk_hi_ok.at(b, i + 1))
                    nc.vector.scalar_tensor_tensor(out=qk_lo[:, i, :], in0=bank[(4 + i) % 8], scalar=b_qk[:, i:i + 1],
                                                   in1=qk_hi[:, i, :], op0=ALU.add, op1=ALU.subtract).then_inc(qk_lo_ok.sem, 1)
                for t in range(NT):
                    dve.wait_ge(v_mm.sem, v_mm.at(b, t + 1))
                    nc.vector.tensor_tensor(o32[:, t, :], bank[4 + t], b_v[:, :], ALU.add).then_inc(v32_ok.sem, 1)
                for t in range(NT):
                    dve.wait_ge(v_hi_ok.sem, v_hi_ok.at(b, t + 1))
                    nc.vector.tensor_tensor(v_lo[:, t, :, :], o32[:, t, :].rearrange("p (h d) -> p h d", h=H),
                                            v_hi[:, t, :, 0:HD], ALU.subtract).then_inc(v_lo_ok.sem, 1)
                with dve.Fori(0, PAIRS) as hp:
                    for u, cuts in enumerate((((3, 0, 512),), ((2, 0, 384), (0, 384, 512)), ((1, 0, 256),))):
                        dve.wait_ge(s_mm.sem, s_mm.at(b, u + 1) + 3 * hp)
                        for t, c0, c1 in cuts:
                            i = nc.vector.tensor_reduce(mx[:, t, bass.ts(hp, 2)], ps[:, 2 * u:2 * u + 2, c0:c1], AX.X, ALU.max)
                        i.then_inc(s_max.sem, 1)
                with dve.Fori(0, PAIRS) as hp:
                    for i in range(2):
                        dve.wait_ge(pv_mm.sem, pv_mm.at(b, i + 1) + 2 * hp)
                        o = bank[6 + i][:, 0:NT * (HD + 1)].rearrange("p (t c) -> p t c", t=NT)
                        nc.vector.reciprocal(rden[:, i, :], o[:, :, HD]).then_inc(rec_ok.sem, 1)
                        dve.wait_ge(rec_ok.sem, rec_ok.at(b, i + 1) + 2 * hp)
                        dst = o32[:, :, :].rearrange("p t (g i d) -> p t g i d", i=2, d=HD)[:, :, bass.ts(hp, 1), i, :].rearrange("p t a d -> p t (a d)")
                        nc.vector.tensor_tensor(dst, o[:, :, 0:HD],
                                                rden[:, i, :].unsqueeze(2).to_broadcast([P, NT, HD]), ALU.mult).then_inc(norm_ok.sem, 1)
                    dve.wait_ge(ew_hi.sem, ew_hi.at(b, 1) + hp)
                    nc.vector.tensor_tensor(wst2[:, 1, :], w2f[:, 0, :], wst2[:, 0, :], ALU.subtract)
                    nc.vector.tensor_tensor(wst2[64:P, 2, :], w2f[64:P, 1, :], wst2[64:P, 2, :], ALU.subtract).then_inc(ew_lo2.sem, 1)
                halves_lo(b, 4)
                dve.wait_ge(out_st.sem, out_st.at(b, 0))
                for t in range(NT):
                    dve.wait_ge(wo_mm.sem, wo_mm.at(b, t + 1))
                    if t == 0:
                        dve.wait_ge(xbo_ok.sem, xbo_ok.at(b, 4))
                    nc.vector.tensor_tensor(x1[:, t, :], bank[4 + t], x[:, t, :], ALU.add).then_inc(x1_ok.sem, 1)
                dve.wait_ge(x1_ok.sem, x1_ok.at(b, 4))
                layer_norm(b, 1, x1)
                for lin in range(2):
                    scales(b, lin)
                    scaled_rows(b, lin, 1)
                    scaled_rows(b, lin, 0)
                    clip(b, lin, 1)
                    weight_steps(b, lin)
                    clip(b, lin, 0)
                    weight_steps_out(b, lin)
                    if lin == 0:
                        for t in range(NT):
                            dve.wait_ge(l_mm.sem, l_mm.at(b, t + 1))
                            nc.vector.scalar_tensor_tensor(out=o32[:, t, :], in0=bank[t], scalar=rscale[:, 0, t:t + 1],
                                                           in1=wscb[:, :], op0=ALU.mult, op1=ALU.mult).then_inc(l_ok.sem, 1)
                        for t in range(NT):
                            dve.wait_ge(th_ok.sem, th_ok.at(b, t + 1))
                            nc.vector.scalar_tensor_tensor(out=act[:, t, :], in0=th[:, t, :], scalar=1.0, in1=o32[:, t, 0:QI],
                                                           op0=ALU.add, op1=ALU.mult).then_inc(a1_ok.sem, 1)
                        for t in range(NT):
                            dve.wait_ge(a1_ok.sem, a1_ok.at(b, t + 1))
                            nc.vector.scalar_tensor_tensor(out=act[:, t, :], in0=act[:, t, :], scalar=0.5, in1=o32[:, t, QI:2 * QI],
                                                           op0=ALU.mult, op1=ALU.mult).then_inc(a_ok.sem, 1)
                    else:
                        for t in range(NT):
                            dve.wait_ge(l_mm.sem, l_mm.at(b, 4 + t + 1))
                            nc.vector.scalar_tensor_tensor(out=o32[:, t, :], in0=bank[t], scalar=rscale[:, 0, t:t + 1],
                                                           in1=wscb[:, :], op0=ALU.mult, op1=ALU.mult).then_inc(l_ok.sem, 1)
                        for t in range(NT):
                            dve.wait_ge(l_ok.sem, l_ok.at(b, 4 + t + 1))
                            nc.vector.tensor_tensor(x1[:, t, :], o32[:, t, :], x1[:, t, :], ALU.add).then_inc(x2_ok.sem, 1)
                dve.wait_ge(x2_ok.sem, x2_ok.at(b, 4))
                layer_norm(b, 2, x1)
                halves_lo(b, 8)
                dve.wait_ge(lg_mm.sem, lg_mm.at(b, 1))
                route(b)

        @block.tensor
        def _(pe):
            pe.wait_ge(s_one.sem, 7)
            pe.wait_ge(s_const.sem, N_CONST * 16)
            pe.wait_ge(s_wlo.sem, 5)

            def transposes(src, banks, sem):
                for k in range(KD):
                    for t in range(NT):
                        i = nc.tensor.transpose(bank[banks + k][:, t * P:(t + 1) * P], src[:, t, k * P:(k + 1) * P], eye32[:, :])
                    i.then_inc(sem, 1)

            def three(out_ap, lh, ll, rh, rl):
                n = len(lh)
                for k in range(n):
                    nc.tensor.matmul(out_ap, lh[k], rh[k], start=(k == 0), stop=False)
                    nc.tensor.matmul(out_ap, lh[k], rl[k], start=False, stop=False)
                    i = nc.tensor.matmul(out_ap, ll[k], rh[k], start=False, stop=(k == n - 1))
                return i

            def one_head(operand, rows, h, c0, c1):
                return operand[0:rows, bass.ds(h, 1), c0:c1].rearrange("p a c -> p (a c)")

            def score_maxima(b, hp, first):
                for u, cuts in enumerate((((3, 0),), ((2, 0), (0, 384)), ((1, 0),))):
                    if not first:
                        pe.wait_ge(s_max.sem, s_max.at(b, u - 2) + 3 * hp)
                    for t, c in cuts:
                        for i in range(2):
                            o = ps[:, 2 * u + i, c:c + (t + 1) * P]
                            nc.tensor.matmul(o, one_head(qop, KB, 2 * hp + i, t * P, (t + 1) * P),
                                             one_head(kop, KB, 2 * hp + i, 0, (t + 1) * P), start=True, stop=False)
                            n = nc.tensor.matmul(o[:, t * P:(t + 1) * P], eyeb[:, :], mask_qk[:, :], start=False, stop=True)
                    n.then_inc(s_mm.sem, 1)

            def scores_T(b, h, i, first=False):
                if not first:
                    pe.wait_ge(ehi_ok.sem, ehi_ok.at(b, -1) + h)
                for j in range(NT):
                    bk_, c = divmod(POFF[j], 512)
                    o = ps[:, 3 * i + bk_, c:c + S - j * P]
                    nc.tensor.matmul(o, one_head(kop, KM, h, j * P, (j + 1) * P), one_head(qop, KM, h, j * P, S), start=True, stop=False)
                    n = nc.tensor.matmul(o[:, 0:P], eyeb[:, :], mask_kq[:, :], start=False, stop=True)
                n.then_inc(st_mm.sem, 1)

            def values(b, h, i, first=False):
                pe.wait_ge(elo_ok.sem, elo_ok.at(b, 1) + h)
                if not first:
                    pe.wait_ge(norm_ok.sem, norm_ok.at(b, -1) + h)
                for t in range(NT):
                    o = bank[6 + i][:, t * (HD + 1):(t + 1) * (HD + 1)]
                    for j in range(t + 1):
                        c = POFF[j] + (t - j) * P
                        vh = v_hi[:, j, bass.ds(h, 1), :].rearrange("p a c -> p (a c)")
                        vl = v_lo[:, j, bass.ds(h, 1), :].rearrange("p a c -> p (a c)")
                        nc.tensor.matmul(o, p_hi[:, i, c:c + P], vh, start=(j == 0), stop=False)
                        nc.tensor.matmul(o[:, 0:HD], p_hi[:, i, c:c + P], vl, start=False, stop=False)
                        n = nc.tensor.matmul(o, p_lo[:, i, c:c + P], vh, start=False, stop=(j == t))
                n.then_inc(pv_mm.sem, 1)

            def quantised(b, lin):
                n = (KD, 2)[lin]
                for side, src in ((0, (xn, act)[lin]), (1, (fw, cw)[lin])):
                    if side == 1:
                        ld = (fw_ld, cw_ld)[lin]
                        pe.wait_ge(ld.sem, ld.at(b, 1))
                    elif lin == 0:
                        pe.wait_ge(xn_ok.sem, xn_ok.at(b, 8))
                    else:
                        pe.wait_ge(a_ok.sem, a_ok.at(b, 4))
                    for k in range(n):
                        bk_ = (4 * side, 4 + 2 * side)[lin] + k
                        for t in range(4):
                            i = nc.tensor.transpose(bank[bk_][:, t * P:(t + 1) * P], src[:, t, k * P:(k + 1) * P], eye32[:, :])
                        i.then_inc(am_mm.sem, 1)
                for m, side in enumerate((1, 0)):
                    pe.wait_ge(dg_ok.sem, dg_ok.at(b, 2 * lin + m + 1))
                    for k in range(n):
                        i = nc.tensor.matmul(bank[(0, 4)[lin] + side][:, k * P:(k + 1) * P], ones32[:, :], dg[:, side, k, :],
                                             start=True, stop=True)
                    i.then_inc(bc_mm.sem, 1)
                for m, (side, src) in enumerate(((1, wqz), (0, xq))):
                    pe.wait_ge(q3_ok.sem, q3_ok.at(b, 8 * lin + 4 * m + 4))
                    for k in range(n):
                        bk_ = (((2, 4)[side] + k // 2), (6, 7)[side])[lin]
                        for t in range(4):
                            c = (k % 2) * 512 + t * P
                            i = nc.tensor.transpose(psb[:, bk_, c:c + P], src[:, t, k * P:(k + 1) * P], eyeb[:, :])
                        if k % 2 == 1:
                            i.then_inc(qt_mm.sem, 1)
                pe.wait_ge(wd_ok.sem, wd_ok.at(b, lin + 1))
                for t in range(4):
                    i = nc.tensor.matmul(bank[(6, 4)[lin]][:, t * P:(t + 1) * P], ones32[:, :], dg[:, 1, t, :], start=True, stop=True)
                i.then_inc(wd_mm.sem, 1)
                pe.wait_ge(qt_ok.sem, qt_ok.at(b, (4, 6)[lin]))
                for t in range(NT):
                    for k in range(n):
                        i = nc.tensor.matmul(bank[t], xqT[:, k, t * P:(t + 1) * P], wqT[:, k, :], start=(k == 0), stop=(k == n - 1))
                    i.then_inc(l_mm.sem, 1)

            tiles = lambda a, t: [a[:, k, t * P:(t + 1) * P] for k in range(KD)]
            cols = lambda a: [a[:, k, :] for k in range(KD)]
            with pe.Fori(0, B) as b:
                pe.wait_ge(xn_ok.sem, xn_ok.at(b, 4))
                transposes(xn, 0, t_mm.sem)
                pe.wait_ge(t_lo_ok.sem, t_lo_ok.at(b, 4))
                for i in range(8):
                    w, g = i // 4, i % 4
                    three(bank[(4 + i) % 8], tiles(w_hi[:, w], g), tiles(w_lo[:, w], g), cols(t_hi), cols(t_lo)).then_inc(qk_mm.sem, 1)
                for t in range(NT):
                    pe.wait_ge(qk_lo_ok.sem, qk_lo_ok.at(b, t + 1))
                    three(bank[4 + t], tiles(t_hi, t), tiles(t_lo, t), cols(w_hi[:, 2]), cols(w_lo[:, 2])).then_inc(v_mm.sem, 1)
                pe.wait_ge(qk_lo_ok.sem, qk_lo_ok.at(b, 8))
                pe.wait_ge(v32_ok.sem, v32_ok.at(b, 4))
                pe.wait_ge(op_ld.sem, op_ld.at(b, 24))
                for g in range(2):
                    if g == 0:
                        score_maxima(b, 0, True)
                    with pe.Fori((1, 4)[g], (4, 8)[g]) as hp:
                        score_maxima(b, hp, False)
                    pe.wait_ge(s_max.sem, s_max.at(b, 12 * g + 12))
                    if g == 1:
                        pe.wait_ge(m_row_ok.sem, m_row_ok.at(b, 1))
                    for t in range(NT):
                        n = nc.tensor.transpose(ps[0:H // 2, 6, t * P:(t + 1) * P], mx[:, t, 8 * g:8 * g + 8], eye32[:, :])
                    n.then_inc(m_mm.sem, 1)
                pe.wait_ge(m_ld.sem, m_ld.at(b, 2))
                pe.wait_ge(v_lo_ok.sem, v_lo_ok.at(b, 4))
                scores_T(b, 0, 0, True)
                scores_T(b, 1, 1, True)
                values(b, 0, 0, True)
                scores_T(b, 2, 0)
                values(b, 1, 1, True)
                with pe.Fori(1, PAIRS - 1) as hp:
                    scores_T(b, 2 * hp + 1, 1)
                    values(b, 2 * hp, 0)
                    scores_T(b, 2 * hp + 2, 0)
                    values(b, 2 * hp + 1, 1)
                scores_T(b, H - 1, 1)
                values(b, H - 2, 0)
                values(b, H - 1, 1)
                pe.wait_ge(norm_ok.sem, norm_ok.at(b, H))
                transposes(o32, 0, t_mm.sem)
                pe.wait_ge(t_lo_ok.sem, t_lo_ok.at(b, 8))
                for t in range(NT):
                    three(bank[4 + t], tiles(t_hi, t), tiles(t_lo, t), cols(w_hi[:, 3]), cols(w_lo[:, 3])).then_inc(wo_mm.sem, 1)
                quantised(b, 0)
                quantised(b, 1)
                pe.wait_ge(xn_ok.sem, xn_ok.at(b, 12))
                transposes(xn, 4, t_mm.sem)
                pe.wait_ge(t_lo_ok.sem, t_lo_ok.at(b, 12))
                for t in range(NT):
                    n = three(bank[0][:, t * E:(t + 1) * E], tiles(t_hi, t), tiles(t_lo, t), cols(g_hi), cols(g_lo))
                n.then_inc(lg_mm.sem, 1)
                pe.wait_ge(r_mask.sem, r_mask.at(b, 1))
                for t in range(NT):
                    for u in range(t + 1):
                        nc.tensor.matmul(bank[0][:, 128 + t * E:128 + (t + 1) * E], (onesb, before)[u == t][:, :], chosenb[:, u, :],
                                         start=(u == 0), stop=(u == t))
                for t in range(NT):
                    n = nc.tensor.matmul(bank[1][:, 0:E], onesb[:, :], chosenb[:, t, :], start=(t == 0), stop=(t == NT - 1))
                n.then_inc(rk_mm.sem, 1)



def expert_part(nc, eye32_c, eye16_c, tile_c, counts, split_w, x3_rows, table, out):
    with ExitStack() as ctx:
        def sb(name, shape, dt):
            return ctx.enter_context(nc.sbuf_tensor(name, shape, dt))

        def sem(name):
            return ctx.enter_context(nc.semaphore(name))

        ps = ctx.enter_context(nc.psum_tensor("ps2", [P, 8, 512], F32))
        ps16 = ps[:, :, :].bitcast(F16)
        XT, GU, HT, Y = 0, 2, 4, 6
        COLS = 2 * P

        eye32, eye16, tile_no = sb("eye32b", [P, P], F32), sb("eye16b", [P, P], F16), sb("tile_no", [P, 2], F32)
        need, first, le, row1 = sb("need", [P, E], F32), sb("first", [P, E], F32), sb("le", [P, 2, E], F32), sb("row1", [P, E], F32)
        first_i = sb("first_i", [P, E], I32)
        own = sb("own", [P, 4, 2], F32)
        block_i = sb("block_i", [P, 2], I32)
        lists = sb("lists", [P, 2, P, 2], I32)
        listf = sb("listf", [P, 2, P], F32)
        tokens = sb("tokens", [P, COLS], I32)
        gates = sb("gates", [P, COLS], F32)
        weight_at, weight_no = sb("weight_at", [1, COLS], I32), sb("weight_no", [1, COLS], I32)
        wbuf = sb("wbuf", [P, 2 * (WC + W2C)], F16)
        xg = sb("xg", [P, 2, 2 * D], F16)
        xT = sb("xT", [P, 2, 2 * D], F16)
        idx_g, idx_s, gcol = sb("idx_g", [P, 2], I32), sb("idx_s", [P, 2], I32), sb("gcol", [P, 2], F32)
        th, h1, h = sb("th2", [P, 2, F], F32), sb("h1", [P, 2, F], F32), sb("h", [P, 2, 2 * P], F32)
        hT_hi, hT_lo = sb("hT_hi", [P, 2, 2 * P], F16), sb("hT_lo", [P, 2, 2 * P], F16)
        y = sb("y", [P, 2, D], F32)
        idle_p, idle_q, pacer = sb("idle_p2", [P, 1], F32), sb("idle_q", [P, 1], F32), sb("pacer", [P, 1], F32)

        s_in, s_plan, s_blk, s_list = sem("s_in"), sem("s_plan"), sem("s_blk"), sem("s_list")
        s_lt, s_tr, s_out, s_ready = sem("s_lt"), sem("s_tr"), sem("s_out_lists"), sem("s_ready")
        idx_ok, g_done, xt_mm, xt_ok = sem("idx_ok"), [sem("g_done0"), sem("g_done1")], sem("xt_mm"), sem("xt_ok")
        gu_mm, th_ok, h1_ok, h_ok = sem("gu_mm"), sem("th2_ok"), sem("h1_ok"), sem("h_ok")
        ht_mm, hth_ok, htl_ok, y_mm, y_ok = sem("ht_mm"), sem("hth_ok"), sem("htl_ok"), sem("y_mm"), sem("y_ok")
        acc_st, w_ld, s_idle = sem("acc_st"), sem("w_ld"), sem("s_idle")
        s_pace = sem("s_pace")

        block = ctx.enter_context(nc.Block())

        @block.sync
        def _(sp):
            sp.dma_start(eye32[:, :], eye32_c).then_inc(s_in, 16)
            sp.dma_start(eye16[:, :], eye16_c).then_inc(s_in, 16)
            sp.dma_start(tile_no[:, :], tile_c).then_inc(s_in, 16)
            sp.dma_start(wbuf[:, 0:WC + W2C], split_w[0]).then_inc(w_ld, 16)
            sp.wait_ge(w_ld, 16)
            sp.dma_start(wbuf[:, WC + W2C:2 * (WC + W2C)], split_w[1]).then_inc(w_ld, 16)
            sp.wait_ge(w_ld, 32)
            sp.wait_ge(s_ready, 1)
            with sp.Fori(1, E // 2) as n:
                for side in range(2):
                    done = sp.value_load(first_i[0:1, bass.ds(2 * n + side - 1, 1)], min_val=0, max_val=TILES)
                    sp.wait_ge(y_mm, done)
                    sp.dma_start(wbuf[:, side * (WC + W2C):(side + 1) * (WC + W2C)], split_w[2 * n + side]).then_inc(w_ld, 16)
                    sp.wait_ge(w_ld, 32 * n + 16 * side + 16)
                    sp.dma_start(pacer[0:1, 0:1], eye32_c[0:1, 0:1]).then_inc(s_pace, 16)
            sp.wait_ge(s_pace, 16 * (E - 2))
            sp.wait_ge(acc_st, 16 * TILES)

        @block.gpsimd
        def _(pool):
            pool.wait_ge(s_blk, 1)
            for c in range(2):
                n = (P, TILES - P)[c]
                nc.gpsimd.indirect_dma_start(lists[0:n, c, :, :].rearrange("p s a -> p (s a)"), None,
                                             table.rearrange("(t s) a -> t (s a)", s=P),
                                             bass.IndirectOffsetOnAxis(ap=block_i[0:n, c:c + 1], axis=0)).then_inc(s_list, 16)

            nc.gpsimd.memset(idle_p[:, :], 0.0).then_inc(s_idle, 1)
            pool.wait_ge(s_idle, 1)

            def carry(n):
                pool.wait_ge(s_idle, n)
                nc.gpsimd.tensor_tensor(idle_q[:, :], idle_p[:, :], idle_p[:, :], ALU.add).then_inc(s_idle, 1)

            def gather(i, p, n):
                pool.wait_ge(idx_ok, i + 1)
                carry(n)
                nc.gpsimd.indirect_dma_start(xg[:, p, :], None, x3_rows,
                                             bass.IndirectOffsetOnAxis(ap=idx_g[:, p:p + 1], axis=0)).then_inc(g_done[p], 16)

            def scatter(i, p, first=False):
                if not first:
                    pool.wait_ge(acc_st, 16 * i)
                carry(3 * i + 4)
                pool.wait_ge(y_ok, i + 1)
                carry(3 * i + 5)
                nc.gpsimd.indirect_dma_start(out, bass.IndirectOffsetOnAxis(ap=idx_s[:, p:p + 1], axis=0),
                                             y[:, p, :], None, compute_op=ALU.add).then_inc(acc_st, 16)

            gather(0, 0, 1)
            gather(1, 1, 2)
            for p in range(2):
                gather(p + 2, p, 3 * p + 3)
                scatter(p, p, p == 0)
            with pool.Fori(1, TILES // 2 - 1) as j:
                for p in range(2):
                    gather(2 * j + p + 2, p, 6 * j + 3 * p + 3)
                    scatter(2 * j + p, p)
            for p in range(2):
                i = TILES - 2 + p
                pool.wait_ge(acc_st, 16 * i)
                carry(3 * (TILES - 2) + 3 + 2 * p)
                pool.wait_ge(y_ok, i + 1)
                carry(3 * (TILES - 2) + 4 + 2 * p)
                nc.gpsimd.indirect_dma_start(out, bass.IndirectOffsetOnAxis(ap=idx_s[:, p:p + 1], axis=0),
                                             y[:, p, :], None, compute_op=ALU.add).then_inc(acc_st, 16)

        @block.scalar
        def _(act_e):
            def steps(i, p, first=False):
                act_e.wait_ge(gu_mm, i + 1)
                nc.scalar.activation(th[:, p, :], ps[:, GU + p, 0:F], ACT.Tanh, scale=0.5).then_inc(th_ok, 1)
                act_e.wait_ge(ht_mm, i + 1)
                nc.scalar.copy(hT_hi[:, p, :], ps[:, HT + p, 0:2 * P]).then_inc(hth_ok, 1)
                if not first:
                    act_e.wait_ge(acc_st, 16 * (i - 1))
                act_e.wait_ge(y_mm, i + 1)
                nc.scalar.activation(y[:, p, :], ps[:, Y + p, :], ACT.Copy, scale=gcol[:, p:p + 1]).then_inc(y_ok, 1)

            for p in range(2):
                steps(p, p, True)
            with act_e.Fori(1, TILES // 2) as j:
                for p in range(2):
                    steps(2 * j + p, p)

        @block.vector
        def _(dve):
            count = [0]

            def link(i):
                count[0] += 1
                i.then_inc(s_plan, 1)
                dve.wait_ge(s_plan, count[0])

            link(nc.vector.tensor_scalar(need[:, :], counts[:, :], 1.0 / P, (P - 1.0) / P - 0.5 + 0.5 / P, ALU.mult, ALU.add))
            link(nc.vector.tensor_scalar(need[:, :], need[:, :], MAGIC, MAGIC, ALU.add, ALU.subtract))
            link(nc.vector.tensor_scalar(need[:, :], need[:, :], 1.0, None, ALU.max))
            link(nc.vector.memset(row1[:, :], 1.0))
            link(nc.vector.tensor_tensor_scan(first[:, :], row1[:, :], need[:, :], 0.0, ALU.mult, ALU.add))
            link(nc.vector.tensor_tensor(first[:, :], first[:, :], need[:, :], ALU.subtract))
            link(nc.vector.tensor_copy(first_i[:, :], first[:, :]))
            dve.wait_ge(s_in, 48)
            for c in range(2):
                link(nc.vector.tensor_scalar(le[:, c, :], first[:, :], tile_no[:, c:c + 1], None, ALU.is_le))
            link(nc.vector.tensor_reduce(own[:, 0, :], le[:, :, :], AX.X, ALU.add))
            for c in range(2):
                link(nc.vector.tensor_tensor(le[:, c, :], le[:, c, :], first[:, :], ALU.mult))
            link(nc.vector.tensor_reduce(own[:, 1, :], le[:, :, :], AX.X, ALU.max))
            link(nc.vector.tensor_scalar(own[:, 2, :], own[:, 0, :], -1.0, float(BLOCKS), ALU.add, ALU.mult))
            link(nc.vector.tensor_tensor(own[:, 2, :], own[:, 2, :], own[:, 1, :], ALU.subtract))
            link(nc.vector.tensor_tensor(own[:, 2, :], own[:, 2, :], tile_no[:, :], ALU.add))
            nc.vector.tensor_copy(block_i[:, :], own[:, 2, :]).then_inc(s_blk, 1)
            link(nc.vector.tensor_scalar(own[:, 3, :], own[:, 0, :], 0.5, -0.75, ALU.mult, ALU.add))
            link(nc.vector.tensor_scalar(own[:, 3, :], own[:, 3, :], MAGIC, MAGIC, ALU.add, ALU.subtract))
            link(nc.vector.tensor_scalar(own[:, 3, :], own[:, 3, :], -2.0, -1.0, ALU.mult, ALU.add))
            link(nc.vector.tensor_tensor(own[:, 3, :], own[:, 3, :], own[:, 0, :], ALU.add))
            link(nc.vector.tensor_scalar(own[:, 3, :], own[:, 3, :], float(WC + W2C), None, ALU.mult))
            link(nc.vector.tensor_scalar(own[:, 1, :], own[:, 0, :], 16.0, None, ALU.mult))
            nc.vector.memset(listf[:, :, :], 0.0)
            link(nc.vector.memset(tokens[:, :], 0))
            dve.wait_ge(s_list, 32)
            for c in range(2):
                n = (P, TILES - P)[c]
                i = nc.vector.tensor_copy(listf[0:n, c, :], lists[0:n, c, :, 0])
            i.then_inc(s_lt, 1)
            dve.wait_ge(s_tr, 1)
            nc.vector.tensor_copy(tokens[:, 0:TILES], ps[:, 0, 0:TILES])
            nc.vector.tensor_copy(gates[:, 0:TILES], ps[:, 1, 0:TILES])
            nc.vector.tensor_copy(weight_at[:, :], ps[0:1, 2, 0:COLS])
            nc.vector.tensor_copy(weight_no[:, :], ps[0:1, 3, 0:COLS]).then_inc(s_ready, 1)
            dve.wait_ge(s_ready, 1)

            def index_gather(i, p, first=False):
                if not first:
                    dve.wait_ge(g_done[p], 8 * (i - p))
                nc.vector.tensor_copy(idx_g[:, p:p + 1], tokens[:, bass.ds(i, 1)]).then_inc(idx_ok, 1)

            def x_out(i, p, first=False):
                dve.wait_ge(xt_mm, i + 1)
                nc.vector.tensor_copy(xT[:, p, :], ps16[:, XT + p, :]).then_inc(xt_ok, 1)

            def hidden(i, p, first=False):
                dve.wait_ge(th_ok, i + 1)
                nc.vector.scalar_tensor_tensor(out=h1[:, p, :], in0=th[:, p, :], scalar=1.0, in1=ps[:, GU + p, 0:F],
                                               op0=ALU.add, op1=ALU.mult).then_inc(h1_ok, 1)
                dve.wait_ge(h1_ok, i + 1)
                nc.vector.scalar_tensor_tensor(out=h[:, p, 0:P], in0=h1[:, p, 0:P], scalar=0.5, in1=ps[:, GU + p, F:F + P],
                                               op0=ALU.mult, op1=ALU.mult)
                twice = lambda a: a.unsqueeze(1).to_broadcast([P, 2, F - P])
                nc.vector.scalar_tensor_tensor(out=h[:, p, P:2 * P].rearrange("p (a c) -> p a c", a=2), in0=twice(h1[:, p, P:F]), scalar=0.5,
                                               in1=twice(ps[:, GU + p, F + P:2 * F]), op0=ALU.mult, op1=ALU.mult).then_inc(h_ok, 1)

            def h_out(i, p, first=False):
                if not first:
                    dve.wait_ge(acc_st, 16 * (i - 1))
                nc.vector.tensor_copy(idx_s[:, p:p + 1], tokens[:, bass.ds(i, 1)])
                nc.vector.tensor_copy(gcol[:, p:p + 1], gates[:, bass.ds(i, 1)])
                dve.wait_ge(hth_ok, i + 1)
                nc.vector.tensor_tensor(hT_lo[:, p, :], ps[:, HT + p, 0:2 * P], hT_hi[:, p, :], ALU.subtract).then_inc(htl_ok, 1)

            for i in range(4):
                index_gather(i, i % 2, i < 2)
                if i < 2:
                    x_out(i, i)
            for i in range(2):
                hidden(i, i, True)
                x_out(i + 2, i) 
                index_gather(i + 4, i)
                h_out(i, i, True)
            with dve.Fori(1, TILES // 2 - 2) as j:
                for p in range(2):
                    i = 2 * j + p
                    hidden(i, p)
                    x_out(i + 2, p)
                    index_gather(i + 4, p)
                    h_out(i, p)
            for i in range(TILES - 4, TILES):
                hidden(i, i % 2)
                if i < TILES - 2:
                    x_out(i + 2, i % 2)
                h_out(i, i % 2)

        @block.tensor
        def _(pe):
            pe.wait_ge(s_in, 48)
            pe.wait_ge(s_lt, 1)
            for c in range(2):
                n = (P, TILES - P)[c]
                nc.tensor.transpose(ps[:, 0, c * P:c * P + n], listf[0:n, c, :], eye32[0:n, 0:n])
                nc.tensor.transpose(ps[:, 1, c * P:c * P + n], lists[0:n, c, :, 1].bitcast(F32), eye32[0:n, 0:n])
                nc.tensor.transpose(ps[0:1, 2, c * P:(c + 1) * P], own[:, 3, c:c + 1], eye32[:, :])
                m = nc.tensor.transpose(ps[0:1, 3, c * P:(c + 1) * P], own[:, 1, c:c + 1], eye32[:, :])
            m.then_inc(s_tr, 1)
            pe.wait_ge(s_ready, 1)

            def x_in(i, p, first=False):
                pe.wait_ge(g_done[p], 8 * (i - p) + 16)
                if not first:
                    pe.wait_ge(xt_ok, i - 1)
                for k in range(2 * KD):
                    n = nc.tensor.transpose(ps16[:, XT + p, k * P:(k + 1) * P], xg[:, p, k * P:(k + 1) * P], eye16[:, :])
                n.then_inc(xt_mm, 1)

            def up(i, p, first=False):
                at = pe.value_load(weight_at[0:1, bass.ds(i, 1)], min_val=0, max_val=WC + W2C)
                no = pe.value_load(weight_no[0:1, bass.ds(i, 1)], min_val=16, max_val=16 * E)
                pe.wait_ge(w_ld, no)
                pe.wait_ge(xt_ok, i + 1)
                if not first:
                    pe.wait_ge(h_ok, i - 1)
                o = ps[:, GU + p, 0:2 * F]
                for k in range(KD):
                    hi, lo = xT[:, p, k * P:(k + 1) * P], xT[:, p, (KD + k) * P:(KD + k + 1) * P]
                    w_hi = wbuf[:, bass.ds(at + k * 4 * F, 2 * F)]
                    w_lo = wbuf[:, bass.ds(at + k * 4 * F + 2 * F, 2 * F)]
                    nc.tensor.matmul(o, hi, w_hi, start=(k == 0), stop=False)
                    nc.tensor.matmul(o, hi, w_lo, start=False, stop=False)
                    n = nc.tensor.matmul(o, lo, w_hi, start=False, stop=(k == KD - 1))
                n.then_inc(gu_mm, 1)

            def turn(i, p, first=False):
                pe.wait_ge(h_ok, i + 1)
                if not first:
                    pe.wait_ge(htl_ok, i - 1)
                nc.tensor.transpose(ps[:, HT + p, 0:P], h[:, p, 0:P], eye32[:, :])
                n = nc.tensor.transpose(ps[:, HT + p, P:2 * P], h[:, p, P:2 * P], eye32[:, :])
                n.then_inc(ht_mm, 1)

            def down(i, p, first=False):
                at = pe.value_load(weight_at[0:1, bass.ds(i, 1)], min_val=0, max_val=WC + W2C)
                pe.wait_ge(htl_ok, i + 1)
                if not first:
                    pe.wait_ge(y_ok, i - 1)
                w = [wbuf[:, bass.ds(at + WC + a * D, D)] for a in range(3)]
                for n, (l, r) in enumerate(((hT_hi[:, p, 0:P], w[0]), (hT_hi[:, p, 0:P], w[1]), (hT_lo[:, p, 0:P], w[0]),
                                            (hT_hi[:, p, P:2 * P], w[2]), (hT_lo[:, p, P:2 * P], w[2]))):
                    m = nc.tensor.matmul(ps[:, Y + p, :], l, r, start=(n == 0), stop=(n == 4))
                m.then_inc(y_mm, 1)

            x_in(0, 0, True)
            x_in(1, 1, True)
            up(0, 0, True)
            for i in range(2):
                x_in(i + 2, i)
                turn(i, i, True)
                up(i + 1, 1 - i, i == 0)
                down(i, i, True)
            with pe.Fori(1, TILES // 2 - 1) as j:
                for p in range(2):
                    x_in(2 * j + p + 2, p)
                    turn(2 * j + p, p)
                    up(2 * j + p + 1, 1 - p)
                    down(2 * j + p, p)
            turn(TILES - 2, 0)
            up(TILES - 1, 1)
            down(TILES - 2, 0)
            turn(TILES - 1, 1)
            down(TILES - 1, 1)


def lay_out(inputs):
    g = {k: np.asarray(v) for k, v in inputs.items()}
    rows = lambda v: np.ascontiguousarray(np.broadcast_to(v[None, :], (P, D)))
    cols = lambda v: np.ascontiguousarray(v.reshape(KD, P).T)
    a = {
        "x_in": g["x"], "fside": g["fside_BxS2xS2_0"], "ctx_w": g["ctx_1024"],
        "wq": g["L0_attn_wq"], "bq": cols(g["L0_attn_bq"]), "wk": g["L0_attn_wk"], "bk": cols(g["L0_attn_bk"]),
        "wv": g["L0_attn_wv"], "bv": rows(g["L0_attn_bv"]), "wo": g["L0_attn_wo"], "bo": rows(g["L0_attn_bo"]),
        "wg": np.ascontiguousarray(g["L0_ffn_wg"].T), "w1": g["L0_ffn_w1"], "v1": g["L0_ffn_v1"], "w2": g["L0_ffn_w2"],
    }
    a.update(shape_constants())
    return a


def kernel(**inputs):
    import concourse.bacc as bacc
    from concourse.bass_utils import run_bass_kernel_spmd

    nc = bacc.Bacc("TRN2", target_bir_lowering=False, num_devices=1)
    arrays = lay_out(inputs)
    args = [nc.dram_tensor(name, a.shape, mybir.dt.from_np(a.dtype), kind="ExternalInput").ap() for name, a in arrays.items()]
    args.append(nc.dram_tensor("out", [TOK + P, D], F32, kind="ExternalOutput").ap())
    decoder_kernel(nc, *args)
    r = run_bass_kernel_spmd(nc, [arrays], core_ids=[0])
    return r.results[0]["out"][0:TOK].reshape(B, S, D)
```

```python
from contextlib import ExitStack

import numpy as np
import concourse.bass as bass
from concourse import mybir

F32, F16, BF16, I32 = mybir.dt.float32, mybir.dt.float16, mybir.dt.bfloat16, mybir.dt.int32
ALU, ACT, AX = mybir.AluOpType, mybir.ActivationFunctionType, mybir.AxisListType

P = 128
B, S, D = 4, 512, 512
NT, KD = S // P, D // P
H, HD = 16, 32
HG = P // HD
PAIRS = H // 2
QI = 256
E, TOPK, F = 32, 8, 192
EB = E // B
LN_EPS, Q_EPS, QMAX = 1e-5, 1e-6, 127.0
MAGIC = 1.5 * 2.0 ** 23
SCALE = 1.0 / np.sqrt(np.float32(HD))
KB = 3 * HD + 16
KM = KB + 1
WC = KD * 2 * 2 * F
W2C = 3 * D
TOK = B * S
REGION = TOK
BLOCKS = REGION // P
TILES = TOK * TOPK // P + E
TABLE = E * BLOCKS + TILES
KT = TOPK * NT
POFF = {0: 0, 1: 512, 3: 896, 2: 1024}
PCOLS = 1280


def shape_constants():
    def parts(x, n):
        out = []
        for _ in range(n):
            h = x.astype(np.float16)
            out.append(h)
            x = x - h.astype(np.float64)
        return out

    eye = np.eye(P, dtype=np.float32)
    i = np.arange(P)
    bf = lambda a: (np.ascontiguousarray(a, np.float32).view(np.uint32) >> 16).astype(np.uint16)
    later = np.where(i[None, :] > i[:, None], np.float32(-1e30), np.float32(0))
    start = np.float32(2.0 ** (-8.0 / H))
    slope = np.array([2.0 ** (-8.0 / H) * (2.0 ** (-8.0 / H)) ** h for h in range(H)], np.float32)
    c = slope.astype(np.float64) * np.sqrt(HD)
    pos = np.arange(S)
    k_rows = np.zeros((32, S), np.float16)
    q_rows = np.zeros((32, H, S), np.float16)
    for n, part in enumerate(parts(c, 3)):
        k_rows[n] = pos % P
        q_rows[n] = part[:, None]
    for j in range(NT):
        for n, part in enumerate(parts(c[:, None] * (P * j - pos)[None, :], 3)):
            k_rows[3 + 3 * j + n] = (pos // P == j)
            q_rows[3 + 3 * j + n] = part
    k_rows[16] = 1
    return {
        "c_eye32": eye, "c_eye16": eye.astype(np.float16), "c_eyeb": bf(eye),
        "c_mask_qk": bf(later), "c_mask_kq": bf(later.T),
        "c_k_rows": k_rows, "c_q_rows": q_rows,
        "c_before": bf(i[:, None] < i[None, :]),
        "c_pads": np.stack([TOK + np.arange(TABLE * P, dtype=np.int32) % P, np.zeros(TABLE * P, np.int32)], 1),
        "c_tok": (np.arange(NT)[None, :] * P + i[:, None]).astype(np.float32),
        "c_keep": np.tile((np.arange(NT * E) % E != 0).astype(np.float32), (P, 1)),
        "c_base": np.tile((np.arange(NT * E) % E * REGION).astype(np.float32), (P, 1)),
        "c_rank": np.tile(np.repeat(np.arange(1, TOPK + 1), NT * E).astype(np.float32), (P, 1)),
        "c_pad_pos": (E * REGION + np.arange(KT)[None, :] * P + i[:, None]).astype(np.int32),
        "c_pad_pay": np.tile(np.stack([TOK + i, 0 * i], 1)[:, None, :], (1, KT, 1)).astype(np.int32),
        "c_tile": np.stack([i, i + P], 1).astype(np.float32),
    }


class Signal:

    def __init__(self, sem, per, each=1, start=0):
        self.sem, self.per, self.each, self.start = sem, per, each, start

    def at(self, b, n):
        if isinstance(b, int):
            return self.start + self.each * (b * self.per + n)
        return b * (self.each * self.per) + (self.start + self.each * n)


def decoder_kernel(nc, x_in, fside, ctx_w, wq, bq, wk, bk, wv, bv, wo, bo, wg, w1, v1, w2,
                   eye32_c, eye16_c, eyeb_c, mask_qk_c, mask_kq_c, k_rows_c, q_rows_c,
                   before_c, pads_c, tok_c, keep_c, base_c, rank_c, pad_pos_c, pad_pay_c, tile_c, out):
    with nc.sbuf_tensor("counts", [P, E], F32) as counts:
        split_w = nc.dram_tensor("split_w", [E, P, WC + W2C], F16, kind="Internal").ap()
        x3_rows = nc.dram_tensor("x3_rows", [TOK + P, 2 * D], F16, kind="Internal").ap()
        table = nc.dram_tensor("table", [TABLE * P, 2], I32, kind="Internal").ap()
        dense_part(nc, x_in, fside, ctx_w, wq, bq, wk, bk, wv, bv, wo, bo, wg, w1, v1, w2,
                   eye32_c, eye16_c, eyeb_c, mask_qk_c, mask_kq_c, k_rows_c, q_rows_c,
                   before_c, pads_c, tok_c, keep_c, base_c, rank_c, pad_pos_c, pad_pay_c,
                   counts, split_w, x3_rows, table, out)
        expert_part(nc, eye32_c, eye16_c, tile_c, counts, split_w, x3_rows, table, out)


def dense_part(nc, x_in, fside, ctx_w, wq, bq, wk, bk, wv, bv, wo, bo, wg, w1, v1, w2,
               eye32_c, eye16_c, eyeb_c, mask_qk_c, mask_kq_c, k_rows_c, q_rows_c,
               before_c, pads_c, tok_c, keep_c, base_c, rank_c, pad_pos_c, pad_pay_c,
               counts, split_w, x3_rows, table, out):
    ctx = ExitStack()
    with ctx:
        def sb(name, shape, dt):
            return ctx.enter_context(nc.sbuf_tensor(name, shape, dt))

        started = []

        def sig(name, per=1, each=1, start=0):
            s = Signal(ctx.enter_context(nc.semaphore(name)), per, each, start)
            if start:
                started.append(s)
            return s

        ps = ctx.enter_context(nc.psum_tensor("ps", [P, 8, 512], F32))
        psb = ps[:, :, :].bitcast(BF16)

        eye32, eye16, eyeb = sb("eye32", [P, P], F32), sb("eye16", [P, P], F16), sb("eyeb", [P, P], BF16)
        mask_qk, mask_kq = sb("mask_qk", [P, P], BF16), sb("mask_kq", [P, P], BF16)
        ones32 = sb("ones32", [P, P], F32)
        eps, neg_half, half = sb("eps", [P, 4], F32), sb("neg_half", [P, 4], F32), sb("half", [P, 4], F32)
        w_hi = sb("w_hi", [P, 4, KD, D], F16)
        w_lo = sb("w_lo", [P, 4, KD, D], F16)
        b_qk = sb("b_qk", [P, 2 * KD], F32)
        b_v, b_o = sb("b_v", [P, D], F32), sb("b_o", [P, D], F32)
        x = sb("x", [P, NT, D], F32)
        x1 = sb("x1", [P, NT, D], F32)
        xn = sb("xn", [P, NT, D], F32)
        t_hi, t_lo = sb("t_hi", [P, KD, S], F16), sb("t_lo", [P, KD, S], F16)
        qk_hi, qk_lo = sb("qk_hi", [P, 8, S], F16), sb("qk_lo", [P, 8, S], F16)
        qop, kop = sb("qop", [P, H, S], F16), sb("kop", [P, H, S], F16)
        v_hi = sb("v_hi", [P, NT, H, HD + 1], F16)
        v_lo = sb("v_lo", [P, NT, H, HD], F16)
        mx = sb("mx", [P, NT, H], F32)
        m_row = sb("m_row", [H // 2, 2, S], F16)
        p32, p_hi, p_lo = sb("p32", [P, 2, PCOLS], F32), sb("p_hi", [P, 2, PCOLS], F16), sb("p_lo", [P, 2, PCOLS], F16)
        rden = sb("rden", [P, 2, NT], F32)
        o32 = sb("o32", [P, NT, D], F32)
        stats, mv, ve, rstd = sb("stats", [P, NT, 6], F32), sb("mv", [P, NT, 2], F32), sb("ve", [P, NT], F32), sb("rstd", [P, NT], F32)
        fw = sb("fw", [P, KD, D], F32)
        cw = sb("cw", [P, KD, QI], F32)
        act = sb("act", [P, NT, QI], F32)
        th = p32[:, :, :].rearrange("p a c -> p (a c)")[:, 0:NT * QI].rearrange("p (t c) -> p t c", t=NT)
        amax, sq = sb("amax", [P, 2, KD], F32), sb("sq", [P, 6, KD], F32)
        dg = sb("dg", [P, 2, KD, P], F32)
        rowmax, rscale, rinv = sb("rowmax", [P, 2, 4], F32), sb("rscale", [P, 2, 4], F32), sb("rinv", [P, 2, 4], F32)
        xq = qk_hi[:, 0:4, :].bitcast(BF16)
        wqz = qk_hi[:, 4:8, :].bitcast(BF16)
        xqT = qk_lo[:, 0:4, :].bitcast(BF16)
        wqT = qk_lo[:, 4:8, :].bitcast(BF16)
        wscb = sb("wscb", [P, D], F32)

        s_const = sig("s_const", 1, 16)
        s_wld = [sig(f"s_wld{n}", 1, 16) for n in range(5)]
        s_whi, s_wlo = sig("s_whi"), sig("s_wlo")
        s_one, s_mg = sig("s_one"), sig("s_mg")
        x_ld = sig("x_ld", 1, 16)
        fw_ld, cw_ld = sig("fw_ld", 1, 16), sig("cw_ld", 1, 16)
        ln_st, ln_mv, ln_rs = sig("ln_st", 3), sig("ln_mv", 3), sig("ln_rs", 3)
        pl_ve = sig("pl_ve", 3)
        xn_ok = sig("xn_ok", 12)
        t_mm = sig("t_mm", 12)
        t_hi_ok, t_lo_ok = sig("t_hi_ok", 12), sig("t_lo_ok", 12)
        qk_mm, qk_hi_ok, qk_lo_ok = sig("qk_mm", 8), sig("qk_hi_ok", 8), sig("qk_lo_ok", 8)
        op_ld = sig("op_ld", 24, 16)
        v_mm, v32_ok, v_hi_ok, v_lo_ok = sig("v_mm", 4), sig("v32_ok", 4), sig("v_hi_ok", 4), sig("v_lo_ok", 4)
        s_mm, s_max = sig("s_mm", 3 * PAIRS), sig("s_max", 3 * PAIRS)
        m_mm, m_row_ok, m_ld = sig("m_mm", 2), sig("m_row_ok", 2), sig("m_ld", 2, 16)
        st_mm, e32_ok, ehi_ok, elo_ok = sig("st_mm", H), sig("e32_ok", H), sig("ehi_ok", H), sig("elo_ok", H)
        pv_mm, rec_ok, norm_ok = sig("pv_mm", H), sig("rec_ok", H), sig("norm_ok", H)
        xbo_ok = sig("xbo_ok", 4)
        wo_mm, x1_ok = sig("wo_mm", 4), sig("x1_ok", 4, start=1)
        am_mm, am_ok = sig("am_mm", 12), sig("am_ok", 12)
        qs_link = sig("qs_link", 12)
        qs_rat, qs_pow = sig("qs_rat", 2), sig("qs_pow", 2)
        dg_ok, bc_mm = sig("dg_ok", 4), sig("bc_mm", 4)
        sc_ok, rm_ok, ri_ok = sig("sc_ok", 16), sig("rm_ok", 4), sig("ri_ok", 4)
        q1_ok, q2_ok, q3_ok = sig("q1_ok", 16), sig("q2_ok", 16), sig("q3_ok", 16, start=1)
        qt_mm, qt_ok = sig("qt_mm", 6), sig("qt_ok", 6)
        wsb_ok = sig("wsb_ok", 2)
        l_mm, l_ok = sig("l_mm", 8), sig("l_ok", 8)
        th_ok, a1_ok, a_ok = sig("th_ok", 4), sig("a1_ok", 4), sig("a_ok", 4)
        x2_ok = sig("x2_ok", 4)
        out_st = sig("out_st", 1, 16, start=1)
        wd_ok, wd_mm = sig("wd_ok", 2), sig("wd_mm", 2)
        lg_mm, lg_ok = sig("lg_mm"), sig("lg_ok")
        magic, idle, idle_p = sb("magic", [P, 2], F32), sb("idle", [P, 1], F32), sb("idle_p", [P, 1], F32)
        g_hi, g_lo = sb("g_hi", [P, KD, E], F16), sb("g_lo", [P, KD, E], F16)
        primer = sb("primer", [P, 8], F32)
        before, onesb = sb("before", [P, P], BF16), sb("onesb", [P, P], BF16)
        keep, base, tokf = sb("keep", [P, NT * E], F32), sb("base", [P, NT * E], F32), sb("tokf", [P, NT], F32)
        rank = sb("rank", [P, TOPK, NT * E], F32)
        lg, sm, rep = sb("lg", [P, NT, E], F32), sb("sm", [P, NT, E], F32), sb("rep", [P, NT, E], F32)
        top, r4 = sb("top", [P, NT, TOPK], F32), sb("r4", [P, 4, NT], F32)
        chosen, chosenb = sb("chosen", [P, NT, E], F32), sb("chosenb", [P, NT, E], BF16)
        nth, slot, gate = sb("nth", [P, NT * E], F32), sb("slot", [P, NT, E], F32), sb("gate", [P, NT, E], F32)
        hit = o32[:, 0:2, :].rearrange("p a (k c) -> p (a k) c", c=NT * E)
        hit2 = o32[:, 2:4, :].rearrange("p a (k c) -> p (a k) c", c=NT * E)
        posf, pos = sb("posf", [P, KT], F32), sb("pos", [P, KT], I32)
        gatek = sb("gatek", [P, KT], F32)
        pay = sb("pay", [P, KT, 2], I32)
        x3 = qk_hi[:, :, :].rearrange("p (t a) d -> p t (a d)", a=2)
        zeros = sb("zeros", [P, D], F32)
        wst = sb("wst", [P, WC + 4 * D], F16)
        wst13 = wst[:, 0:WC].rearrange("p (k s f) -> p k s f", k=KD, s=2)
        wst2 = wst[:, WC:WC + 4 * D].rearrange("p (a s d) -> p a s d", a=2, s=2)
        w13f = fw[:, 0:3, :].rearrange("p a c -> p (a c)").rearrange("p (k f) -> p k f", k=KD)
        w2f = act[:, :, :].rearrange("p a c -> p (a c)").rearrange("p (a d) -> p a d", a=2)
        ew13_ld, ew2_ld, ew_st = sig("ew13_ld", 2 * EB, 16), sig("ew2_ld", 3 * EB, 16), sig("ew_st", 3 * EB, 16, start=1)
        ew_hi, ew_lo13, ew_lo2 = sig("ew_hi", 2 * EB), sig("ew_lo13", EB, start=1), sig("ew_lo2", EB, start=1)
        r_link, r_rep, r_ex, r_exp = sig("r_link", 15), sig("r_rep"), sig("r_ex"), sig("r_exp")
        r_mask, rk_mm, r_pos, r_tok = sig("r_mask"), sig("rk_mm"), sig("r_pos", start=1), sig("r_tok")
        x3_hi, x3_lo, x3_st = sig("x3_hi", 4), sig("x3_lo"), sig("x3_st", 1, 16, start=1)
        tb_st = sig("tb_st", KT, 16)
        init_st = sig("init_st", 1, 16)

        N_CONST = 17 + H
        bank = [ps[:, i, :] for i in range(8)]
        x_dram = x_in.rearrange("b (t p) d -> b p t d", p=P)
        o_dram = out[0:B * S, :].rearrange("(b t p) d -> b p t d", p=P, t=NT)
        x3_dram = x3_rows[0:TOK, :].rearrange("(b t p) d -> b p t d", p=P, t=NT)
        fw_dram = fside.rearrange("b (t p) d -> b p t d", p=P)
        cw_dram = ctx_w.rearrange("b (t p) d -> b p t d", p=P)
        QKV = {"q": 0, "k": 1, "v": 2, "o": 3}

        block = ctx.enter_context(nc.Block())

        @block.sync
        def _(sp):
            for dst, src in ((keep, keep_c), (base, base_c), (tokf, tok_c), (before, before_c), (pos, pad_pos_c), (eye32, eye32_c), (eye16, eye16_c), (eyeb, eyeb_c), (mask_qk, mask_qk_c),
                             (mask_kq, mask_kq_c), (b_v, bv), (b_o, bo), (b_qk[:, 0:KD], bq), (b_qk[:, KD:2 * KD], bk)):
                sp.dma_start(dst[:, :].bitcast(src.dtype), src).then_inc(s_const.sem, 16)
            sp.dma_start(rank[:, :, :], rank_c.rearrange("p (k c) -> p k c", k=TOPK)).then_inc(s_const.sem, 16)
            sp.dma_start(pay[:, :, :], pad_pay_c).then_inc(s_const.sem, 16)
            sp.dma_start(qop[3 * HD:4 * HD, :, :], q_rows_c).then_inc(s_const.sem, 16)
            for h in range(H):
                sp.dma_start(kop[3 * HD:4 * HD, h, :], k_rows_c).then_inc(s_const.sem, 16)
            for n, w in enumerate((wq, wk, wv, wo)):
                if n >= 2:
                    sp.wait_ge(s_wlo.sem, n - 1)
                sp.dma_start((x, x1)[n % 2][:, :, :], w.rearrange("(k p) n -> p k n", p=P)).then_inc(s_wld[n].sem, 16)
            sp.dma_start(fw[:, :, 0:E], wg.rearrange("(k p) n -> p k n", p=P)).then_inc(s_wld[4].sem, 16)
            sp.dma_start(table, pads_c).then_inc(init_st.sem, 16)
            sp.wait_ge(s_one.sem, 7)
            sp.dma_start(out[TOK:TOK + P, :], zeros[:, :]).then_inc(init_st.sem, 16)
            sp.dma_start(x3_rows[TOK:TOK + P, :], zeros[:, :].bitcast(F16)).then_inc(init_st.sem, 16)
            sp.wait_ge(s_wlo.sem, 5)
            with sp.Fori(0, B) as b:
                sp.wait_ge(x1_ok.sem, x1_ok.at(b, 0))
                sp.dma_start(x[:, :, :], x_dram[b]).then_inc(x_ld.sem, 16)
                sp.wait_ge(q3_ok.sem, q3_ok.at(b, 0))
                sp.dma_start(cw[:, :, :], cw_dram[b]).then_inc(cw_ld.sem, 16)
                for which, dst, (hi_rows, lo_row) in ((0, qop, ((0, 32), 64)), (1, kop, ((0, 64), 32))):
                    sp.wait_ge(qk_hi_ok.sem, qk_hi_ok.at(b, 4 * which + 4))
                    for r in hi_rows:
                        for i in range(HG):
                            sp.dma_start(dst[r:r + HD, i::HG, :], qk_hi[HD * i:HD * i + HD, 4 * which:4 * which + 4, :]).then_inc(op_ld.sem, 16)
                    sp.wait_ge(qk_lo_ok.sem, qk_lo_ok.at(b, 4 * which + 4))
                    for i in range(HG):
                        sp.dma_start(dst[lo_row:lo_row + HD, i::HG, :], qk_lo[HD * i:HD * i + HD, 4 * which:4 * which + 4, :]).then_inc(op_ld.sem, 16)
                with sp.Fori(0, EB) as n:
                    e = b * EB + n
                    sp.wait_ge(ew_lo13.sem, ew_lo13.at(b, 0) + n)
                    sp.dma_start(w13f[:, :, 0:F], w1.rearrange("e (k p) f -> e p k f", p=P)[e]).then_inc(ew13_ld.sem, 16)
                    sp.dma_start(w13f[:, :, F:2 * F], v1.rearrange("e (k p) f -> e p k f", p=P)[e]).then_inc(ew13_ld.sem, 16)
                    sp.wait_ge(ew_lo2.sem, ew_lo2.at(b, 0) + n)
                    sp.dma_start(w2f[:, 0, :], w2[:, 0:P, :][e]).then_inc(ew2_ld.sem, 16)
                    for side in range(2):
                        sp.dma_start(w2f[64 * side:64 * side + 64, 1, :], w2[:, P:F, :][e]).then_inc(ew2_ld.sem, 16)
                    sp.wait_ge(ew_lo2.sem, ew_lo2.at(b, 1) + n)
                    sp.dma_start(split_w[e][:, 0:WC + 2 * D], wst[:, 0:WC + 2 * D]).then_inc(ew_st.sem, 16)
                    sp.dma_start(split_w[e][0:64, WC + 2 * D:WC + W2C], wst2[0:64, 1, 0, :]).then_inc(ew_st.sem, 16)
                    sp.dma_start(split_w[e][64:P, WC + 2 * D:WC + W2C], wst2[64:P, 1, 1, :]).then_inc(ew_st.sem, 16)
                sp.dma_start(fw[:, :, :], fw_dram[b]).then_inc(fw_ld.sem, 16)
            sp.wait_ge(ew_st.sem, ew_st.at(B, 0))
            sp.wait_ge(out_st.sem, out_st.at(B, 0))
            sp.wait_ge(x3_st.sem, x3_st.at(B, 0))
            sp.wait_ge(init_st.sem, 16 * 3)
            sp.wait_ge(tb_st.sem, 16 * KT * (B + 1))

        @block.gpsimd
        def _(pool):
            nc.gpsimd.memset(ones32[:, :], 1.0).then_inc(s_one.sem, 1)
            nc.gpsimd.memset(neg_half[:, :], -0.5).then_inc(s_one.sem, 1)
            nc.gpsimd.memset(half[:, :], 0.5).then_inc(s_one.sem, 1)
            nc.gpsimd.memset(eps[:, :], LN_EPS).then_inc(s_one.sem, 1)
            nc.gpsimd.memset(v_hi[:, :, :, :], 1.0).then_inc(s_one.sem, 1)
            nc.gpsimd.memset(onesb[:, :], 1.0).then_inc(s_one.sem, 1)
            nc.gpsimd.memset(zeros[:, :], 0.0).then_inc(s_one.sem, 1)
            for n, s in enumerate(started):
                nc.gpsimd.memset(primer[:, n:n + 1], 0.0).then_inc(s.sem, 1)
            pool.wait_ge(s_one.sem, 7)
            pool.wait_ge(s_const.sem, N_CONST * 16)

            def ln_scale(b, n):
                pool.wait_ge(ln_mv.sem, ln_mv.at(b, n + 1))
                nc.gpsimd.tensor_tensor(ve[:, :], mv[:, :, 1], eps[:, :], ALU.add).then_inc(pl_ve.sem, 1)
                pool.wait_ge(pl_ve.sem, pl_ve.at(b, n + 1))
                nc.gpsimd.tensor_tensor(rstd[:, :], ve[:, :], neg_half[:, :], ALU.pow).then_inc(ln_rs.sem, 1)

            def smooth(b, lin):
                n = (KD, 2)[lin]
                pool.wait_ge(qs_rat.sem, qs_rat.at(b, lin + 1))
                nc.gpsimd.tensor_tensor(sq[:, 3, 0:n], sq[:, 2, 0:n], half[:, 0:n], ALU.pow).then_inc(qs_pow.sem, 1)

            def none(a, c):
                return zeros[:, 0:1].unsqueeze(2).to_broadcast([P, a, c])

            def scatter_choices(b):
                pool.wait_ge(r_pos.sem, r_pos.at(b, 0))
                nc.gpsimd.tensor_tensor(idle_p[:, :], eps[:, 0:1], eps[:, 0:1], ALU.add)
                for c in range(KT):
                    nc.gpsimd.indirect_dma_start(table, bass.IndirectOffsetOnAxis(ap=pos[:, c:c + 1], axis=0),
                                                 pay[:, c, :], None).then_inc(tb_st.sem, 16)

            pool.wait_ge(init_st.sem, 48)
            with pool.Fori(0, B) as b:
                ln_scale(b, 0)
                pool.wait_ge(xn_ok.sem, xn_ok.at(b, 4))
                for t in range(NT):
                    nc.gpsimd.tensor_tensor(x[:, t, :], x[:, t, :], b_o[:, :], ALU.add).then_inc(xbo_ok.sem, 1)
                scatter_choices(b)

                with pool.Fori(0, EB) as n:
                    pool.wait_ge(ew13_ld.sem, ew13_ld.at(b, 2) + 32 * n)
                    pool.wait_ge(ew_st.sem, ew_st.at(b, 0) + 48 * n)
                    nc.gpsimd.tensor_tensor(wst13[:, :, 0, :], w13f[:, :, :], none(KD, 2 * F), ALU.add).then_inc(ew_hi.sem, 1)
                    pool.wait_ge(ew_hi.sem, ew_hi.at(b, 1) + 2 * n)
                    nc.gpsimd.tensor_tensor(wst13[:, :, 1, :], w13f[:, :, :], wst13[:, :, 0, :], ALU.subtract).then_inc(ew_lo13.sem, 1)
                    pool.wait_ge(ew2_ld.sem, ew2_ld.at(b, 3) + 48 * n)
                    nc.gpsimd.tensor_tensor(wst2[:, :, 0, :], w2f[:, :, :], none(2, D), ALU.add).then_inc(ew_hi.sem, 1)
                    pool.wait_ge(ew_hi.sem, ew_hi.at(b, 2) + 2 * n)
                    nc.gpsimd.tensor_tensor(wst2[:, :, 1, :], w2f[:, :, :], wst2[:, :, 0, :], ALU.subtract).then_inc(ew_lo2.sem, 1)
                ln_scale(b, 1)
                smooth(b, 0)
                smooth(b, 1)
                ln_scale(b, 2)
                pool.wait_ge(x3_hi.sem, x3_hi.at(b, 4))
                nc.gpsimd.tensor_tensor(x3[:, :, D:2 * D], xn[:, :, :], x3[:, :, 0:D], ALU.subtract).then_inc(x3_lo.sem, 1)
            scatter_choices(B)

        @block.scalar
        def _(act_e):
            act_e.wait_ge(s_mg.sem, 2)
            for n in range(4):
                act_e.wait_ge(s_wld[n].sem, 16)
                nc.scalar.copy(w_hi[:, n, :, :], (x, x1)[n % 2][:, :, :]).then_inc(s_whi.sem, 1)
            act_e.wait_ge(s_wld[4].sem, 16)
            nc.scalar.copy(g_hi[:, :, :], fw[:, :, 0:E]).then_inc(s_whi.sem, 1)

            def halves_hi(b, first):
                for k in range(KD):
                    act_e.wait_ge(t_mm.sem, t_mm.at(b, first + k + 1))
                    nc.scalar.copy(t_hi[:, k, :], bank[(0, 0, 4)[first // 4] + k]).then_inc(t_hi_ok.sem, 1)

            def quantise(b, lin):
                w = (D, QI)[lin]
                for side, src, dst in ((1, (fw, cw)[lin], wqz), (0, (xn, act)[lin], xq)):
                    n = 8 * lin + 4 * (1 - side)
                    act_e.wait_ge(ri_ok.sem, ri_ok.at(b, 2 * lin + 2 - side))
                    for t in range(4):
                        nc.scalar.activation(src[:, t, 0:w], src[:, t, 0:w], ACT.Identity, bias=magic[:, 0:1],
                                             scale=rinv[:, side, t:t + 1]).then_inc(q1_ok.sem, 1)
                    for t in range(4):
                        act_e.wait_ge(q2_ok.sem, q2_ok.at(b, n + t + 1))
                        nc.scalar.activation(dst[:, t, 0:w], src[:, t, 0:w], ACT.Identity, bias=magic[:, 1:2],
                                             scale=1.0).then_inc(q3_ok.sem, 1)

            def quantT_out(b, lin, side):
                if lin == 0:
                    for half_ in range(2):
                        act_e.wait_ge(qt_mm.sem, qt_mm.at(b, 2 * (1 - side) + half_ + 1))
                        nc.scalar.copy((xqT, wqT)[side][:, 2 * half_:2 * half_ + 2, :],
                                       psb[:, (2, 4)[side] + half_, :].rearrange("p (k c) -> p k c", k=2)).then_inc(qt_ok.sem, 1)
                else:
                    act_e.wait_ge(qt_mm.sem, qt_mm.at(b, 4 + (1 - side) + 1))
                    nc.scalar.copy((xqT, wqT)[side][:, 0:2, :],
                                   psb[:, (6, 7)[side], :].rearrange("p (k c) -> p k c", k=2)).then_inc(qt_ok.sem, 1)

            with act_e.Fori(0, B) as b:
                halves_hi(b, 0)
                act_e.wait_ge(x3_st.sem, x3_st.at(b, 0))
                for i in range(8):
                    act_e.wait_ge(qk_mm.sem, qk_mm.at(b, i + 1))
                    nc.scalar.activation(qk_hi[:, i, :], bank[(4 + i) % 8], ACT.Identity, bias=b_qk[:, i:i + 1], scale=1.0).then_inc(qk_hi_ok.sem, 1)
                for t in range(NT):
                    act_e.wait_ge(v32_ok.sem, v32_ok.at(b, t + 1))
                    nc.scalar.copy(v_hi[:, t, :, 0:HD], o32[:, t, :].rearrange("p (h d) -> p h d", h=H)).then_inc(v_hi_ok.sem, 1)
                for g in range(2):
                    act_e.wait_ge(m_mm.sem, m_mm.at(b, g + 1))
                    nc.scalar.mul(m_row[:, g, :], ps[0:H // 2, 6, :], -1.0).then_inc(m_row_ok.sem, 1)
                    act_e.wait_ge(m_row_ok.sem, m_row_ok.at(b, g + 1))
                    act_e.dma_start(qop[KB:KB + 1, 8 * g:8 * g + 8, :], m_row[:, g, :]).then_inc(m_ld.sem, 16)
                def exponentials(b, hp, first):
                    for i in range(2):
                        if not first:
                            act_e.wait_ge(pv_mm.sem, pv_mm.at(b, i - 1) + 2 * hp)
                            act_e.wait_ge(elo_ok.sem, elo_ok.at(b, i - 1) + 2 * hp)
                        act_e.wait_ge(st_mm.sem, st_mm.at(b, i + 1) + 2 * hp)
                        src = ps[:, 3 * i:3 * i + 3, :].rearrange("p a c -> p (a c)")[:, 0:PCOLS]
                        nc.scalar.activation(p32[:, i, :], src, ACT.Exp, scale=float(SCALE)).then_inc(e32_ok.sem, 1)
                        nc.scalar.activation(p_hi[:, i, :], src, ACT.Exp, scale=float(SCALE)).then_inc(ehi_ok.sem, 1)
                exponentials(b, 0, True)
                with act_e.Fori(1, PAIRS) as hp:
                    exponentials(b, hp, False)
                halves_hi(b, 4)
                quantise(b, 0)
                quantT_out(b, 0, 1)
                quantT_out(b, 0, 0)
                for t in range(NT):
                    act_e.wait_ge(l_ok.sem, l_ok.at(b, t + 1))
                    nc.scalar.activation(th[:, t, :], o32[:, t, 0:QI], ACT.Tanh, scale=0.5).then_inc(th_ok.sem, 1)
                quantise(b, 1)
                quantT_out(b, 1, 1)
                quantT_out(b, 1, 0)
                act_e.wait_ge(x2_ok.sem, x2_ok.at(b, 4))
                act_e.dma_start(o_dram[b], x1[:, :, :]).then_inc(out_st.sem, 16)
                for t in range(NT):
                    act_e.wait_ge(xn_ok.sem, xn_ok.at(b, 8 + t + 1))
                    nc.scalar.copy(x3[:, t, 0:D], xn[:, t, :]).then_inc(x3_hi.sem, 1)
                halves_hi(b, 8)
                act_e.wait_ge(r_ex.sem, r_ex.at(b, 1))
                nc.scalar.activation(sm[:, :, :], lg[:, :, :], ACT.Exp).then_inc(r_exp.sem, 1)
                act_e.wait_ge(x3_lo.sem, x3_lo.at(b, 1))
                act_e.dma_start(x3_dram[b], x3[:, :, :]).then_inc(x3_st.sem, 16)

        @block.vector
        def _(dve):
            nc.vector.memset(magic[:, 0:1], MAGIC).then_inc(s_mg.sem, 1)
            nc.vector.memset(magic[:, 1:2], -MAGIC).then_inc(s_mg.sem, 1)
            dve.wait_ge(s_one.sem, 7)
            for n in range(4):
                dve.wait_ge(s_whi.sem, n + 1)
                nc.vector.tensor_tensor(w_lo[:, n, :, :], (x, x1)[n % 2][:, :, :], w_hi[:, n, :, :], ALU.subtract).then_inc(s_wlo.sem, 1)
            dve.wait_ge(s_whi.sem, 5)
            nc.vector.tensor_tensor(g_lo[:, :, :], fw[:, :, 0:E], g_hi[:, :, :], ALU.subtract).then_inc(s_wlo.sem, 1)

            def layer_norm(b, n, src):
                for t in range(NT):
                    i = nc.vector.bn_stats(stats[:, t, :], src[:, t, :])
                i.then_inc(ln_st.sem, 1)
                dve.wait_ge(ln_st.sem, ln_st.at(b, n + 1))
                nc.vector.memset(idle[:, :], 0.0)
                for t in range(NT):
                    i = nc.vector.bn_aggr(mv[:, t, :], stats[:, t, :])
                i.then_inc(ln_mv.sem, 1)
                dve.wait_ge(ln_rs.sem, ln_rs.at(b, n + 1))
                for t in range(NT):
                    nc.vector.tensor_scalar(xn[:, t, :], src[:, t, :], mv[:, t, 0:1], rstd[:, t:t + 1],
                                            ALU.subtract, ALU.mult).then_inc(xn_ok.sem, 1)

            def halves_lo(b, first):
                for k in range(KD):
                    dve.wait_ge(t_hi_ok.sem, t_hi_ok.at(b, first + k + 1))
                    nc.vector.tensor_tensor(t_lo[:, k, :], bank[(0, 0, 4)[first // 4] + k], t_hi[:, k, :],
                                            ALU.subtract).then_inc(t_lo_ok.sem, 1)

            def scales(b, lin):
                n = (KD, 2)[lin]
                step = [6 * lin]

                def link(i):
                    step[0] += 1
                    i.then_inc(qs_link.sem, 1)
                    dve.wait_ge(qs_link.sem, qs_link.at(b, step[0]))

                for side in range(2):
                    for k in range(n):
                        m = 8 * lin + n * side + k
                        dve.wait_ge(am_mm.sem, am_mm.at(b, m + 1))
                        nc.vector.tensor_reduce(amax[:, side, k:k + 1], bank[(4 * side, 4 + 2 * side)[lin] + k], AX.X, ALU.max,
                                                apply_absolute_value=True).then_inc(am_ok.sem, 1)
                dve.wait_ge(am_ok.sem, am_ok.at(b, 8 + 4 * lin))
                link(nc.vector.tensor_scalar(sq[:, 0:2, 0:n], amax[:, :, 0:n], Q_EPS, None, ALU.max))
                link(nc.vector.reciprocal(sq[:, 1, 0:n], sq[:, 1, 0:n]))
                nc.vector.tensor_tensor(sq[:, 2, 0:n], sq[:, 0, 0:n], sq[:, 1, 0:n], ALU.mult).then_inc(qs_rat.sem, 1)
                dve.wait_ge(qs_pow.sem, qs_pow.at(b, lin + 1))
                link(nc.vector.tensor_scalar(sq[:, 4, 0:n], sq[:, 3, 0:n], Q_EPS, None, ALU.max))
                link(nc.vector.reciprocal(sq[:, 5, 0:n], sq[:, 4, 0:n]))
                for side in (1, 0):
                    for k in range(n):
                        i = nc.vector.tensor_scalar(dg[:, side, k, :], eye32[:, :], sq[:, (5, 4)[side], k:k + 1], None, ALU.mult)
                    i.then_inc(dg_ok.sem, 1)

            def scaled_rows(b, lin, side):
                w = (D, QI)[lin]
                src = ((xn, act), (fw, cw))[side][lin]
                m = 2 * lin + (1 - side)
                dve.wait_ge(bc_mm.sem, bc_mm.at(b, m + 1))
                if side == 1:
                    ld = (fw_ld, cw_ld)[lin]
                    dve.wait_ge(ld.sem, ld.at(b, 1))
                for t in range(4):
                    nc.vector.tensor_tensor(src[:, t, 0:w], src[:, t, 0:w], bank[(0, 4)[lin] + side][:, 0:w], ALU.mult).then_inc(sc_ok.sem, 1)
                for t in range(4):
                    dve.wait_ge(sc_ok.sem, sc_ok.at(b, 4 * m + t + 1))
                    i = nc.vector.tensor_reduce(rowmax[:, side, t:t + 1], src[:, t, 0:w], AX.X, ALU.max, apply_absolute_value=True)
                i.then_inc(rm_ok.sem, 1)
                dve.wait_ge(rm_ok.sem, rm_ok.at(b, m + 1))
                i = nc.vector.tensor_scalar(rscale[:, side, :], rowmax[:, side, :], Q_EPS, 1.0 / QMAX, ALU.max, ALU.mult)
                i.then_inc(qs_link.sem, 1)
                dve.wait_ge(qs_link.sem, qs_link.at(b, 6 * lin + 4 + (1 - side) + 1))
                nc.vector.reciprocal(rinv[:, side, :], rscale[:, side, :]).then_inc(ri_ok.sem, 1)

            def clip(b, lin, side):
                w = (D, QI)[lin]
                src = ((xn, act), (fw, cw))[side][lin]
                for t in range(4):
                    dve.wait_ge(q1_ok.sem, q1_ok.at(b, 8 * lin + 4 * (1 - side) + t + 1))
                    nc.vector.tensor_scalar(src[:, t, 0:w], src[:, t, 0:w], MAGIC - QMAX, MAGIC + QMAX, ALU.max, ALU.min).then_inc(q2_ok.sem, 1)

            def weight_steps(b, lin):
                for t in range(4):
                    i = nc.vector.tensor_scalar(dg[:, 1, t, :], eye32[:, :], rscale[:, 1, t:t + 1], None, ALU.mult)
                i.then_inc(wd_ok.sem, 1)

            def weight_steps_out(b, lin):
                dve.wait_ge(wd_mm.sem, wd_mm.at(b, lin + 1))
                nc.vector.tensor_copy(wscb[:, :], bank[(6, 4)[lin]]).then_inc(wsb_ok.sem, 1)
                dve.wait_ge(wsb_ok.sem, wsb_ok.at(b, lin + 1))

            def route(b):
                step = [0]

                def link(i):
                    step[0] += 1
                    i.then_inc(r_link.sem, 1)
                    dve.wait_ge(r_link.sem, r_link.at(b, step[0]))

                spread = lambda a: a.unsqueeze(2).to_broadcast([P, NT, E])
                flat = lambda a: a[:, :, :].rearrange("p t e -> p (t e)")
                raw = bank[0][:, 0:NT * E].rearrange("p (t e) -> p t e", t=NT)
                link(nc.vector.tensor_reduce(r4[:, 0, :], raw, AX.X, ALU.max))
                nc.vector.tensor_tensor(lg[:, :, :], raw, spread(r4[:, 0, :]), ALU.subtract).then_inc(r_ex.sem, 1)
                dve.wait_ge(r_exp.sem, r_exp.at(b, 1))
                link(nc.vector.tensor_reduce(r4[:, 1, :], sm[:, :, :], AX.X, ALU.add))
                link(nc.vector.reciprocal(r4[:, 1, :], r4[:, 1, :]))
                nc.vector.tensor_tensor(sm[:, :, :], sm[:, :, :], spread(r4[:, 1, :]), ALU.mult).then_inc(r_rep.sem, 1)
                dve.wait_ge(r_rep.sem, r_rep.at(b, 1))
                nc.vector.memset(idle[:, :], 0.0)
                for t in range(NT):
                    i = nc.vector.max(out=top[:, t, :], in_=sm[:, t, :])
                i.then_inc(r_link.sem, 1)
                step[0] += 1
                dve.wait_ge(r_link.sem, r_link.at(b, step[0]))
                nc.vector.memset(idle[:, :], 0.0)
                for t in range(NT):
                    i = nc.vector.match_replace(out=rep[:, t, :], in_to_replace=top[:, t, :], in_values=sm[:, t, :], imm_value=-1.0)
                link(i)
                nc.vector.tensor_scalar(chosenb[:, :, :], rep[:, :, :], 0.0, None, ALU.is_lt).then_inc(r_mask.sem, 1)
                link(nc.vector.tensor_scalar(chosen[:, :, :], rep[:, :, :], 0.0, None, ALU.is_lt))
                nc.vector.tensor_tensor_scan(nth[:, :], keep[:, :], flat(chosen), 0.0, ALU.mult, ALU.add)
                link(nc.vector.tensor_tensor(gate[:, :, :], sm[:, :, :], chosen[:, :, :], ALU.mult))
                nc.vector.tensor_tensor(nth[:, :], nth[:, :], flat(chosen), ALU.mult)
                link(nc.vector.tensor_reduce(r4[:, 2, :], gate[:, :, :], AX.X, ALU.add))
                link(nc.vector.reciprocal(r4[:, 2, :], r4[:, 2, :]))
                nc.vector.tensor_tensor(gate[:, :, :], gate[:, :, :], spread(r4[:, 2, :]), ALU.mult)
                dve.wait_ge(rk_mm.sem, rk_mm.at(b, 1))
                nc.vector.tensor_tensor(flat(slot), bank[0][:, 128:128 + NT * E], base[:, :], ALU.add).then_inc(r_link.sem, 1)
                step[0] += 1
                link(nc.vector.tensor_tensor(hit[:, :, :], nth[:, :].unsqueeze(1).to_broadcast([P, TOPK, NT * E]), rank[:, :, :], ALU.is_equal))
                link(nc.vector.tensor_tensor(slot[:, :, :], slot[:, :, :], counts[:, :].unsqueeze(1).to_broadcast([P, NT, E]), ALU.add))
                nc.vector.tensor_tensor(counts[:, :], counts[:, :], bank[1][:, 0:E], ALU.add)
                link(nc.vector.tensor_tensor(hit2[:, :, :], hit[:, :, :], flat(slot).unsqueeze(1).to_broadcast([P, TOPK, NT * E]), ALU.mult))
                nc.vector.tensor_reduce(posf[:, :], hit2[:, :, :].rearrange("p k (t e) -> p (k t) e", e=E), AX.X, ALU.add)
                link(nc.vector.tensor_tensor(hit[:, :, :], hit[:, :, :], flat(gate).unsqueeze(1).to_broadcast([P, TOPK, NT * E]), ALU.mult))
                link(nc.vector.tensor_reduce(gatek[:, :], hit[:, :, :].rearrange("p k (t e) -> p (k t) e", e=E), AX.X, ALU.add))
                dve.wait_ge(tb_st.sem, tb_st.at(b, KT))
                nc.vector.tensor_copy(pos[:, :], posf[:, :])
                nc.vector.tensor_copy(pay[:, :, 1].bitcast(F32), gatek[:, :])
                for k in range(TOPK):
                    i = nc.vector.tensor_copy(pay[:, k * NT:(k + 1) * NT, 0], tokf[:, :])
                i.then_inc(r_pos.sem, 1)
                dve.wait_ge(r_pos.sem, r_pos.at(b, 1))
                nc.vector.tensor_scalar(tokf[:, :], tokf[:, :], float(S), None, ALU.add).then_inc(r_tok.sem, 1)

            dve.wait_ge(s_const.sem, N_CONST * 16)
            nc.vector.memset(counts[:, :], 0.0).then_inc(s_mg.sem, 1)
            with dve.Fori(0, B) as b:
                dve.wait_ge(x_ld.sem, x_ld.at(b, 1))
                layer_norm(b, 0, x)
                halves_lo(b, 0)
                for i in range(8):
                    dve.wait_ge(qk_hi_ok.sem, qk_hi_ok.at(b, i + 1))
                    nc.vector.scalar_tensor_tensor(out=qk_lo[:, i, :], in0=bank[(4 + i) % 8], scalar=b_qk[:, i:i + 1],
                                                   in1=qk_hi[:, i, :], op0=ALU.add, op1=ALU.subtract).then_inc(qk_lo_ok.sem, 1)
                for t in range(NT):
                    dve.wait_ge(v_mm.sem, v_mm.at(b, t + 1))
                    nc.vector.tensor_tensor(o32[:, t, :], bank[4 + t], b_v[:, :], ALU.add).then_inc(v32_ok.sem, 1)
                for t in range(NT):
                    dve.wait_ge(v_hi_ok.sem, v_hi_ok.at(b, t + 1))
                    nc.vector.tensor_tensor(v_lo[:, t, :, :], o32[:, t, :].rearrange("p (h d) -> p h d", h=H),
                                            v_hi[:, t, :, 0:HD], ALU.subtract).then_inc(v_lo_ok.sem, 1)
                with dve.Fori(0, PAIRS) as hp:
                    for u, cuts in enumerate((((3, 0, 512),), ((2, 0, 384), (0, 384, 512)), ((1, 0, 256),))):
                        dve.wait_ge(s_mm.sem, s_mm.at(b, u + 1) + 3 * hp)
                        for t, c0, c1 in cuts:
                            i = nc.vector.tensor_reduce(mx[:, t, bass.ts(hp, 2)], ps[:, 2 * u:2 * u + 2, c0:c1], AX.X, ALU.max)
                        i.then_inc(s_max.sem, 1)
                def remainder(b, h, i, first=False):
                    if not first:
                        dve.wait_ge(pv_mm.sem, pv_mm.at(b, -1) + h)
                    dve.wait_ge(ehi_ok.sem, ehi_ok.at(b, 1) + h)
                    nc.vector.tensor_tensor(p_lo[:, i, :], p32[:, i, :], p_hi[:, i, :], ALU.subtract).then_inc(elo_ok.sem, 1)

                def normalised(b, hp, i):
                    dve.wait_ge(pv_mm.sem, pv_mm.at(b, i + 1) + 2 * hp)
                    o = bank[6 + i][:, 0:NT * (HD + 1)].rearrange("p (t c) -> p t c", t=NT)
                    nc.vector.reciprocal(rden[:, i, :], o[:, :, HD]).then_inc(rec_ok.sem, 1)
                    dve.wait_ge(rec_ok.sem, rec_ok.at(b, i + 1) + 2 * hp)
                    dst = o32[:, :, :].rearrange("p t (g i d) -> p t g i d", i=2, d=HD)[:, :, bass.ds(hp, 1), i, :].rearrange("p t a d -> p t (a d)")
                    nc.vector.tensor_tensor(dst, o[:, :, 0:HD],
                                            rden[:, i, :].unsqueeze(2).to_broadcast([P, NT, HD]), ALU.mult).then_inc(norm_ok.sem, 1)

                remainder(b, 0, 0, True)
                remainder(b, 1, 1, True)
                with dve.Fori(0, PAIRS - 1) as hp:
                    normalised(b, hp, 0)
                    remainder(b, 2 * hp + 2, 0)
                    normalised(b, hp, 1)
                    remainder(b, 2 * hp + 3, 1)
                normalised(b, PAIRS - 1, 0)
                normalised(b, PAIRS - 1, 1)
                halves_lo(b, 4)
                dve.wait_ge(out_st.sem, out_st.at(b, 0))
                for t in range(NT):
                    dve.wait_ge(wo_mm.sem, wo_mm.at(b, t + 1))
                    if t == 0:
                        dve.wait_ge(xbo_ok.sem, xbo_ok.at(b, 4))
                    nc.vector.tensor_tensor(x1[:, t, :], bank[4 + t], x[:, t, :], ALU.add).then_inc(x1_ok.sem, 1)
                dve.wait_ge(x1_ok.sem, x1_ok.at(b, 4))
                layer_norm(b, 1, x1)
                for lin in range(2):
                    scales(b, lin)
                    scaled_rows(b, lin, 1)
                    scaled_rows(b, lin, 0)
                    clip(b, lin, 1)
                    weight_steps(b, lin)
                    clip(b, lin, 0)
                    weight_steps_out(b, lin)
                    if lin == 0:
                        for t in range(NT):
                            dve.wait_ge(l_mm.sem, l_mm.at(b, t + 1))
                            nc.vector.scalar_tensor_tensor(out=o32[:, t, :], in0=bank[t], scalar=rscale[:, 0, t:t + 1],
                                                           in1=wscb[:, :], op0=ALU.mult, op1=ALU.mult).then_inc(l_ok.sem, 1)
                        for t in range(NT):
                            dve.wait_ge(th_ok.sem, th_ok.at(b, t + 1))
                            nc.vector.scalar_tensor_tensor(out=act[:, t, :], in0=th[:, t, :], scalar=1.0, in1=o32[:, t, 0:QI],
                                                           op0=ALU.add, op1=ALU.mult).then_inc(a1_ok.sem, 1)
                        for t in range(NT):
                            dve.wait_ge(a1_ok.sem, a1_ok.at(b, t + 1))
                            nc.vector.scalar_tensor_tensor(out=act[:, t, :], in0=act[:, t, :], scalar=0.5, in1=o32[:, t, QI:2 * QI],
                                                           op0=ALU.mult, op1=ALU.mult).then_inc(a_ok.sem, 1)
                    else:
                        for t in range(NT):
                            dve.wait_ge(l_mm.sem, l_mm.at(b, 4 + t + 1))
                            nc.vector.scalar_tensor_tensor(out=o32[:, t, :], in0=bank[t], scalar=rscale[:, 0, t:t + 1],
                                                           in1=wscb[:, :], op0=ALU.mult, op1=ALU.mult).then_inc(l_ok.sem, 1)
                        for t in range(NT):
                            dve.wait_ge(l_ok.sem, l_ok.at(b, 4 + t + 1))
                            nc.vector.tensor_tensor(x1[:, t, :], o32[:, t, :], x1[:, t, :], ALU.add).then_inc(x2_ok.sem, 1)
                dve.wait_ge(x2_ok.sem, x2_ok.at(b, 4))
                layer_norm(b, 2, x1)
                halves_lo(b, 8)
                dve.wait_ge(lg_mm.sem, lg_mm.at(b, 1))
                route(b)

        @block.tensor
        def _(pe):
            pe.wait_ge(s_one.sem, 7)
            pe.wait_ge(s_const.sem, N_CONST * 16)
            pe.wait_ge(s_wlo.sem, 5)

            def transposes(src, banks, sem):
                for k in range(KD):
                    for t in range(NT):
                        i = nc.tensor.transpose(bank[banks + k][:, t * P:(t + 1) * P], src[:, t, k * P:(k + 1) * P], eye32[:, :])
                    i.then_inc(sem, 1)

            def three(out_ap, lh, ll, rh, rl):
                n = len(lh)
                for k in range(n):
                    nc.tensor.matmul(out_ap, lh[k], rh[k], start=(k == 0), stop=False)
                    nc.tensor.matmul(out_ap, lh[k], rl[k], start=False, stop=False)
                    i = nc.tensor.matmul(out_ap, ll[k], rh[k], start=False, stop=(k == n - 1))
                return i

            def one_head(operand, rows, h, c0, c1):
                return operand[0:rows, bass.ds(h, 1), c0:c1].rearrange("p a c -> p (a c)")

            def score_maxima(b, hp, first):
                for u, cuts in enumerate((((3, 0),), ((2, 0), (0, 384)), ((1, 0),))):
                    if not first:
                        pe.wait_ge(s_max.sem, s_max.at(b, u - 2) + 3 * hp)
                    for t, c in cuts:
                        for i in range(2):
                            o = ps[:, 2 * u + i, c:c + (t + 1) * P]
                            nc.tensor.matmul(o, one_head(qop, KB, 2 * hp + i, t * P, (t + 1) * P),
                                             one_head(kop, KB, 2 * hp + i, 0, (t + 1) * P), start=True, stop=False)
                            n = nc.tensor.matmul(o[:, t * P:(t + 1) * P], eyeb[:, :], mask_qk[:, :], start=False, stop=True)
                    n.then_inc(s_mm.sem, 1)

            def scores_T(b, h, i, first=False):
                if not first:
                    pe.wait_ge(ehi_ok.sem, ehi_ok.at(b, -1) + h)
                for j in range(NT):
                    bk_, c = divmod(POFF[j], 512)
                    o = ps[:, 3 * i + bk_, c:c + S - j * P]
                    nc.tensor.matmul(o, one_head(kop, KM, h, j * P, (j + 1) * P), one_head(qop, KM, h, j * P, S), start=True, stop=False)
                    n = nc.tensor.matmul(o[:, 0:P], eyeb[:, :], mask_kq[:, :], start=False, stop=True)
                n.then_inc(st_mm.sem, 1)

            def values(b, h, i, first=False):
                pe.wait_ge(elo_ok.sem, elo_ok.at(b, 1) + h)
                if not first:
                    pe.wait_ge(norm_ok.sem, norm_ok.at(b, -1) + h)
                for t in range(NT):
                    o = bank[6 + i][:, t * (HD + 1):(t + 1) * (HD + 1)]
                    for j in range(t + 1):
                        c = POFF[j] + (t - j) * P
                        vh = v_hi[:, j, bass.ds(h, 1), :].rearrange("p a c -> p (a c)")
                        vl = v_lo[:, j, bass.ds(h, 1), :].rearrange("p a c -> p (a c)")
                        nc.tensor.matmul(o, p_hi[:, i, c:c + P], vh, start=(j == 0), stop=False)
                        nc.tensor.matmul(o[:, 0:HD], p_hi[:, i, c:c + P], vl, start=False, stop=False)
                        n = nc.tensor.matmul(o, p_lo[:, i, c:c + P], vh, start=False, stop=(j == t))
                n.then_inc(pv_mm.sem, 1)

            def quantised(b, lin):
                n = (KD, 2)[lin]
                for side, src in ((0, (xn, act)[lin]), (1, (fw, cw)[lin])):
                    if side == 1:
                        ld = (fw_ld, cw_ld)[lin]
                        pe.wait_ge(ld.sem, ld.at(b, 1))
                    elif lin == 0:
                        pe.wait_ge(xn_ok.sem, xn_ok.at(b, 8))
                    else:
                        pe.wait_ge(a_ok.sem, a_ok.at(b, 4))
                    for k in range(n):
                        bk_ = (4 * side, 4 + 2 * side)[lin] + k
                        for t in range(4):
                            i = nc.tensor.transpose(bank[bk_][:, t * P:(t + 1) * P], src[:, t, k * P:(k + 1) * P], eye32[:, :])
                        i.then_inc(am_mm.sem, 1)
                for m, side in enumerate((1, 0)):
                    pe.wait_ge(dg_ok.sem, dg_ok.at(b, 2 * lin + m + 1))
                    for k in range(n):
                        i = nc.tensor.matmul(bank[(0, 4)[lin] + side][:, k * P:(k + 1) * P], ones32[:, :], dg[:, side, k, :],
                                             start=True, stop=True)
                    i.then_inc(bc_mm.sem, 1)
                for m, (side, src) in enumerate(((1, wqz), (0, xq))):
                    pe.wait_ge(q3_ok.sem, q3_ok.at(b, 8 * lin + 4 * m + 4))
                    for k in range(n):
                        bk_ = (((2, 4)[side] + k // 2), (6, 7)[side])[lin]
                        for t in range(4):
                            c = (k % 2) * 512 + t * P
                            i = nc.tensor.transpose(psb[:, bk_, c:c + P], src[:, t, k * P:(k + 1) * P], eyeb[:, :])
                        if k % 2 == 1:
                            i.then_inc(qt_mm.sem, 1)
                pe.wait_ge(wd_ok.sem, wd_ok.at(b, lin + 1))
                for t in range(4):
                    i = nc.tensor.matmul(bank[(6, 4)[lin]][:, t * P:(t + 1) * P], ones32[:, :], dg[:, 1, t, :], start=True, stop=True)
                i.then_inc(wd_mm.sem, 1)
                pe.wait_ge(qt_ok.sem, qt_ok.at(b, (4, 6)[lin]))
                for t in range(NT):
                    for k in range(n):
                        i = nc.tensor.matmul(bank[t], xqT[:, k, t * P:(t + 1) * P], wqT[:, k, :], start=(k == 0), stop=(k == n - 1))
                    i.then_inc(l_mm.sem, 1)

            tiles = lambda a, t: [a[:, k, t * P:(t + 1) * P] for k in range(KD)]
            cols = lambda a: [a[:, k, :] for k in range(KD)]
            with pe.Fori(0, B) as b:
                pe.wait_ge(xn_ok.sem, xn_ok.at(b, 4))
                transposes(xn, 0, t_mm.sem)
                pe.wait_ge(t_lo_ok.sem, t_lo_ok.at(b, 4))
                for i in range(8):
                    w, g = i // 4, i % 4
                    three(bank[(4 + i) % 8], tiles(w_hi[:, w], g), tiles(w_lo[:, w], g), cols(t_hi), cols(t_lo)).then_inc(qk_mm.sem, 1)
                for t in range(NT):
                    pe.wait_ge(qk_lo_ok.sem, qk_lo_ok.at(b, t + 1))
                    three(bank[4 + t], tiles(t_hi, t), tiles(t_lo, t), cols(w_hi[:, 2]), cols(w_lo[:, 2])).then_inc(v_mm.sem, 1)
                pe.wait_ge(qk_lo_ok.sem, qk_lo_ok.at(b, 8))
                pe.wait_ge(v32_ok.sem, v32_ok.at(b, 4))
                pe.wait_ge(op_ld.sem, op_ld.at(b, 24))
                for g in range(2):
                    if g == 0:
                        score_maxima(b, 0, True)
                    with pe.Fori((1, 4)[g], (4, 8)[g]) as hp:
                        score_maxima(b, hp, False)
                    pe.wait_ge(s_max.sem, s_max.at(b, 12 * g + 12))
                    if g == 1:
                        pe.wait_ge(m_row_ok.sem, m_row_ok.at(b, 1))
                    for t in range(NT):
                        n = nc.tensor.transpose(ps[0:H // 2, 6, t * P:(t + 1) * P], mx[:, t, 8 * g:8 * g + 8], eye32[:, :])
                    n.then_inc(m_mm.sem, 1)
                pe.wait_ge(m_ld.sem, m_ld.at(b, 2))
                pe.wait_ge(v_lo_ok.sem, v_lo_ok.at(b, 4))
                scores_T(b, 0, 0, True)
                scores_T(b, 1, 1, True)
                values(b, 0, 0, True)
                scores_T(b, 2, 0)
                values(b, 1, 1, True)
                with pe.Fori(1, PAIRS - 1) as hp:
                    scores_T(b, 2 * hp + 1, 1)
                    values(b, 2 * hp, 0)
                    scores_T(b, 2 * hp + 2, 0)
                    values(b, 2 * hp + 1, 1)
                scores_T(b, H - 1, 1)
                values(b, H - 2, 0)
                values(b, H - 1, 1)
                pe.wait_ge(norm_ok.sem, norm_ok.at(b, H))
                transposes(o32, 0, t_mm.sem)
                pe.wait_ge(t_lo_ok.sem, t_lo_ok.at(b, 8))
                for t in range(NT):
                    three(bank[4 + t], tiles(t_hi, t), tiles(t_lo, t), cols(w_hi[:, 3]), cols(w_lo[:, 3])).then_inc(wo_mm.sem, 1)
                quantised(b, 0)
                quantised(b, 1)
                pe.wait_ge(xn_ok.sem, xn_ok.at(b, 12))
                transposes(xn, 4, t_mm.sem)
                pe.wait_ge(t_lo_ok.sem, t_lo_ok.at(b, 12))
                for t in range(NT):
                    n = three(bank[0][:, t * E:(t + 1) * E], tiles(t_hi, t), tiles(t_lo, t), cols(g_hi), cols(g_lo))
                n.then_inc(lg_mm.sem, 1)
                pe.wait_ge(r_mask.sem, r_mask.at(b, 1))
                for t in range(NT):
                    for u in range(t + 1):
                        nc.tensor.matmul(bank[0][:, 128 + t * E:128 + (t + 1) * E], (onesb, before)[u == t][:, :], chosenb[:, u, :],
                                         start=(u == 0), stop=(u == t))
                for t in range(NT):
                    n = nc.tensor.matmul(bank[1][:, 0:E], onesb[:, :], chosenb[:, t, :], start=(t == 0), stop=(t == NT - 1))
                n.then_inc(rk_mm.sem, 1)



def expert_part(nc, eye32_c, eye16_c, tile_c, counts, split_w, x3_rows, table, out):
    with ExitStack() as ctx:
        def sb(name, shape, dt):
            return ctx.enter_context(nc.sbuf_tensor(name, shape, dt))

        def sem(name):
            return ctx.enter_context(nc.semaphore(name))

        ps = ctx.enter_context(nc.psum_tensor("ps2", [P, 8, 512], F32))
        ps16 = ps[:, :, :].bitcast(F16)
        XT, GU, HT, Y = 0, 2, 4, 6
        AHEAD = 8
        COLS = 2 * P

        eye32, eye16, tile_no = sb("eye32b", [P, P], F32), sb("eye16b", [P, P], F16), sb("tile_no", [P, 2], F32)
        need, first, le, row1 = sb("need", [P, E], F32), sb("first", [P, E], F32), sb("le", [P, 2, E], F32), sb("row1", [P, E], F32)
        first_i = sb("first_i", [P, E], I32)
        own = sb("own", [P, 4, 2], F32)
        block_i = sb("block_i", [P, 2], I32)
        lists = sb("lists", [P, 2, P, 2], I32)
        listf = sb("listf", [P, 2, P], F32)
        tokens = sb("tokens", [P, COLS], I32)
        gates = sb("gates", [P, COLS], F32)
        weight_no = sb("weight_no", [1, COLS], I32)
        wbuf = sb("wbuf", [P, 2 * (WC + W2C)], F16)
        xg = sb("xg", [P, AHEAD, 2 * D], F16)
        xT = sb("xT", [P, 2, 2 * D], F16)
        idx_g, idx_s, gcol = sb("idx_g", [P, AHEAD], I32), sb("idx_s", [P, 2], I32), sb("gcol", [P, 2], F32)
        th, h1, h = sb("th2", [P, 2, F], F32), sb("h1", [P, 2, F], F32), sb("h", [P, 2, 2 * P], F32)
        hT_hi, hT_lo = sb("hT_hi", [P, 2, 2 * P], F16), sb("hT_lo", [P, 2, 2 * P], F16)
        y = sb("y", [P, 2, D], F32)
        idle_p, idle_q, pacer = sb("idle_p2", [P, 1], F32), sb("idle_q", [P, 1], F32), sb("pacer", [P, 1], F32)

        s_in, s_plan, s_blk, s_list = sem("s_in"), sem("s_plan"), sem("s_blk"), sem("s_list")
        s_lt, s_tr, s_out, s_ready = sem("s_lt"), sem("s_tr"), sem("s_out_lists"), sem("s_ready")
        idx_ok, g_done, xt_mm, xt_ok = sem("idx_ok"), [sem(f"g_done{q}") for q in range(AHEAD)], sem("xt_mm"), sem("xt_ok")
        gu_mm, th_ok, h1_ok, h_ok = sem("gu_mm"), sem("th2_ok"), sem("h1_ok"), sem("h_ok")
        ht_mm, hth_ok, htl_ok, y_mm, y_ok = sem("ht_mm"), sem("hth_ok"), sem("htl_ok"), sem("y_mm"), sem("y_ok")
        acc_st, w_ld, s_idle = sem("acc_st"), sem("w_ld"), sem("s_idle")
        s_pace = sem("s_pace")

        block = ctx.enter_context(nc.Block())

        @block.sync
        def _(sp):
            sp.dma_start(eye32[:, :], eye32_c).then_inc(s_in, 16)
            sp.dma_start(eye16[:, :], eye16_c).then_inc(s_in, 16)
            sp.dma_start(tile_no[:, :], tile_c).then_inc(s_in, 16)
            sp.dma_start(wbuf[:, WC + W2C:2 * (WC + W2C)], split_w[0]).then_inc(w_ld, 16)
            sp.wait_ge(w_ld, 16)
            sp.dma_start(wbuf[:, 0:WC + W2C], split_w[1]).then_inc(w_ld, 16)
            sp.wait_ge(w_ld, 32)
            sp.wait_ge(s_ready, 1)
            with sp.Fori(1, E // 2) as n:
                for side in range(2):
                    done = sp.value_load(first_i[0:1, bass.ds(2 * n + side - 1, 1)], min_val=0, max_val=TILES)
                    sp.wait_ge(y_mm, done)
                    sp.dma_start(wbuf[:, (1 - side) * (WC + W2C):(2 - side) * (WC + W2C)], split_w[2 * n + side]).then_inc(w_ld, 16)
                    sp.wait_ge(w_ld, 32 * n + 16 * side + 16)
                    sp.dma_start(pacer[0:1, 0:1], eye32_c[0:1, 0:1]).then_inc(s_pace, 16)
            sp.wait_ge(s_pace, 16 * (E - 2))
            sp.wait_ge(acc_st, 16 * TILES)

        @block.gpsimd
        def _(pool):
            pool.wait_ge(s_blk, 1)
            for c in range(2):
                n = (P, TILES - P)[c]
                nc.gpsimd.indirect_dma_start(lists[0:n, c, :, :].rearrange("p s a -> p (s a)"), None,
                                             table.rearrange("(t s) a -> t (s a)", s=P),
                                             bass.IndirectOffsetOnAxis(ap=block_i[0:n, c:c + 1], axis=0)).then_inc(s_list, 16)

            nc.gpsimd.memset(idle_p[:, :], 0.0).then_inc(s_idle, 1)
            pool.wait_ge(s_idle, 1)

            def carry(n):
                pool.wait_ge(s_idle, n)
                nc.gpsimd.tensor_tensor(idle_q[:, :], idle_p[:, :], idle_p[:, :], ALU.add).then_inc(s_idle, 1)

            def gather(i, q, n):
                pool.wait_ge(idx_ok, i + 1)
                carry(n)
                nc.gpsimd.indirect_dma_start(xg[:, q, :], None, x3_rows,
                                             bass.IndirectOffsetOnAxis(ap=idx_g[:, q:q + 1], axis=0)).then_inc(g_done[q], 16)

            def scatter(i, p, n, first=False):
                if not first:
                    pool.wait_ge(acc_st, 16 * i)
                carry(n)
                pool.wait_ge(y_ok, i + 1)
                carry(n + 1)
                nc.gpsimd.indirect_dma_start(out, bass.IndirectOffsetOnAxis(ap=idx_s[:, p:p + 1], axis=0),
                                             y[:, p, :], None, compute_op=ALU.add).then_inc(acc_st, 16)

            for q in range(AHEAD):
                gather(q, q, q + 1)
            first_n = AHEAD + 1
            for q in range(AHEAD):
                gather(q + AHEAD, q, first_n + 3 * q)
                scatter(q, q % 2, first_n + 3 * q + 1, q == 0)
            with pool.Fori(1, TILES // AHEAD - 1) as j:
                for q in range(AHEAD):
                    i = AHEAD * j + q
                    gather(i + AHEAD, q, 3 * i + first_n)
                    scatter(i, q % 2, 3 * i + first_n + 1)
            for q in range(AHEAD):
                i = TILES - AHEAD + q
                scatter(i, q % 2, 3 * (TILES - AHEAD) + first_n + 2 * q)

        @block.scalar
        def _(act_e):
            def gate_tanh(i, p):
                act_e.wait_ge(gu_mm, i + 1)
                nc.scalar.activation(th[:, p, :], ps[:, GU + p, 0:F], ACT.Tanh, scale=0.5).then_inc(th_ok, 1)

            def step(i, p, first=False, more=True):
                act_e.wait_ge(ht_mm, i + 1)
                nc.scalar.copy(hT_hi[:, p, :], ps[:, HT + p, 0:2 * P]).then_inc(hth_ok, 1)
                if more:
                    gate_tanh(i + 1, 1 - p)
                if not first:
                    act_e.wait_ge(acc_st, 16 * (i - 1))
                act_e.wait_ge(y_mm, i + 1)
                nc.scalar.activation(y[:, p, :], ps[:, Y + p, :], ACT.Copy, scale=gcol[:, p:p + 1]).then_inc(y_ok, 1)

            gate_tanh(0, 0)
            for p in range(2):
                step(p, p, True)
            with act_e.Fori(1, TILES // 2 - 1) as j:
                for p in range(2):
                    step(2 * j + p, p)
            for p in range(2):
                step(TILES - 2 + p, p, more=p == 0)

        @block.vector
        def _(dve):
            count = [0]

            def link(i):
                count[0] += 1
                i.then_inc(s_plan, 1)
                dve.wait_ge(s_plan, count[0])

            link(nc.vector.tensor_scalar(need[:, :], counts[:, :], 1.0 / P, (P - 1.0) / P - 0.5 + 0.5 / P, ALU.mult, ALU.add))
            link(nc.vector.tensor_scalar(need[:, :], need[:, :], MAGIC, MAGIC, ALU.add, ALU.subtract))
            link(nc.vector.tensor_scalar(need[:, :], need[:, :], 1.0, None, ALU.max))
            link(nc.vector.memset(row1[:, :], 1.0))
            link(nc.vector.tensor_tensor_scan(first[:, :], row1[:, :], need[:, :], 0.0, ALU.mult, ALU.add))
            link(nc.vector.tensor_tensor(first[:, :], first[:, :], need[:, :], ALU.subtract))
            link(nc.vector.tensor_copy(first_i[:, :], first[:, :]))
            dve.wait_ge(s_in, 48)
            for c in range(2):
                link(nc.vector.tensor_scalar(le[:, c, :], first[:, :], tile_no[:, c:c + 1], None, ALU.is_le))
            link(nc.vector.tensor_reduce(own[:, 0, :], le[:, :, :], AX.X, ALU.add))
            for c in range(2):
                link(nc.vector.tensor_tensor(le[:, c, :], le[:, c, :], first[:, :], ALU.mult))
            link(nc.vector.tensor_reduce(own[:, 1, :], le[:, :, :], AX.X, ALU.max))
            link(nc.vector.tensor_scalar(own[:, 2, :], own[:, 0, :], -1.0, float(BLOCKS), ALU.add, ALU.mult))
            link(nc.vector.tensor_tensor(own[:, 2, :], own[:, 2, :], own[:, 1, :], ALU.subtract))
            link(nc.vector.tensor_tensor(own[:, 2, :], own[:, 2, :], tile_no[:, :], ALU.add))
            nc.vector.tensor_copy(block_i[:, :], own[:, 2, :]).then_inc(s_blk, 1)
            link(nc.vector.tensor_scalar(own[:, 1, :], own[:, 0, :], 16.0, None, ALU.mult))
            nc.vector.memset(listf[:, :, :], 0.0)
            link(nc.vector.memset(tokens[:, :], 0))
            dve.wait_ge(s_list, 32)
            for c in range(2):
                n = (P, TILES - P)[c]
                i = nc.vector.tensor_copy(listf[0:n, c, :], lists[0:n, c, :, 0])
            i.then_inc(s_lt, 1)
            dve.wait_ge(s_tr, 1)
            nc.vector.tensor_copy(tokens[:, 0:TILES], ps[:, 0, 0:TILES])
            nc.vector.tensor_copy(gates[:, 0:TILES], ps[:, 1, 0:TILES])
            nc.vector.tensor_copy(weight_no[:, :], ps[0:1, 3, 0:COLS]).then_inc(s_ready, 1)
            dve.wait_ge(s_ready, 1)

            def index_gather(i, q, first=False):
                if not first:
                    dve.wait_ge(g_done[q], 16 // AHEAD * (i - q))
                nc.vector.tensor_copy(idx_g[:, q:q + 1], tokens[:, bass.ds(i, 1)]).then_inc(idx_ok, 1)

            def x_out(i, p, first=False):
                dve.wait_ge(xt_mm, i + 1)
                nc.vector.tensor_copy(xT[:, p, :], ps16[:, XT + p, :]).then_inc(xt_ok, 1)

            def hidden(i, p, first=False):
                dve.wait_ge(th_ok, i + 1)
                nc.vector.scalar_tensor_tensor(out=h1[:, p, :], in0=th[:, p, :], scalar=1.0, in1=ps[:, GU + p, 0:F],
                                               op0=ALU.add, op1=ALU.mult).then_inc(h1_ok, 1)
                dve.wait_ge(h1_ok, i + 1)
                nc.vector.scalar_tensor_tensor(out=h[:, p, 0:P], in0=h1[:, p, 0:P], scalar=0.5, in1=ps[:, GU + p, F:F + P],
                                               op0=ALU.mult, op1=ALU.mult)
                twice = lambda a: a.unsqueeze(1).to_broadcast([P, 2, F - P])
                nc.vector.scalar_tensor_tensor(out=h[:, p, P:2 * P].rearrange("p (a c) -> p a c", a=2), in0=twice(h1[:, p, P:F]), scalar=0.5,
                                               in1=twice(ps[:, GU + p, F + P:2 * F]), op0=ALU.mult, op1=ALU.mult).then_inc(h_ok, 1)

            def h_out(i, p, first=False):
                if not first:
                    dve.wait_ge(acc_st, 16 * (i - 1))
                nc.vector.tensor_copy(idx_s[:, p:p + 1], tokens[:, bass.ds(i, 1)])
                nc.vector.tensor_copy(gcol[:, p:p + 1], gates[:, bass.ds(i, 1)])
                dve.wait_ge(hth_ok, i + 1)
                nc.vector.tensor_tensor(hT_lo[:, p, :], ps[:, HT + p, 0:2 * P], hT_hi[:, p, :], ALU.subtract).then_inc(htl_ok, 1)

            def step(i, q, first=False, gathers=True, more=True):
                if gathers:
                    index_gather(i + AHEAD, q)
                hidden(i, q % 2)
                if more:
                    x_out(i + 2, q % 2)
                h_out(i, q % 2, first)

            for q in range(AHEAD):
                index_gather(q, q, True)
            for q in range(2):
                x_out(q, q)
            for q in range(AHEAD):
                step(q, q, first=q < 2)
            with dve.Fori(1, TILES // AHEAD - 1) as j:
                for q in range(AHEAD):
                    step(AHEAD * j + q, q)
            for q in range(AHEAD):
                step(TILES - AHEAD + q, q, gathers=False, more=q < AHEAD - 2)

        @block.tensor
        def _(pe):
            pe.wait_ge(s_in, 48)
            pe.wait_ge(s_lt, 1)
            for c in range(2):
                n = (P, TILES - P)[c]
                nc.tensor.transpose(ps[:, 0, c * P:c * P + n], listf[0:n, c, :], eye32[0:n, 0:n])
                nc.tensor.transpose(ps[:, 1, c * P:c * P + n], lists[0:n, c, :, 1].bitcast(F32), eye32[0:n, 0:n])
                m = nc.tensor.transpose(ps[0:1, 3, c * P:(c + 1) * P], own[:, 1, c:c + 1], eye32[:, :])
            m.then_inc(s_tr, 1)
            pe.wait_ge(s_ready, 1)

            def x_in(i, q, first=False):
                p = q % 2
                pe.wait_ge(g_done[q], 16 // AHEAD * (i - q) + 16)
                if not first:
                    pe.wait_ge(xt_ok, i - 1)
                for k in range(2 * KD):
                    n = nc.tensor.transpose(ps16[:, XT + p, k * P:(k + 1) * P], xg[:, q, k * P:(k + 1) * P], eye16[:, :])
                n.then_inc(xt_mm, 1)

            def weights(i):
                loaded = pe.value_load(weight_no[0:1, bass.ds(i, 1)], min_val=16, max_val=16 * E)
                return loaded, ((loaded % 32) * ((WC + W2C) // 16)).with_bounds(min_val=0, max_val=WC + W2C)

            def up(i, p, loaded, at, first=False):
                pe.wait_ge(w_ld, loaded)
                pe.wait_ge(xt_ok, i + 1)
                if not first:
                    pe.wait_ge(h_ok, i - 1)
                o = ps[:, GU + p, 0:2 * F]
                for k in range(KD):
                    hi, lo = xT[:, p, k * P:(k + 1) * P], xT[:, p, (KD + k) * P:(KD + k + 1) * P]
                    w_hi = wbuf[:, bass.ds(at + k * 4 * F, 2 * F)]
                    w_lo = wbuf[:, bass.ds(at + k * 4 * F + 2 * F, 2 * F)]
                    nc.tensor.matmul(o, hi, w_hi, start=(k == 0), stop=False)
                    nc.tensor.matmul(o, hi, w_lo, start=False, stop=False)
                    n = nc.tensor.matmul(o, lo, w_hi, start=False, stop=(k == KD - 1))
                n.then_inc(gu_mm, 1)

            def turn(i, p, first=False):
                pe.wait_ge(h_ok, i + 1)
                if not first:
                    pe.wait_ge(htl_ok, i - 1)
                nc.tensor.transpose(ps[:, HT + p, 0:P], h[:, p, 0:P], eye32[:, :])
                n = nc.tensor.transpose(ps[:, HT + p, P:2 * P], h[:, p, P:2 * P], eye32[:, :])
                n.then_inc(ht_mm, 1)

            def down(i, p, at, first=False):
                pe.wait_ge(htl_ok, i + 1)
                if not first:
                    pe.wait_ge(y_ok, i - 1)
                w = [wbuf[:, bass.ds(at + WC + a * D, D)] for a in range(3)]
                for n, (l, r) in enumerate(((hT_hi[:, p, 0:P], w[0]), (hT_hi[:, p, 0:P], w[1]), (hT_lo[:, p, 0:P], w[0]),
                                            (hT_hi[:, p, P:2 * P], w[2]), (hT_lo[:, p, P:2 * P], w[2]))):
                    m = nc.tensor.matmul(ps[:, Y + p, :], l, r, start=(n == 0), stop=(n == 4))
                m.then_inc(y_mm, 1)

            x_in(0, 0, True)
            x_in(1, 1, True)
            up(0, 0, *weights(0), True)
            def step(i, q, at, first=False, more=2):
                if more > 0:
                    loaded, at_next = weights(i + 1)
                if more > 1:
                    x_in(i + 2, (q + 2) % AHEAD)
                turn(i, q % 2, first)
                if more > 0:
                    up(i + 1, (q + 1) % 2, loaded, at_next, first and q == 0)
                down(i, q % 2, at, first)
                return at_next if more > 0 else None

            at = weights(0)[1]
            for q in range(AHEAD):
                at = step(q, q, at, first=q < 2)
            with pe.Fori(1, TILES // AHEAD - 1) as j:
                at = weights(AHEAD * j)[1]
                for q in range(AHEAD):
                    at = step(AHEAD * j + q, q, at)
            at = weights(TILES - AHEAD)[1]
            for q in range(AHEAD):
                at = step(TILES - AHEAD + q, q, at, more=AHEAD - 1 - q)


def lay_out(inputs):
    g = {k: np.asarray(v) for k, v in inputs.items()}
    rows = lambda v: np.ascontiguousarray(np.broadcast_to(v[None, :], (P, D)))
    cols = lambda v: np.ascontiguousarray(v.reshape(KD, P).T)
    a = {
        "x_in": g["x"], "fside": g["fside_BxS2xS2_0"], "ctx_w": g["ctx_1024"],
        "wq": g["L0_attn_wq"], "bq": cols(g["L0_attn_bq"]), "wk": g["L0_attn_wk"], "bk": cols(g["L0_attn_bk"]),
        "wv": g["L0_attn_wv"], "bv": rows(g["L0_attn_bv"]), "wo": g["L0_attn_wo"], "bo": rows(g["L0_attn_bo"]),
        "wg": np.ascontiguousarray(g["L0_ffn_wg"].T), "w1": g["L0_ffn_w1"], "v1": g["L0_ffn_v1"], "w2": g["L0_ffn_w2"],
    }
    a.update(shape_constants())
    return a


def kernel(**inputs):
    import concourse.bacc as bacc
    from concourse.bass_utils import run_bass_kernel_spmd

    nc = bacc.Bacc("TRN2", target_bir_lowering=False, num_devices=1)
    arrays = lay_out(inputs)
    args = [nc.dram_tensor(name, a.shape, mybir.dt.from_np(a.dtype), kind="ExternalInput").ap() for name, a in arrays.items()]
    args.append(nc.dram_tensor("out", [TOK + P, D], F32, kind="ExternalOutput").ap())
    decoder_kernel(nc, *args)
    r = run_bass_kernel_spmd(nc, [arrays], core_ids=[0])
    return r.results[0]["out"][0:TOK].reshape(B, S, D)
```

```python
from contextlib import ExitStack

import numpy as np
import concourse.bass as bass
from concourse import mybir

F32, F16, BF16, I32 = mybir.dt.float32, mybir.dt.float16, mybir.dt.bfloat16, mybir.dt.int32
ALU, ACT, AX = mybir.AluOpType, mybir.ActivationFunctionType, mybir.AxisListType

P = 128
B, S, D = 4, 512, 512
NT, KD = S // P, D // P
H, HD = 16, 32
HG = P // HD
PAIRS = H // 2
QI = 256
E, TOPK, F = 32, 8, 192
EB = 7
LATE = E - B * EB
LN_EPS, Q_EPS, QMAX = 1e-5, 1e-6, 127.0
MAGIC = 1.5 * 2.0 ** 23
SCALE = 1.0 / np.sqrt(np.float32(HD))
KB = 3 * HD + 16
KM = KB + 1
WC = KD * 2 * 2 * F
W2C = 4 * D
TOK = B * S
REGION = TOK
BLOCKS = REGION // P
TILES = TOK * TOPK // P + E
TABLE = E * BLOCKS + TILES
KT = TOPK * NT
POFF = {0: 0, 1: 512, 3: 896, 2: 1024}
PCOLS = 1280


def shape_constants():
    def parts(x, n):
        out = []
        for _ in range(n):
            h = x.astype(np.float16)
            out.append(h)
            x = x - h.astype(np.float64)
        return out

    eye = np.eye(P, dtype=np.float32)
    i = np.arange(P)
    bf = lambda a: (np.ascontiguousarray(a, np.float32).view(np.uint32) >> 16).astype(np.uint16)
    later = np.where(i[None, :] > i[:, None], np.float32(-1e30), np.float32(0))
    start = np.float32(2.0 ** (-8.0 / H))
    slope = np.array([2.0 ** (-8.0 / H) * (2.0 ** (-8.0 / H)) ** h for h in range(H)], np.float32)
    c = slope.astype(np.float64) * np.sqrt(HD)
    pos = np.arange(S)
    k_rows = np.zeros((32, S), np.float16)
    q_rows = np.zeros((32, H, S), np.float16)
    for n, part in enumerate(parts(c, 3)):
        k_rows[n] = pos % P
        q_rows[n] = part[:, None]
    for j in range(NT):
        for n, part in enumerate(parts(c[:, None] * (P * j - pos)[None, :], 3)):
            k_rows[3 + 3 * j + n] = (pos // P == j)
            q_rows[3 + 3 * j + n] = part
    k_rows[16] = 1
    return {
        "c_eye32": eye, "c_eye16": eye.astype(np.float16), "c_eyeb": bf(eye),
        "c_mask_qk": bf(later), "c_mask_kq": bf(later.T),
        "c_k_rows": k_rows, "c_q_rows": q_rows,
        "c_before": bf(i[:, None] < i[None, :]),
        "c_pads": np.stack([TOK + np.arange(TABLE * P, dtype=np.int32) % P, np.zeros(TABLE * P, np.int32)], 1),
        "c_tok": (np.arange(NT)[None, :] * P + i[:, None]).astype(np.float32),
        "c_keep": np.tile((np.arange(NT * E) % E != 0).astype(np.float32), (P, 1)),
        "c_base": np.tile((np.arange(NT * E) % E * REGION).astype(np.float32), (P, 1)),
        "c_rank": np.tile(np.arange(1, TOPK + 1).astype(np.float32), (P, 1)),
        "c_pad_pos": (E * REGION + np.arange(KT)[None, :] * P + i[:, None]).astype(np.int32),
        "c_pad_pay": np.tile(np.stack([TOK + i, 0 * i], 1)[:, None, :], (1, KT, 1)).astype(np.int32),
        "c_tile": np.stack([i, i + P], 1).astype(np.float32),
    }


class Signal:

    def __init__(self, sem, per, each=1, start=0):
        self.sem, self.per, self.each, self.start = sem, per, each, start

    def at(self, b, n):
        if isinstance(b, int):
            return self.start + self.each * (b * self.per + n)
        return b * (self.each * self.per) + (self.start + self.each * n)


def decoder_kernel(nc, x_in, fside, ctx_w, wq, bq, wk, bk, wv, bv, wo, bo, wg, w1, v1, w2,
                   eye32_c, eye16_c, eyeb_c, mask_qk_c, mask_kq_c, k_rows_c, q_rows_c,
                   before_c, pads_c, tok_c, keep_c, base_c, rank_c, pad_pos_c, pad_pay_c, tile_c, out):
    with nc.sbuf_tensor("counts", [P, E], F32) as counts, nc.sbuf_tensor("pos", [P, KT], I32) as pos, \
            nc.sbuf_tensor("pay", [P, KT, 2], I32) as pay:
        split_w = nc.dram_tensor("split_w", [E, P, WC + W2C], F16, kind="Internal").ap()
        x3_rows = nc.dram_tensor("x3_rows", [TOK + P, 2 * D], F16, kind="Internal").ap()
        table = nc.dram_tensor("table", [TABLE * P, 2], I32, kind="Internal").ap()
        dense_part(nc, x_in, fside, ctx_w, wq, bq, wk, bk, wv, bv, wo, bo, wg, w1, v1, w2,
                   eye32_c, eye16_c, eyeb_c, mask_qk_c, mask_kq_c, k_rows_c, q_rows_c,
                   before_c, pads_c, tok_c, keep_c, base_c, rank_c, pad_pos_c, pad_pay_c,
                   counts, pos, pay, split_w, x3_rows, table, out)
        expert_part(nc, w1, v1, w2, eye32_c, eye16_c, tile_c, counts, pos, pay, split_w, x3_rows, table, out)


def dense_part(nc, x_in, fside, ctx_w, wq, bq, wk, bk, wv, bv, wo, bo, wg, w1, v1, w2,
               eye32_c, eye16_c, eyeb_c, mask_qk_c, mask_kq_c, k_rows_c, q_rows_c,
               before_c, pads_c, tok_c, keep_c, base_c, rank_c, pad_pos_c, pad_pay_c,
               counts, pos, pay, split_w, x3_rows, table, out):
    ctx = ExitStack()
    with ctx:
        def sb(name, shape, dt):
            return ctx.enter_context(nc.sbuf_tensor(name, shape, dt))

        started = []

        def sig(name, per=1, each=1, start=0):
            s = Signal(ctx.enter_context(nc.semaphore(name)), per, each, start)
            if start:
                started.append(s)
            return s

        ps = ctx.enter_context(nc.psum_tensor("ps", [P, 8, 512], F32))
        psb = ps[:, :, :].bitcast(BF16)

        eye32, eye16, eyeb = sb("eye32", [P, P], F32), sb("eye16", [P, P], F16), sb("eyeb", [P, P], BF16)
        mask_qk, mask_kq = sb("mask_qk", [P, P], BF16), sb("mask_kq", [P, P], BF16)
        ones32 = sb("ones32", [P, P], F32)
        eps, neg_half, half = sb("eps", [P, 4], F32), sb("neg_half", [P, 4], F32), sb("half", [P, 4], F32)
        w_hi = sb("w_hi", [P, 4, KD, D], F16)
        w_lo = sb("w_lo", [P, 4, KD, D], F16)
        b_qk = sb("b_qk", [P, 2 * KD], F32)
        b_v, b_o = sb("b_v", [P, KD], F32), sb("b_o", [P, D], F32)
        x = sb("x", [P, NT, D], F32)
        x1 = sb("x1", [P, NT, D], F32)
        xn, xa = sb("xn", [P, NT, D], F32), sb("xa", [P, NT, D], F32)
        t_hi, t_lo = sb("t_hi", [P, KD, S], F16), sb("t_lo", [P, KD, S], F16)
        qk_hi, qk_lo = sb("qk_hi", [P, 8, S], F16), sb("qk_lo", [P, 8, S], F16)
        qop, kop = sb("qop", [P, H, S], F16), sb("kop", [P, H, S], F16)
        v_hi = sb("v_hi", [P, NT, H, HD + 1], F16)
        v_lo = sb("v_lo", [P, NT, H, HD], F16)
        mx = sb("mx", [P, NT, H], F32)
        m_row = sb("m_row", [H // 2, 2, S], F16)
        p32, p_hi, p_lo = sb("p32", [P, 2, PCOLS], F32), sb("p_hi", [P, 2, PCOLS], F16), sb("p_lo", [P, 2, PCOLS], F16)
        rden = sb("rden", [P, 2, NT], F32)
        o32 = sb("o32", [P, NT, D], F32)
        stats, mv, ve, rstd = sb("stats", [P, NT, 6], F32), sb("mv", [P, NT, 2], F32), sb("ve", [P, NT], F32), sb("rstd", [P, NT], F32)
        fw = sb("fw", [P, KD, D], F32)
        cw = sb("cw", [P, KD, QI], F32)
        act = sb("act", [P, NT, QI], F32)
        th = p32[:, :, :].rearrange("p a c -> p (a c)")[:, 0:NT * QI].rearrange("p (t c) -> p t c", t=NT)
        amax, sq = sb("amax", [P, 2, KD], F32), sb("sq", [P, 6, KD], F32)
        dg = sb("dg", [P, 2, KD, P], F32)
        rowmax, rscale, rinv = sb("rowmax", [P, 2, 4], F32), sb("rscale", [P, 2, 4], F32), sb("rinv", [P, 2, 4], F32)
        half_of = lambda a: a[:, :, :].rearrange("p a c -> p (a c)")[:, 0:KD * D].rearrange("p (t c) -> p t c", t=KD).bitcast(BF16)
        xq, wqz = half_of(p_hi), half_of(p_lo)
        wst = sb("wst", [P, WC + W2C], F16)
        wqT, xqT = (wst[:, n * KD * D:(n + 1) * KD * D].rearrange("p (t c) -> p t c", t=KD).bitcast(BF16) for n in range(2))
        wscb = sb("wscb", [P, D], F32)

        s_const = sig("s_const", 1, 16)
        s_wld = [sig(f"s_wld{n}", 1, 16) for n in range(5)]
        s_whi, s_wlo = sig("s_whi"), sig("s_wlo")
        s_one, s_mg = sig("s_one"), sig("s_mg")
        x_ld, xa_ld = sig("x_ld", 1, 16), sig("xa_ld", 1, 16)
        fw_ld, cw_ld = sig("fw_ld", 1, 16), sig("cw_ld", 1, 16)
        lna = [sig(f"lna_{n}") for n in ("stats", "mean", "var", "rstd")]
        ln = [sig(f"ln_{n}", 2) for n in ("stats", "mean", "var", "rstd")]
        xa_ok, xn_ok = sig("xa_ok", 4), sig("xn_ok", 8)
        ta_mm, ta_hi_ok, ta_lo_ok = sig("ta_mm", 4), sig("ta_hi_ok", 4), sig("ta_lo_ok", 4)
        t_mm = sig("t_mm", 8)
        t_hi_ok, t_lo_ok = sig("t_hi_ok", 8), sig("t_lo_ok", 8)
        bo_dg, bo_mm, bo_ok = sig("bo_dg"), sig("bo_mm"), sig("bo_ok")
        qk_mm, qk_hi_ok, qk_lo_ok = sig("qk_mm", 8), sig("qk_hi_ok", 8), sig("qk_lo_ok", 8)
        op_ld = sig("op_ld", 24, 16)
        v_mm, v_hi_ok, v_lo_ok = sig("v_mm", 4), sig("v_hi_ok", 4), sig("v_lo_ok", 4)
        s_mm, s_max = sig("s_mm", 3 * PAIRS), sig("s_max", 3 * PAIRS)
        m_mm, m_row_ok, m_ld = sig("m_mm", 2), sig("m_row_ok", 2), sig("m_ld", 2, 16)
        st_mm, e32_ok, ehi_ok, elo_ok = sig("st_mm", H), sig("e32_ok", H), sig("ehi_ok", H), sig("elo_ok", H)
        pv_mm, rec_ok, norm_ok = sig("pv_mm", H), sig("rec_ok", H), sig("norm_ok", H)
        xbo_ok = sig("xbo_ok", 4)
        wo_mm, x1_ok = sig("wo_mm", 4), sig("x1_ok", 4, start=1)
        am_mm, am_ok = sig("am_mm", 12), sig("am_ok", 12)
        qs_link = sig("qs_link", 12)
        qs_rat, qs_pow = sig("qs_rat", 2), sig("qs_pow", 2)
        dg_ok, bc_mm = sig("dg_ok", 4), sig("bc_mm", 4)
        sc_ok, rm_ok, ri_ok = sig("sc_ok", 16), sig("rm_ok", 4), sig("ri_ok", 4)
        q1_ok, q2_ok, q3_ok = sig("q1_ok", 16), sig("q2_ok", 16), sig("q3_ok", 16, start=1)
        qt_mm, qt_ok = sig("qt_mm", 6), sig("qt_ok", 6)
        wsb_ok = sig("wsb_ok", 2)
        l_mm, l_ok = sig("l_mm", 8), sig("l_ok", 8)
        th_ok, a1_ok, a_ok = sig("th_ok", 4), sig("a1_ok", 4), sig("a_ok", 4)
        x2_ok = sig("x2_ok", 4)
        out_st = sig("out_st", 1, 16, start=1)
        wd_ok, wd_mm = sig("wd_ok", 2), sig("wd_mm", 2)
        lg_mm, lg_ok = sig("lg_mm"), sig("lg_ok")
        magic, idle, idle_p = sb("magic", [P, 2], F32), sb("idle", [P, 1], F32), sb("idle_p", [P, 1], F32)
        g_hi, g_lo = sb("g_hi", [P, KD, E], F16), sb("g_lo", [P, KD, E], F16)
        primer = sb("primer", [P, 8], F32)
        before, onesb = sb("before", [P, P], BF16), sb("onesb", [P, P], BF16)
        keep, base, tokf = sb("keep", [P, NT * E], F32), sb("base", [P, NT * E], F32), sb("tokf", [P, NT], F32)
        rank = sb("rank", [P, TOPK], F32)
        lg, sm, rep = sb("lg", [P, NT, E], F32), sb("sm", [P, NT, E], F32), sb("rep", [P, NT, E], F32)
        top, r4 = sb("top", [P, NT, TOPK], F32), sb("r4", [P, 4, NT], F32)
        chosen, chosenb = sb("chosen", [P, NT, E], F32), sb("chosenb", [P, NT, E], BF16)
        nth, slot, gate = sb("nth", [P, NT * E], F32), sb("slot", [P, NT, E], F32), sb("gate", [P, NT, E], F32)
        hit = o32[:, 0:2, :].rearrange("p a (k c) -> p (a k) c", c=NT * E)
        hit2 = o32[:, 2:4, :].rearrange("p a (k c) -> p (a k) c", c=NT * E)
        posf = sb("posf", [P, KT], F32)
        gatek = sb("gatek", [P, KT], F32)
        x3 = wst[:, 0:NT * 2 * D].rearrange("p (t d) -> p t d", t=NT)
        zeros = wscb
        wst13 = wst[:, 0:WC].rearrange("p (k s f) -> p k s f", k=KD, s=2)
        wst2 = wst[:, WC:WC + W2C].rearrange("p (a s d) -> p a s d", a=2, s=2)
        w13f = fw[:, 0:3, :].rearrange("p a c -> p (a c)").rearrange("p (k f) -> p k f", k=KD)
        w2f = act[:, :, :].rearrange("p a c -> p (a c)").rearrange("p (a d) -> p a d", a=2)
        ew13_ld, ew2_ld, ew13_st, ew2_st = sig("ew13_ld", 2 * EB, 16), sig("ew2_ld", 3 * EB, 16), sig("ew13_st", EB, 16, start=1), sig("ew2_st", EB, 16, start=1)
        ew_hi, ew_lo13, ew_lo2 = sig("ew_hi", 2 * EB), sig("ew_lo13", EB), sig("ew_lo2", EB)
        ROUTE_LINKS = 15
        r_read = sig("r_read", 1, start=1)
        r_link, r_rep, r_ex, r_exp = sig("r_link", ROUTE_LINKS), sig("r_rep"), sig("r_ex"), sig("r_exp")
        r_mask, rk_mm, r_pos, r_tok = sig("r_mask"), sig("rk_mm"), sig("r_pos", start=1), sig("r_tok")
        x3_hi, x3_lo, x3_st = sig("x3_hi", 4), sig("x3_lo"), sig("x3_st", 1, 16, start=1)
        tb_st = sig("tb_st", KT, 16)
        init_st = sig("init_st", 1, 16)

        N_CONST = 18
        bank = [ps[:, i, :] for i in range(8)]
        x_dram = x_in.rearrange("b (t p) d -> b p t d", p=P)
        o_dram = out[0:B * S, :].rearrange("(b t p) d -> b p t d", p=P, t=NT)
        x3_dram = x3_rows[0:TOK, :].rearrange("(b t p) d -> b p t d", p=P, t=NT)
        fw_dram = fside.rearrange("b (t p) d -> b p t d", p=P)
        cw_dram = ctx_w.rearrange("b (t p) d -> b p t d", p=P)

        PAUSES = (((0, 1), (2, 3), (4,), (5,)), ((6, 7), (8, 9), (10,), (11,)))
        NEXT = lambda b, lin, pause, more: [(b + 1, n) for n in PAUSES[lin][pause]] if more else []
        AMAX_BANK = (((0, 1, 2, 3), (0, 1, 2, 3)), ((4, 5), (0, 1)))
        FILL = [6, 7]

        block = ctx.enter_context(nc.Block())

        @block.sync
        def _(sp):
            weights = [w.rearrange("(k p) n -> p k n", p=P) for w in (wq, wk, wv, wo)]
            for n in range(2):
                sp.dma_start((x, x1)[n][:, :, :], weights[n]).then_inc(s_wld[n].sem, 16)
            sp.dma_start(xa[:, :, :], x_dram[0]).then_inc(xa_ld.sem, 16)
            for dst, src in ((keep, keep_c), (base, base_c), (tokf, tok_c), (before, before_c), (pos, pad_pos_c),
                             (eye32, eye32_c), (eye16, eye16_c), (eyeb, eyeb_c), (mask_qk, mask_qk_c), (mask_kq, mask_kq_c), (b_v, bv), (b_o, bo), (b_qk[:, 0:KD], bq), (b_qk[:, KD:2 * KD], bk)):
                sp.dma_start(dst[:, :].bitcast(src.dtype), src).then_inc(s_const.sem, 16)
            sp.dma_start(rank[:, :], rank_c).then_inc(s_const.sem, 16)
            sp.dma_start(pay[:, :, :], pad_pay_c).then_inc(s_const.sem, 16)
            sp.dma_start(qop[3 * HD:4 * HD, :, :], q_rows_c).then_inc(s_const.sem, 16)
            sp.dma_start(kop[3 * HD:4 * HD, :, :], k_rows_c.unsqueeze(1).to_broadcast([HD, H, S])).then_inc(s_const.sem, 16)
            for n in range(2, 4):
                sp.wait_ge(s_wlo.sem, n - 1)
                sp.dma_start((x, x1)[n % 2][:, :, :], weights[n]).then_inc(s_wld[n].sem, 16)
            sp.dma_start(fw[:, :, 0:E], wg.rearrange("(k p) n -> p k n", p=P)).then_inc(s_wld[4].sem, 16)
            sp.dma_start(table, pads_c).then_inc(init_st.sem, 16)
            sp.wait_ge(s_one.sem, 7)
            sp.dma_start(out[TOK:TOK + P, :], zeros[:, :]).then_inc(init_st.sem, 16)
            sp.dma_start(x3_rows[TOK:TOK + P, :], zeros[:, :].bitcast(F16)).then_inc(init_st.sem, 16)
            sp.wait_ge(s_wlo.sem, 5)

            def attention_operands(b):
                for which, dst, (hi_rows, lo_row) in ((0, qop, ((0, 32), 64)), (1, kop, ((0, 64), 32))):
                    sp.wait_ge(qk_hi_ok.sem, qk_hi_ok.at(b, 4 * which + 4))
                    for r in hi_rows:
                        for i in range(HG):
                            sp.dma_start(dst[r:r + HD, i::HG, :], qk_hi[HD * i:HD * i + HD, 4 * which:4 * which + 4, :]).then_inc(op_ld.sem, 16)
                    sp.wait_ge(qk_lo_ok.sem, qk_lo_ok.at(b, 4 * which + 4))
                    for i in range(HG):
                        sp.dma_start(dst[lo_row:lo_row + HD, i::HG, :], qk_lo[HD * i:HD * i + HD, 4 * which:4 * which + 4, :]).then_inc(op_ld.sem, 16)

            def load13(e):
                sp.dma_start(w13f[:, :, 0:F], w1.rearrange("e (k p) f -> e p k f", p=P)[e]).then_inc(ew13_ld.sem, 16)
                sp.dma_start(w13f[:, :, F:2 * F], v1.rearrange("e (k p) f -> e p k f", p=P)[e]).then_inc(ew13_ld.sem, 16)

            def load2(e):
                sp.dma_start(w2f[:, 0, :], w2[:, 0:P, :][e]).then_inc(ew2_ld.sem, 16)
                for side in range(2):
                    sp.dma_start(w2f[64 * side:64 * side + 64, 1, :], w2[:, P:F, :][e]).then_inc(ew2_ld.sem, 16)

            def store_and_load(b, n, more):
                e = b * EB + n
                sp.wait_ge(ew_lo13.sem, ew_lo13.at(b, 1) + n)
                if more:
                    load13(e + 1)
                sp.dma_start(split_w[e][:, 0:WC], wst[:, 0:WC]).then_inc(ew13_st.sem, 16)
                sp.wait_ge(ew_lo2.sem, ew_lo2.at(b, 1) + n)
                if more:
                    load2(e + 1)
                sp.dma_start(split_w[e][:, WC:WC + W2C], wst[:, WC:WC + W2C]).then_inc(ew2_st.sem, 16)

            def batch(b, more):
                if more:
                    sp.wait_ge(ta_mm.sem, ta_mm.at(b, 4))
                    sp.dma_start(xa[:, :, :], x_dram[b + 1]).then_inc(xa_ld.sem, 16)
                sp.wait_ge(q3_ok.sem, q3_ok.at(b, 0))
                sp.dma_start(cw[:, :, :], cw_dram[b]).then_inc(cw_ld.sem, 16)
                load13(b * EB)
                load2(b * EB)
                with sp.Fori(0, EB - 1) as n:
                    store_and_load(b, n, True)
                store_and_load(b, EB - 1, False)
                sp.dma_start(fw[:, :, :], fw_dram[b]).then_inc(fw_ld.sem, 16)
                if more:
                    sp.wait_ge(x1_ok.sem, x1_ok.at(b, 4))
                    sp.dma_start(x[:, :, :], x_dram[b + 1]).then_inc(x_ld.sem, 16)
                    attention_operands(b + 1)

            sp.dma_start(x[:, :, :], x_dram[0]).then_inc(x_ld.sem, 16)
            attention_operands(0)
            with sp.Fori(0, B - 1) as b:
                batch(b, True)
            batch(B - 1, False)
            sp.wait_ge(ew13_st.sem, ew13_st.at(B, 0))
            sp.wait_ge(ew2_st.sem, ew2_st.at(B, 0))
            sp.wait_ge(out_st.sem, out_st.at(B, 0))
            sp.wait_ge(x3_st.sem, x3_st.at(B, 0))
            sp.wait_ge(init_st.sem, 16 * 3)
            sp.wait_ge(tb_st.sem, tb_st.at(B, 0))
            sp.wait_ge(r_pos.sem, r_pos.at(B, 0))

        @block.gpsimd
        def _(pool):
            nc.gpsimd.memset(ones32[:, :], 1.0).then_inc(s_one.sem, 1)
            nc.gpsimd.memset(neg_half[:, :], -0.5).then_inc(s_one.sem, 1)
            nc.gpsimd.memset(half[:, :], 0.5).then_inc(s_one.sem, 1)
            nc.gpsimd.memset(eps[:, :], LN_EPS).then_inc(s_one.sem, 1)
            nc.gpsimd.memset(v_hi[:, :, :, :], 1.0).then_inc(s_one.sem, 1)
            nc.gpsimd.memset(onesb[:, :], 1.0).then_inc(s_one.sem, 1)
            nc.gpsimd.memset(zeros[:, :], 0.0).then_inc(s_one.sem, 1)
            for n, s in enumerate(started):
                nc.gpsimd.memset(primer[:, n:n + 1], 0.0).then_inc(s.sem, 1)
            pool.wait_ge(s_one.sem, 7)
            pool.wait_ge(s_const.sem, N_CONST * 16)

            def ln_scale(b, n, sigs):
                _, mean, var, root = sigs
                pool.wait_ge(mean.sem, mean.at(b, n + 1))
                nc.gpsimd.tensor_tensor(ve[:, :], mv[:, :, 1], eps[:, :], ALU.add).then_inc(var.sem, 1)
                pool.wait_ge(var.sem, var.at(b, n + 1))
                nc.gpsimd.tensor_tensor(rstd[:, :], ve[:, :], neg_half[:, :], ALU.pow).then_inc(root.sem, 1)

            def smooth(b, lin):
                n = (KD, 2)[lin]
                pool.wait_ge(qs_rat.sem, qs_rat.at(b, lin + 1))
                nc.gpsimd.tensor_tensor(sq[:, 3, 0:n], sq[:, 2, 0:n], half[:, 0:n], ALU.pow).then_inc(qs_pow.sem, 1)

            def none(a, c):
                return zeros[:, 0:1].unsqueeze(2).to_broadcast([P, a, c])

            def scatter_choices(b, part):
                if part == 0:
                    pool.wait_ge(r_pos.sem, r_pos.at(b, 0))
                    nc.gpsimd.tensor_tensor(idle_p[:, :], eps[:, 0:1], eps[:, 0:1], ALU.add)
                for c in range(KT // 2 * part, KT // 2 * (part + 1)):
                    nc.gpsimd.indirect_dma_start(table, bass.IndirectOffsetOnAxis(ap=pos[:, c:c + 1], axis=0),
                                                 pay[:, c, :], None).then_inc(tb_st.sem, 16)

            pool.wait_ge(init_st.sem, 48)
            ln_scale(0, 0, lna)
            pool.wait_ge(bo_ok.sem, 1)

            def batch(b, more):
                pool.wait_ge(x_ld.sem, x_ld.at(b, 1))
                for t in range(NT):
                    nc.gpsimd.tensor_tensor(x[:, t, :], x[:, t, :], b_o[:, :], ALU.add).then_inc(xbo_ok.sem, 1)

                with pool.Fori(0, EB) as n:
                    pool.wait_ge(ew13_ld.sem, ew13_ld.at(b, 2) + 32 * n)
                    pool.wait_ge(ew13_st.sem, ew13_st.at(b, 0) + 16 * n)
                    pool.wait_ge(x3_st.sem, x3_st.at(b, 0))
                    nc.gpsimd.tensor_tensor(wst13[:, :, 0, :], w13f[:, :, :], none(KD, 2 * F), ALU.add).then_inc(ew_hi.sem, 1)
                    pool.wait_ge(ew_hi.sem, ew_hi.at(b, 1) + 2 * n)
                    nc.gpsimd.tensor_tensor(wst13[:, :, 1, :], w13f[:, :, :], wst13[:, :, 0, :], ALU.subtract).then_inc(ew_lo13.sem, 1)
                    pool.wait_ge(ew2_ld.sem, ew2_ld.at(b, 3) + 48 * n)
                    pool.wait_ge(ew2_st.sem, ew2_st.at(b, 0) + 16 * n)
                    nc.gpsimd.tensor_tensor(wst2[:, :, 0, :], w2f[:, :, :], none(2, D), ALU.add).then_inc(ew_hi.sem, 1)
                    pool.wait_ge(ew_hi.sem, ew_hi.at(b, 2) + 2 * n)
                    nc.gpsimd.tensor_tensor(wst2[:, :, 1, :], w2f[:, :, :], wst2[:, :, 0, :], ALU.subtract).then_inc(ew_lo2.sem, 1)
                if more:
                    ln_scale(b + 1, 0, lna)
                ln_scale(b, 0, ln)
                smooth(b, 0)
                scatter_choices(b, 0)
                smooth(b, 1)
                scatter_choices(b, 1)
                ln_scale(b, 1, ln)
                pool.wait_ge(x3_hi.sem, x3_hi.at(b, 4))
                nc.gpsimd.tensor_tensor(x3[:, :, D:2 * D], xn[:, :, :], x3[:, :, 0:D], ALU.subtract).then_inc(x3_lo.sem, 1)

            with pool.Fori(0, B - 1) as b:
                batch(b, True)
            batch(B - 1, False)

        @block.scalar
        def _(act_e):
            act_e.wait_ge(s_mg.sem, 2)
            for n in range(4):
                act_e.wait_ge(s_wld[n].sem, 16)
                nc.scalar.copy(w_hi[:, n, :, :], (x, x1)[n % 2][:, :, :]).then_inc(s_whi.sem, 1)
            act_e.wait_ge(s_wld[4].sem, 16)
            nc.scalar.copy(g_hi[:, :, :], fw[:, :, 0:E]).then_inc(s_whi.sem, 1)

            def halves_hi(b, first, banks, mm, ok):
                for k in range(KD):
                    act_e.wait_ge(mm.sem, mm.at(b, first + k + 1))
                    nc.scalar.copy(t_hi[:, k, :], bank[banks[k]]).then_inc(ok.sem, 1)

            def fill(items):
                for b, n in items:
                    if n < 8:
                        act_e.wait_ge(qk_mm.sem, qk_mm.at(b, n + 1))
                        nc.scalar.activation(qk_hi[:, n, :], bank[FILL[n % 2]], ACT.Identity, bias=b_qk[:, n:n + 1], scale=1.0).then_inc(qk_hi_ok.sem, 1)
                    else:
                        act_e.wait_ge(v_mm.sem, v_mm.at(b, n - 8 + 1))
                        nc.scalar.copy(v_hi[:, n - 8, :, 0:HD], bank[FILL[n % 2]].rearrange("p (h d) -> p h d", h=H)).then_inc(v_hi_ok.sem, 1)

            def quantise(b, lin, more):
                w = (D, QI)[lin]
                for side, src, dst in ((1, (fw, cw)[lin], wqz), (0, (xn, act)[lin], xq)):
                    n = 8 * lin + 4 * (1 - side)
                    act_e.wait_ge(ri_ok.sem, ri_ok.at(b, 2 * lin + 2 - side))
                    for t in range(4):
                        nc.scalar.activation(src[:, t, 0:w], src[:, t, 0:w], ACT.Identity, bias=magic[:, 0:1],
                                             scale=rinv[:, side, t:t + 1]).then_inc(q1_ok.sem, 1)
                    for t in range(4):
                        act_e.wait_ge(q2_ok.sem, q2_ok.at(b, n + t + 1))
                        nc.scalar.activation(dst[:, t, 0:w], src[:, t, 0:w], ACT.Identity, bias=magic[:, 1:2],
                                             scale=1.0).then_inc(q3_ok.sem, 1)
                    fill(NEXT(b, lin, 2 - side, more))

            def quantT_out(b, lin, side):
                if lin == 0:
                    for half_ in range(2):
                        act_e.wait_ge(qt_mm.sem, qt_mm.at(b, 2 * (1 - side) + half_ + 1))
                        nc.scalar.copy((xqT, wqT)[side][:, 2 * half_:2 * half_ + 2, :],
                                       psb[:, (2, 4)[side] + half_, :].rearrange("p (k c) -> p k c", k=2)).then_inc(qt_ok.sem, 1)
                else:
                    act_e.wait_ge(qt_mm.sem, qt_mm.at(b, 4 + (1 - side) + 1))
                    nc.scalar.copy((xqT, wqT)[side][:, 0:2, :],
                                   psb[:, (2, 3)[side], :].rearrange("p (k c) -> p k c", k=2)).then_inc(qt_ok.sem, 1)

            halves_hi(0, 0, (4, 5, 6, 7), ta_mm, ta_hi_ok)
            fill([(0, n) for n in range(12)])

            def maxima_rows(b):
                for g in range(2):
                    act_e.wait_ge(m_mm.sem, m_mm.at(b, g + 1))
                    nc.scalar.mul(m_row[:, g, :], ps[0:H // 2, 6, :], -1.0).then_inc(m_row_ok.sem, 1)
                    act_e.wait_ge(m_row_ok.sem, m_row_ok.at(b, g + 1))
                    act_e.dma_start(qop[KB:KB + 1, 8 * g:8 * g + 8, :], m_row[:, g, :]).then_inc(m_ld.sem, 16)

            maxima_rows(0)

            def batch(b, more):
                def exponentials(b, hp, first):
                    for i in range(2):
                        if not first:
                            act_e.wait_ge(elo_ok.sem, elo_ok.at(b, i - 1) + 2 * hp)
                        act_e.wait_ge(st_mm.sem, st_mm.at(b, i + 1) + 2 * hp)
                        src = ps[:, 3 * i:3 * i + 3, :].rearrange("p a c -> p (a c)")[:, 0:PCOLS]
                        nc.scalar.activation(p32[:, i, :], src, ACT.Exp, scale=float(SCALE)).then_inc(e32_ok.sem, 1)
                        if not first:
                            act_e.wait_ge(pv_mm.sem, pv_mm.at(b, i - 1) + 2 * hp)
                        nc.scalar.activation(p_hi[:, i, :], src, ACT.Exp, scale=float(SCALE)).then_inc(ehi_ok.sem, 1)
                exponentials(b, 0, True)
                with act_e.Fori(1, PAIRS) as hp:
                    exponentials(b, hp, False)
                halves_hi(b, 0, (0, 1, 2, 3), t_mm, t_hi_ok)
                if more:
                    halves_hi(b + 1, 0, (4, 5, 6, 7), ta_mm, ta_hi_ok)
                act_e.wait_ge(ew13_st.sem, ew13_st.at(b, EB))
                act_e.wait_ge(ew2_st.sem, ew2_st.at(b, EB))
                for lin in range(2):
                    fill(NEXT(b, lin, 0, more))
                    quantise(b, lin, more)
                    quantT_out(b, lin, 1)
                    quantT_out(b, lin, 0)
                    if lin == 0:
                        for t in range(NT):
                            act_e.wait_ge(l_ok.sem, l_ok.at(b, t + 1))
                            nc.scalar.activation(th[:, t, :], o32[:, t, 0:QI], ACT.Tanh, scale=0.5).then_inc(th_ok.sem, 1)
                    fill(NEXT(b, lin, 3, more))
                act_e.wait_ge(x2_ok.sem, x2_ok.at(b, 4))
                act_e.dma_start(o_dram[b], x1[:, :, :]).then_inc(out_st.sem, 16)
                for t in range(NT):
                    act_e.wait_ge(xn_ok.sem, xn_ok.at(b, 4 + t + 1))
                    nc.scalar.copy(x3[:, t, 0:D], xn[:, t, :]).then_inc(x3_hi.sem, 1)
                halves_hi(b, 4, (2, 3, 4, 5), t_mm, t_hi_ok)
                act_e.wait_ge(r_ex.sem, r_ex.at(b, 1))
                nc.scalar.activation(sm[:, :, :], lg[:, :, :], ACT.Exp).then_inc(r_exp.sem, 1)
                act_e.wait_ge(x3_lo.sem, x3_lo.at(b, 1))
                act_e.dma_start(x3_dram[b], x3[:, :, :]).then_inc(x3_st.sem, 16)
                if more:
                    maxima_rows(b + 1)

            with act_e.Fori(0, B - 1) as b:
                batch(b, True)
            batch(B - 1, False)

        @block.vector
        def _(dve):
            nc.vector.memset(magic[:, 0:1], MAGIC).then_inc(s_mg.sem, 1)
            nc.vector.memset(magic[:, 1:2], -MAGIC).then_inc(s_mg.sem, 1)
            dve.wait_ge(s_one.sem, 7)
            def layer_norm(b, n, src, dst, sigs, ok):
                st, mean, _, root = sigs
                for t in range(NT):
                    i = nc.vector.bn_stats(stats[:, t, :], src[:, t, :])
                i.then_inc(st.sem, 1)
                dve.wait_ge(st.sem, st.at(b, n + 1))
                nc.vector.memset(idle[:, :], 0.0)
                for t in range(NT):
                    i = nc.vector.bn_aggr(mv[:, t, :], stats[:, t, :])
                i.then_inc(mean.sem, 1)
                dve.wait_ge(root.sem, root.at(b, n + 1))
                for t in range(NT):
                    nc.vector.tensor_scalar(dst[:, t, :], src[:, t, :], mv[:, t, 0:1], rstd[:, t:t + 1],
                                            ALU.subtract, ALU.mult).then_inc(ok.sem, 1)

            def halves_lo(b, first, banks, hi_ok, ok):
                for k in range(KD):
                    dve.wait_ge(hi_ok.sem, hi_ok.at(b, first + k + 1))
                    nc.vector.tensor_tensor(t_lo[:, k, :], bank[banks[k]], t_hi[:, k, :], ALU.subtract).then_inc(ok.sem, 1)

            def fill(items):
                for b, n in items:
                    if n < 8:
                        dve.wait_ge(qk_hi_ok.sem, qk_hi_ok.at(b, n + 1))
                        nc.vector.scalar_tensor_tensor(out=qk_lo[:, n, :], in0=bank[FILL[n % 2]], scalar=b_qk[:, n:n + 1],
                                                       in1=qk_hi[:, n, :], op0=ALU.add, op1=ALU.subtract).then_inc(qk_lo_ok.sem, 1)
                    else:
                        dve.wait_ge(v_hi_ok.sem, v_hi_ok.at(b, n - 8 + 1))
                        nc.vector.tensor_tensor(v_lo[:, n - 8, :, :], bank[FILL[n % 2]].rearrange("p (h d) -> p h d", h=H),
                                                v_hi[:, n - 8, :, 0:HD], ALU.subtract).then_inc(v_lo_ok.sem, 1)

            def scales(b, lin, more):
                n = (KD, 2)[lin]
                step = [6 * lin]

                def link(i):
                    step[0] += 1
                    i.then_inc(qs_link.sem, 1)
                    dve.wait_ge(qs_link.sem, qs_link.at(b, step[0]))

                for side in (1, 0):
                    for k in range(n):
                        m = 8 * lin + n * (1 - side) + k
                        dve.wait_ge(am_mm.sem, am_mm.at(b, m + 1))
                        nc.vector.tensor_reduce(amax[:, side, k:k + 1], bank[AMAX_BANK[lin][side][k]], AX.X, ALU.max,
                                                apply_absolute_value=True).then_inc(am_ok.sem, 1)
                    if more and lin == 0 and side == 1:
                        halves_lo(b + 1, 0, (4, 5, 6, 7), ta_hi_ok, ta_lo_ok)
                dve.wait_ge(am_ok.sem, am_ok.at(b, 8 + 4 * lin))
                link(nc.vector.tensor_scalar(sq[:, 0:2, 0:n], amax[:, :, 0:n], Q_EPS, None, ALU.max))
                link(nc.vector.reciprocal(sq[:, 1, 0:n], sq[:, 1, 0:n]))
                nc.vector.tensor_tensor(sq[:, 2, 0:n], sq[:, 0, 0:n], sq[:, 1, 0:n], ALU.mult).then_inc(qs_rat.sem, 1)
                dve.wait_ge(qs_pow.sem, qs_pow.at(b, lin + 1))
                link(nc.vector.tensor_scalar(sq[:, 4, 0:n], sq[:, 3, 0:n], Q_EPS, None, ALU.max))
                link(nc.vector.reciprocal(sq[:, 5, 0:n], sq[:, 4, 0:n]))
                for side in (1, 0):
                    for k in range(n):
                        i = nc.vector.tensor_scalar(dg[:, side, k, :], eye32[:, :], sq[:, (5, 4)[side], k:k + 1], None, ALU.mult)
                    i.then_inc(dg_ok.sem, 1)

            def scaled_rows(b, lin, side):
                w = (D, QI)[lin]
                src = ((xn, act), (fw, cw))[side][lin]
                m = 2 * lin + (1 - side)
                dve.wait_ge(bc_mm.sem, bc_mm.at(b, m + 1))
                if side == 1:
                    ld = (fw_ld, cw_ld)[lin]
                    dve.wait_ge(ld.sem, ld.at(b, 1))
                for t in range(4):
                    nc.vector.tensor_tensor(src[:, t, 0:w], src[:, t, 0:w], bank[side][:, 0:w], ALU.mult).then_inc(sc_ok.sem, 1)
                for t in range(4):
                    dve.wait_ge(sc_ok.sem, sc_ok.at(b, 4 * m + t + 1))
                    i = nc.vector.tensor_reduce(rowmax[:, side, t:t + 1], src[:, t, 0:w], AX.X, ALU.max, apply_absolute_value=True)
                i.then_inc(rm_ok.sem, 1)
                dve.wait_ge(rm_ok.sem, rm_ok.at(b, m + 1))
                i = nc.vector.tensor_scalar(rscale[:, side, :], rowmax[:, side, :], Q_EPS, 1.0 / QMAX, ALU.max, ALU.mult)
                i.then_inc(qs_link.sem, 1)
                dve.wait_ge(qs_link.sem, qs_link.at(b, 6 * lin + 4 + (1 - side) + 1))
                nc.vector.reciprocal(rinv[:, side, :], rscale[:, side, :]).then_inc(ri_ok.sem, 1)

            def clip(b, lin, side):
                w = (D, QI)[lin]
                src = ((xn, act), (fw, cw))[side][lin]
                for t in range(4):
                    dve.wait_ge(q1_ok.sem, q1_ok.at(b, 8 * lin + 4 * (1 - side) + t + 1))
                    nc.vector.tensor_scalar(src[:, t, 0:w], src[:, t, 0:w], MAGIC - QMAX, MAGIC + QMAX, ALU.max, ALU.min).then_inc(q2_ok.sem, 1)

            def weight_steps(b, lin):
                for t in range(4):
                    i = nc.vector.tensor_scalar(dg[:, 1, t, :], eye32[:, :], rscale[:, 1, t:t + 1], None, ALU.mult)
                i.then_inc(wd_ok.sem, 1)

            def weight_steps_out(b, lin):
                dve.wait_ge(wd_mm.sem, wd_mm.at(b, lin + 1))
                nc.vector.tensor_copy(wscb[:, :], bank[(1, 4)[lin]]).then_inc(wsb_ok.sem, 1)
                dve.wait_ge(wsb_ok.sem, wsb_ok.at(b, lin + 1))

            def route(b):
                step = [0]

                def link(i):
                    step[0] += 1
                    i.then_inc(r_link.sem, 1)
                    dve.wait_ge(r_link.sem, r_link.at(b, step[0]))

                spread = lambda a: a.unsqueeze(2).to_broadcast([P, NT, E])
                flat = lambda a: a[:, :, :].rearrange("p t e -> p (t e)")
                raw = bank[0][:, 0:NT * E].rearrange("p (t e) -> p t e", t=NT)
                link(nc.vector.tensor_reduce(r4[:, 0, :], raw, AX.X, ALU.max))
                nc.vector.tensor_tensor(lg[:, :, :], raw, spread(r4[:, 0, :]), ALU.subtract).then_inc(r_ex.sem, 1)
                dve.wait_ge(r_exp.sem, r_exp.at(b, 1))
                link(nc.vector.tensor_reduce(r4[:, 1, :], sm[:, :, :], AX.X, ALU.add))
                link(nc.vector.reciprocal(r4[:, 1, :], r4[:, 1, :]))
                nc.vector.tensor_tensor(sm[:, :, :], sm[:, :, :], spread(r4[:, 1, :]), ALU.mult).then_inc(r_rep.sem, 1)
                dve.wait_ge(r_rep.sem, r_rep.at(b, 1))
                nc.vector.memset(idle[:, :], 0.0)
                for t in range(NT):
                    i = nc.vector.max(out=top[:, t, :], in_=sm[:, t, :])
                i.then_inc(r_link.sem, 1)
                step[0] += 1
                dve.wait_ge(r_link.sem, r_link.at(b, step[0]))
                nc.vector.memset(idle[:, :], 0.0)
                for t in range(NT):
                    i = nc.vector.match_replace(out=rep[:, t, :], in_to_replace=top[:, t, :], in_values=sm[:, t, :], imm_value=-1.0)
                link(i)
                nc.vector.tensor_scalar(chosenb[:, :, :], rep[:, :, :], 0.0, None, ALU.is_lt).then_inc(r_mask.sem, 1)
                link(nc.vector.tensor_scalar(chosen[:, :, :], rep[:, :, :], 0.0, None, ALU.is_lt))
                nc.vector.tensor_tensor_scan(nth[:, :], keep[:, :], flat(chosen), 0.0, ALU.mult, ALU.add)
                link(nc.vector.tensor_tensor(gate[:, :, :], sm[:, :, :], chosen[:, :, :], ALU.mult))
                nc.vector.tensor_tensor(nth[:, :], nth[:, :], flat(chosen), ALU.mult)
                link(nc.vector.tensor_reduce(r4[:, 2, :], gate[:, :, :], AX.X, ALU.add))
                link(nc.vector.reciprocal(r4[:, 2, :], r4[:, 2, :]))
                nc.vector.tensor_tensor(gate[:, :, :], gate[:, :, :], spread(r4[:, 2, :]), ALU.mult)
                dve.wait_ge(rk_mm.sem, rk_mm.at(b, 1))
                nc.vector.tensor_tensor(flat(slot), bank[0][:, 128:128 + NT * E], base[:, :], ALU.add).then_inc(r_link.sem, 1)
                dve.wait_ge(r_link.sem, r_link.at(b, ROUTE_LINKS - 5))
                nc.vector.tensor_tensor(slot[:, :, :], slot[:, :, :], counts[:, :].unsqueeze(1).to_broadcast([P, NT, E]), ALU.add).then_inc(r_link.sem, 1)
                dve.wait_ge(r_link.sem, r_link.at(b, ROUTE_LINKS - 4))
                nc.vector.tensor_tensor(counts[:, :], counts[:, :], bank[1][:, 0:E], ALU.add).then_inc(r_read.sem, 1)

            def route_rest(b):
                step = [ROUTE_LINKS - 4]

                def link(i):
                    step[0] += 1
                    i.then_inc(r_link.sem, 1)
                    dve.wait_ge(r_link.sem, r_link.at(b, step[0]))

                flat = lambda a: a[:, :, :].rearrange("p t e -> p (t e)")
                link(nc.vector.tensor_tensor(hit[:, :, :], nth[:, :].unsqueeze(1).to_broadcast([P, TOPK, NT * E]), rank[:, :].unsqueeze(2).to_broadcast([P, TOPK, NT * E]), ALU.is_equal))
                link(nc.vector.tensor_tensor(hit2[:, :, :], hit[:, :, :], flat(slot).unsqueeze(1).to_broadcast([P, TOPK, NT * E]), ALU.mult))
                nc.vector.tensor_reduce(posf[:, :], hit2[:, :, :].rearrange("p k (t e) -> p (k t) e", e=E), AX.X, ALU.add)
                link(nc.vector.tensor_tensor(hit[:, :, :], hit[:, :, :], flat(gate).unsqueeze(1).to_broadcast([P, TOPK, NT * E]), ALU.mult))
                link(nc.vector.tensor_reduce(gatek[:, :], hit[:, :, :].rearrange("p k (t e) -> p (k t) e", e=E), AX.X, ALU.add))
                dve.wait_ge(tb_st.sem, tb_st.at(b, KT))
                nc.vector.tensor_copy(pos[:, :], posf[:, :])
                nc.vector.tensor_copy(pay[:, :, 1].bitcast(F32), gatek[:, :])
                for k in range(TOPK):
                    i = nc.vector.tensor_copy(pay[:, k * NT:(k + 1) * NT, 0], tokf[:, :])
                i.then_inc(r_pos.sem, 1)
                dve.wait_ge(r_pos.sem, r_pos.at(b, 1))
                nc.vector.tensor_scalar(tokf[:, :], tokf[:, :], float(S), None, ALU.add).then_inc(r_tok.sem, 1)

            nc.vector.memset(counts[:, :], 0.0).then_inc(s_mg.sem, 1)
            dve.wait_ge(s_one.sem, 7)
            for n in range(4):
                if n == 2:
                    dve.wait_ge(xa_ld.sem, xa_ld.at(0, 1))
                    layer_norm(0, 0, xa, xa, lna, xa_ok)
                dve.wait_ge(s_whi.sem, n + 1)
                nc.vector.tensor_tensor(w_lo[:, n, :, :], (x, x1)[n % 2][:, :, :], w_hi[:, n, :, :], ALU.subtract).then_inc(s_wlo.sem, 1)
            dve.wait_ge(s_whi.sem, 5)
            nc.vector.tensor_tensor(g_lo[:, :, :], fw[:, :, 0:E], g_hi[:, :, :], ALU.subtract).then_inc(s_wlo.sem, 1)

            halves_lo(0, 0, (4, 5, 6, 7), ta_hi_ok, ta_lo_ok)
            dve.wait_ge(s_const.sem, N_CONST * 16)
            for k in range(KD):
                i = nc.vector.tensor_scalar(dg[:, 0, k, :], ones32[:, :], b_v[:, k:k + 1], None, ALU.mult)
            i.then_inc(bo_dg.sem, 1)
            dve.wait_ge(bo_mm.sem, 1)
            nc.vector.tensor_tensor(b_o[:, :], b_o[:, :], bank[0], ALU.add).then_inc(bo_ok.sem, 1)
            fill([(0, n) for n in range(12)])

            def all_maxima(b):
                with dve.Fori(0, PAIRS) as hp:
                    for u, cuts in enumerate((((3, 0, 512),), ((2, 0, 384), (0, 384, 512)), ((1, 0, 256),))):
                        dve.wait_ge(s_mm.sem, s_mm.at(b, u + 1) + 3 * hp)
                        for t, c0, c1 in cuts:
                            i = nc.vector.tensor_reduce(mx[:, t, bass.ts(hp, 2)], ps[:, 2 * u:2 * u + 2, c0:c1], AX.X, ALU.max)
                        i.then_inc(s_max.sem, 1)

            all_maxima(0)

            def batch(b, more):
                def remainder(b, h, i, first=False):
                    if not first:
                        dve.wait_ge(pv_mm.sem, pv_mm.at(b, -1) + h)
                    dve.wait_ge(ehi_ok.sem, ehi_ok.at(b, 1) + h)
                    nc.vector.tensor_tensor(p_lo[:, i, :], p32[:, i, :], p_hi[:, i, :], ALU.subtract).then_inc(elo_ok.sem, 1)

                def normalised(b, hp, i):
                    dve.wait_ge(pv_mm.sem, pv_mm.at(b, i + 1) + 2 * hp)
                    o = bank[6 + i][:, 0:NT * (HD + 1)].rearrange("p (t c) -> p t c", t=NT)
                    nc.vector.reciprocal(rden[:, i, :], o[:, :, HD]).then_inc(rec_ok.sem, 1)
                    dve.wait_ge(rec_ok.sem, rec_ok.at(b, i + 1) + 2 * hp)
                    dst = o32[:, :, :].rearrange("p t (g i d) -> p t g i d", i=2, d=HD)[:, :, bass.ds(hp, 1), i, :].rearrange("p t a d -> p t (a d)")
                    nc.vector.tensor_tensor(dst, o[:, :, 0:HD],
                                            rden[:, i, :].unsqueeze(2).to_broadcast([P, NT, HD]), ALU.mult).then_inc(norm_ok.sem, 1)

                remainder(b, 0, 0, True)
                remainder(b, 1, 1, True)
                with dve.Fori(0, PAIRS - 1) as hp:
                    normalised(b, hp, 0)
                    remainder(b, 2 * hp + 2, 0)
                    normalised(b, hp, 1)
                    remainder(b, 2 * hp + 3, 1)
                normalised(b, PAIRS - 1, 0)
                normalised(b, PAIRS - 1, 1)
                halves_lo(b, 0, (0, 1, 2, 3), t_hi_ok, t_lo_ok)
                if more:
                    dve.wait_ge(xa_ld.sem, xa_ld.at(b + 1, 1))
                    layer_norm(b + 1, 0, xa, xa, lna, xa_ok)
                dve.wait_ge(out_st.sem, out_st.at(b, 0))
                for t in range(NT):
                    dve.wait_ge(wo_mm.sem, wo_mm.at(b, t + 1))
                    if t == 0:
                        dve.wait_ge(xbo_ok.sem, xbo_ok.at(b, 4))
                    nc.vector.tensor_tensor(x1[:, t, :], bank[4 + t], x[:, t, :], ALU.add).then_inc(x1_ok.sem, 1)
                dve.wait_ge(x1_ok.sem, x1_ok.at(b, 4))
                layer_norm(b, 0, x1, xn, ln, xn_ok)
                for lin in range(2):
                    scales(b, lin, more)
                    scaled_rows(b, lin, 1)
                    fill(NEXT(b, lin, 0, more))
                    scaled_rows(b, lin, 0)
                    clip(b, lin, 1)
                    weight_steps(b, lin)
                    fill(NEXT(b, lin, 1, more))
                    clip(b, lin, 0)
                    fill(NEXT(b, lin, 2, more))
                    weight_steps_out(b, lin)
                    if lin == 0:
                        for t in range(NT):
                            dve.wait_ge(l_mm.sem, l_mm.at(b, t + 1))
                            nc.vector.scalar_tensor_tensor(out=o32[:, t, :], in0=bank[2 + t], scalar=rscale[:, 0, t:t + 1],
                                                           in1=wscb[:, :], op0=ALU.mult, op1=ALU.mult).then_inc(l_ok.sem, 1)
                        for t in range(NT):
                            dve.wait_ge(th_ok.sem, th_ok.at(b, t + 1))
                            nc.vector.scalar_tensor_tensor(out=act[:, t, :], in0=th[:, t, :], scalar=1.0, in1=o32[:, t, 0:QI],
                                                           op0=ALU.add, op1=ALU.mult).then_inc(a1_ok.sem, 1)
                        for t in range(NT):
                            dve.wait_ge(a1_ok.sem, a1_ok.at(b, t + 1))
                            nc.vector.scalar_tensor_tensor(out=act[:, t, :], in0=act[:, t, :], scalar=0.5, in1=o32[:, t, QI:2 * QI],
                                                           op0=ALU.mult, op1=ALU.mult).then_inc(a_ok.sem, 1)
                    else:
                        for t in range(NT):
                            dve.wait_ge(l_mm.sem, l_mm.at(b, 4 + t + 1))
                            nc.vector.scalar_tensor_tensor(out=o32[:, t, :], in0=bank[t], scalar=rscale[:, 0, t:t + 1],
                                                           in1=wscb[:, :], op0=ALU.mult, op1=ALU.mult).then_inc(l_ok.sem, 1)
                        for t in range(NT):
                            dve.wait_ge(l_ok.sem, l_ok.at(b, 4 + t + 1))
                            nc.vector.tensor_tensor(x1[:, t, :], o32[:, t, :], x1[:, t, :], ALU.add).then_inc(x2_ok.sem, 1)
                    fill(NEXT(b, lin, 3, more))
                dve.wait_ge(x2_ok.sem, x2_ok.at(b, 4))
                layer_norm(b, 1, x1, xn, ln, xn_ok)
                halves_lo(b, 4, (2, 3, 4, 5), t_hi_ok, t_lo_ok)
                dve.wait_ge(lg_mm.sem, lg_mm.at(b, 1))
                route(b)
                if more:
                    all_maxima(b + 1)
                route_rest(b)

            with dve.Fori(0, B - 1) as b:
                batch(b, True)
            batch(B - 1, False)

        @block.tensor
        def _(pe):
            pe.wait_ge(s_one.sem, 7)
            pe.wait_ge(s_const.sem, N_CONST * 16)
            def transposes(src, banks, sem):
                for k in range(KD):
                    for t in range(NT):
                        i = nc.tensor.transpose(bank[banks[k]][:, t * P:(t + 1) * P], src[:, t, k * P:(k + 1) * P], eye32[:, :])
                    i.then_inc(sem, 1)

            def three(out_ap, lh, ll, rh, rl):
                n = len(lh)
                for k in range(n):
                    nc.tensor.matmul(out_ap, lh[k], rh[k], start=(k == 0), stop=False)
                    nc.tensor.matmul(out_ap, lh[k], rl[k], start=False, stop=False)
                    i = nc.tensor.matmul(out_ap, ll[k], rh[k], start=False, stop=(k == n - 1))
                return i

            def one_head(operand, rows, h, c0, c1):
                return operand[0:rows, bass.ds(h, 1), c0:c1].rearrange("p a c -> p (a c)")

            def score_maxima(b, hp, first):
                for u, cuts in enumerate((((3, 0),), ((2, 0), (0, 384)), ((1, 0),))):
                    if not first:
                        pe.wait_ge(s_max.sem, s_max.at(b, u - 2) + 3 * hp)
                    for t, c in cuts:
                        for i in range(2):
                            o = ps[:, 2 * u + i, c:c + (t + 1) * P]
                            nc.tensor.matmul(o, one_head(qop, KB, 2 * hp + i, t * P, (t + 1) * P),
                                             one_head(kop, KB, 2 * hp + i, 0, (t + 1) * P), start=True, stop=False)
                            n = nc.tensor.matmul(o[:, t * P:(t + 1) * P], eyeb[:, :], mask_qk[:, :], start=False, stop=True)
                    n.then_inc(s_mm.sem, 1)

            def scores_T(b, h, i, first=False):
                if not first:
                    pe.wait_ge(ehi_ok.sem, ehi_ok.at(b, -1) + h)
                for j in range(NT):
                    bk_, c = divmod(POFF[j], 512)
                    o = ps[:, 3 * i + bk_, c:c + S - j * P]
                    nc.tensor.matmul(o, one_head(kop, KM, h, j * P, (j + 1) * P), one_head(qop, KM, h, j * P, S), start=True, stop=False)
                    n = nc.tensor.matmul(o[:, 0:P], eyeb[:, :], mask_kq[:, :], start=False, stop=True)
                n.then_inc(st_mm.sem, 1)

            def values(b, h, i, first=False):
                pe.wait_ge(elo_ok.sem, elo_ok.at(b, 1) + h)
                if not first:
                    pe.wait_ge(norm_ok.sem, norm_ok.at(b, -1) + h)
                for t in range(NT):
                    o = bank[6 + i][:, t * (HD + 1):(t + 1) * (HD + 1)]
                    for j in range(t + 1):
                        c = POFF[j] + (t - j) * P
                        vh = v_hi[:, j, bass.ds(h, 1), :].rearrange("p a c -> p (a c)")
                        vl = v_lo[:, j, bass.ds(h, 1), :].rearrange("p a c -> p (a c)")
                        nc.tensor.matmul(o, p_hi[:, i, c:c + P], vh, start=(j == 0), stop=False)
                        nc.tensor.matmul(o[:, 0:HD], p_hi[:, i, c:c + P], vl, start=False, stop=False)
                        n = nc.tensor.matmul(o, p_lo[:, i, c:c + P], vh, start=False, stop=(j == t))
                n.then_inc(pv_mm.sem, 1)

            def normed_columns(b):
                pe.wait_ge(xa_ok.sem, xa_ok.at(b, 4))
                transposes(xa, (4, 5, 6, 7), ta_mm.sem)

            def fill(items):
                for b, n in items:
                    out_ap = bank[FILL[n % 2]]
                    if n < 2:
                        pe.wait_ge(ta_lo_ok.sem, ta_lo_ok.at(b, 4))
                    elif n < 10:
                        pe.wait_ge(qk_lo_ok.sem, qk_lo_ok.at(b, n - 1))
                    else:
                        pe.wait_ge(v_lo_ok.sem, v_lo_ok.at(b, n - 9))
                    if n < 8:
                        w, g = divmod(n, 4)
                        three(out_ap, tiles(w_hi[:, w], g), tiles(w_lo[:, w], g), cols(t_hi), cols(t_lo)).then_inc(qk_mm.sem, 1)
                    else:
                        three(out_ap, tiles(t_hi, n - 8), tiles(t_lo, n - 8), cols(w_hi[:, 2]), cols(w_lo[:, 2])).then_inc(v_mm.sem, 1)

            def quantised(b, lin, more):
                n = (KD, 2)[lin]
                if lin == 1:
                    pe.wait_ge(l_ok.sem, l_ok.at(b, 1))
                for side, src in ((1, (fw, cw)[lin]), (0, (xn, act)[lin])):
                    if side == 1:
                        ld = (fw_ld, cw_ld)[lin]
                        pe.wait_ge(ld.sem, ld.at(b, 1))
                    elif lin == 0:
                        if more:
                            pe.wait_ge(x1_ok.sem, x1_ok.at(b, 4))
                            normed_columns(b + 1)
                        pe.wait_ge(xn_ok.sem, xn_ok.at(b, 4))
                    else:
                        pe.wait_ge(a_ok.sem, a_ok.at(b, 4))
                    for k in range(n):
                        bk_ = AMAX_BANK[lin][side][k]
                        if lin == 0 and side == 0:
                            pe.wait_ge(am_ok.sem, am_ok.at(b, k + 1))
                        for t in range(4):
                            i = nc.tensor.transpose(bank[bk_][:, t * P:(t + 1) * P], src[:, t, k * P:(k + 1) * P], eye32[:, :])
                        i.then_inc(am_mm.sem, 1)
                for m, side in enumerate((1, 0)):
                    pe.wait_ge(dg_ok.sem, dg_ok.at(b, 2 * lin + m + 1))
                    for k in range(n):
                        i = nc.tensor.matmul(bank[side][:, k * P:(k + 1) * P], ones32[:, :], dg[:, side, k, :],
                                             start=True, stop=True)
                    i.then_inc(bc_mm.sem, 1)
                fill(NEXT(b, lin, 0, more))
                fill(NEXT(b, lin, 1, more))
                for m, (side, src) in enumerate(((1, wqz), (0, xq))):
                    pe.wait_ge(q3_ok.sem, q3_ok.at(b, 8 * lin + 4 * m + 4))
                    for k in range(n):
                        bk_ = (((2, 4)[side] + k // 2), (2, 3)[side])[lin]
                        for t in range(4):
                            c = (k % 2) * 512 + t * P
                            i = nc.tensor.transpose(psb[:, bk_, c:c + P], src[:, t, k * P:(k + 1) * P], eyeb[:, :])
                        if k % 2 == 1:
                            i.then_inc(qt_mm.sem, 1)
                    if side == 1:
                        fill(NEXT(b, lin, 2, more))
                pe.wait_ge(wd_ok.sem, wd_ok.at(b, lin + 1))
                for t in range(4):
                    i = nc.tensor.matmul(bank[(1, 4)[lin]][:, t * P:(t + 1) * P], ones32[:, :], dg[:, 1, t, :], start=True, stop=True)
                i.then_inc(wd_mm.sem, 1)
                pe.wait_ge(qt_ok.sem, qt_ok.at(b, (4, 6)[lin]))
                for t in range(NT):
                    for k in range(n):
                        i = nc.tensor.matmul(bank[(2, 0)[lin] + t], xqT[:, k, t * P:(t + 1) * P], wqT[:, k, :], start=(k == 0), stop=(k == n - 1))
                    i.then_inc(l_mm.sem, 1)
                fill(NEXT(b, lin, 3, more))

            tiles = lambda a, t: [a[:, k, t * P:(t + 1) * P] for k in range(KD)]
            cols = lambda a: [a[:, k, :] for k in range(KD)]
            normed_columns(0)
            pe.wait_ge(s_wlo.sem, 5)
            pe.wait_ge(bo_dg.sem, 1)
            for k in range(KD):
                i = nc.tensor.matmul(bank[0], dg[:, 0, k, :], x1[:, k, :], start=(k == 0), stop=(k == KD - 1))
            i.then_inc(bo_mm.sem, 1)
            fill([(0, n) for n in range(12)])

            def all_maxima(b):
                pe.wait_ge(v_lo_ok.sem, v_lo_ok.at(b, 4))
                pe.wait_ge(r_read.sem, r_read.at(b, 0))
                pe.wait_ge(op_ld.sem, op_ld.at(b, 24))
                for g in range(2):
                    if g == 0:
                        score_maxima(b, 0, True)
                    with pe.Fori((1, 4)[g], (4, 8)[g]) as hp:
                        score_maxima(b, hp, False)
                    pe.wait_ge(s_max.sem, s_max.at(b, 12 * g + 12))
                    if g == 1:
                        pe.wait_ge(m_row_ok.sem, m_row_ok.at(b, 1))
                    for t in range(NT):
                        n = nc.tensor.transpose(ps[0:H // 2, 6, t * P:(t + 1) * P], mx[:, t, 8 * g:8 * g + 8], eye32[:, :])
                    n.then_inc(m_mm.sem, 1)

            all_maxima(0)

            def batch(b, more):
                pe.wait_ge(m_ld.sem, m_ld.at(b, 2))
                scores_T(b, 0, 0, True)
                scores_T(b, 1, 1, True)
                for h in range(2):
                    scores_T(b, h + 2, h)
                    values(b, h, h, True)
                with pe.Fori(1, PAIRS - 1) as hp:
                    for i in range(2):
                        scores_T(b, 2 * hp + i + 2, i)
                        values(b, 2 * hp + i, i)
                for i in range(2):
                    values(b, H - 2 + i, i)
                pe.wait_ge(norm_ok.sem, norm_ok.at(b, H))
                transposes(o32, (0, 1, 2, 3), t_mm.sem)
                pe.wait_ge(t_lo_ok.sem, t_lo_ok.at(b, 4))
                for t in range(NT):
                    three(bank[4 + t], tiles(t_hi, t), tiles(t_lo, t), cols(w_hi[:, 3]), cols(w_lo[:, 3])).then_inc(wo_mm.sem, 1)
                quantised(b, 0, more)
                quantised(b, 1, more)
                pe.wait_ge(xn_ok.sem, xn_ok.at(b, 8))
                transposes(xn, (2, 3, 4, 5), t_mm.sem)
                pe.wait_ge(t_lo_ok.sem, t_lo_ok.at(b, 8))
                for t in range(NT):
                    n = three(bank[0][:, t * E:(t + 1) * E], tiles(t_hi, t), tiles(t_lo, t), cols(g_hi), cols(g_lo))
                n.then_inc(lg_mm.sem, 1)
                pe.wait_ge(r_mask.sem, r_mask.at(b, 1))
                for t in range(NT):
                    for u in range(t + 1):
                        nc.tensor.matmul(bank[0][:, 128 + t * E:128 + (t + 1) * E], (onesb, before)[u == t][:, :], chosenb[:, u, :],
                                         start=(u == 0), stop=(u == t))
                for t in range(NT):
                    n = nc.tensor.matmul(bank[1][:, 0:E], onesb[:, :], chosenb[:, t, :], start=(t == 0), stop=(t == NT - 1))
                n.then_inc(rk_mm.sem, 1)
                if more:
                    all_maxima(b + 1)

            with pe.Fori(0, B - 1) as b:
                batch(b, True)
            batch(B - 1, False)


def expert_part(nc, w1, v1, w2, eye32_c, eye16_c, tile_c, counts, pos, pay, split_w, x3_rows, table, out):
    with ExitStack() as ctx:
        def sb(name, shape, dt):
            return ctx.enter_context(nc.sbuf_tensor(name, shape, dt))

        def sem(name):
            return ctx.enter_context(nc.semaphore(name))

        ps = ctx.enter_context(nc.psum_tensor("ps2", [P, 8, 512], F32))
        ps16 = ps[:, :, :].bitcast(F16)
        XT, GU, HT, Y = 0, 2, 4, 6
        AHEAD = 8
        WAITING = 8
        RING = 4
        PIECES = 8
        LOADED = 16 * PIECES
        PLACE = 4096
        COLS = 2 * P

        eye32, eye16, tile_no = sb("eye32b", [P, P], F32), sb("eye16b", [P, P], F16), sb("tile_no", [P, 2], F32)
        need, first, le, row1 = sb("need", [P, E], F32), sb("first", [P, E], F32), sb("le", [P, 2, E], F32), sb("row1", [P, E], F32)
        first_i = sb("first_i", [P, E], I32)
        own = sb("own", [P, 4, 2], F32)
        block_i = sb("block_i", [P, 2], I32)
        lists = sb("lists", [P, 2, P, 2], I32)
        listf = sb("listf", [P, 2, P], F32)
        tokens = sb("tokens", [P, COLS], I32)
        gates = sb("gates", [P, COLS], F32)
        weight_no = sb("weight_no", [1, COLS], I32)
        SLOT = WC + W2C
        wbuf = sb("wbuf", [P, (RING + LATE) * SLOT], F16)
        xg = sb("xg", [P, AHEAD, 2 * D], F16)
        xT = sb("xT", [P, 2, 2 * D], F16)
        idx_g, idx_s, gcol = sb("idx_g", [P, AHEAD], I32), sb("idx_s", [P, WAITING], I32), sb("gcol", [P, WAITING], F32)
        th, h1, h = sb("th2", [P, 2, F], F32), sb("h1", [P, 2, F], F32), sb("h", [P, 2, F], F32)
        hs = sb("hs", [P, 2, 2 * F], F16)
        hT = sb("hT", [P, 2, 2 * F], F16)
        y = sb("y", [P, WAITING, D], F32)
        idle_p, idle_q, idle_v, pacer = sb("idle_p2", [P, 1], F32), sb("idle_q", [P, 1], F32), sb("idle_v", [P, 1], F32), sb("pacer", [P, 1], F32)

        s_in, s_plan, s_blk, s_list = sem("s_in"), sem("s_plan"), sem("s_blk"), sem("s_list")
        s_lt, s_tr, s_ready = sem("s_lt"), sem("s_tr"), sem("s_ready")
        idx_ok, g_done, xt_mm, xt_ok = sem("idx_ok"), [sem(f"g_done{q}") for q in range(AHEAD)], sem("xt_mm"), sem("xt_ok")
        gu_mm, th_ok, h1_ok, h_ok = sem("gu_mm"), sem("th2_ok"), sem("h1_ok"), sem("h_ok")
        hh_ok, hl_ok, ht_mm, ht_ok = sem("hh_ok"), sem("hl_ok"), sem("ht_mm"), sem("ht_ok")
        y_mm, y_ok = sem("y_mm"), sem("y_ok")
        acc_st, w_ld, s_idle = sem("acc_st"), sem("w_ld"), sem("s_idle")
        s_pace = sem("s_pace")
        late = sb("late", [P, 2, KD * 2 * F + 2 * D], F32)
        l13, l2 = late[:, :, 0:KD * 2 * F], late[:, :, KD * 2 * F:]
        late_slot = [wbuf[:, (RING + n) * SLOT:(RING + n + 1) * SLOT] for n in range(LATE)]
        late13 = [w[:, 0:WC].rearrange("p (k s f) -> p k s f", k=KD, s=2) for w in late_slot]
        late2 = [w[:, WC:SLOT].rearrange("p (a s d) -> p a s d", a=2, s=2) for w in late_slot]
        late_ld = [sem(f"late_ld{q}") for q in range(2)]
        late_hi, late_lo, s_scat = sem("late_hi"), sem("late_lo"), sem("s_scat")

        block = ctx.enter_context(nc.Block())

        @block.sync
        def _(sp):
            sp.dma_start(eye32[:, :], eye32_c).then_inc(s_in, 16)
            sp.dma_start(eye16[:, :], eye16_c).then_inc(s_in, 16)
            sp.dma_start(tile_no[:, :], tile_c).then_inc(s_in, 16)

            def load_weights(e, side):
                step = SLOT // PIECES
                for c in range(0, SLOT, step):
                    sp.dma_start(wbuf[:, side * SLOT + c:side * SLOT + c + step], split_w[e][:, c:c + step]).then_inc(w_ld, 16)

            load_weights(0, 1)
            sp.wait_ge(w_ld, LOADED)
            load_weights(1, 2)
            sp.wait_ge(w_ld, 2 * LOADED)

            def load_late(n):
                e, q = B * EB + n, n % 2
                for a, w in enumerate((w1, v1)):
                    sp.dma_start(l13[:, q, :].rearrange("p (k f) -> p k f", k=KD)[:, :, a * F:(a + 1) * F],
                                 w.rearrange("e (k p) f -> e p k f", p=P)[e]).then_inc(late_ld[q], 16)
                sp.dma_start(l2[:, q, 0:D], w2[e, 0:P, :]).then_inc(late_ld[q], 16)
                for side in range(2):
                    sp.dma_start(l2[64 * side:64 * side + 64, q, D:2 * D], w2[e, P:F, :]).then_inc(late_ld[q], 16)

            load_late(0)
            load_late(1)
            for n in range(LATE - 2):
                sp.wait_ge(late_lo, n + 1)
                load_late(n + 2)
            load_weights(2, 3)
            sp.wait_ge(w_ld, 3 * LOADED)
            load_weights(3, 0)
            sp.wait_ge(w_ld, 4 * LOADED)
            sp.wait_ge(s_ready, 1)
            with sp.Fori(1, B * EB // RING) as n:
                for side in range(RING):
                    done = sp.value_load(first_i[0:1, bass.ds(RING * n + side - RING + 1, 1)], min_val=0, max_val=TILES)
                    sp.wait_ge(y_mm, done)
                    load_weights(RING * n + side, (side + 1) % RING)
                    sp.wait_ge(w_ld, RING * LOADED * n + LOADED * (side + 1))
                    sp.dma_start(pacer[0:1, 0:1], eye32_c[0:1, 0:1]).then_inc(s_pace, 16)
            sp.wait_ge(s_pace, 16 * (B * EB - RING))
            sp.wait_ge(acc_st, 16 * TILES)

        @block.gpsimd
        def _(pool):
            for c in range(KT):
                nc.gpsimd.indirect_dma_start(table, bass.IndirectOffsetOnAxis(ap=pos[:, c:c + 1], axis=0),
                                             pay[:, c, :], None).then_inc(s_scat, 16)
            pool.wait_ge(s_scat, 16 * KT)
            pool.wait_ge(s_blk, 1)
            for c in range(2):
                n = (P, TILES - P)[c]
                nc.gpsimd.indirect_dma_start(lists[0:n, c, :, :].rearrange("p s a -> p (s a)"), None,
                                             table.rearrange("(t s) a -> t (s a)", s=P),
                                             bass.IndirectOffsetOnAxis(ap=block_i[0:n, c:c + 1], axis=0)).then_inc(s_list, 16)

            nc.gpsimd.memset(idle_p[:, :], 0.0).then_inc(s_idle, 1)
            pool.wait_ge(s_idle, 1)

            def carry(n):
                pool.wait_ge(s_idle, n)
                nc.gpsimd.tensor_tensor(idle_q[:, :], idle_p[:, :], idle_p[:, :], ALU.add).then_inc(s_idle, 1)

            def gather(i, q, n):
                pool.wait_ge(idx_ok, i + 1)
                carry(n)
                nc.gpsimd.indirect_dma_start(xg[:, q, :], None, x3_rows,
                                             bass.IndirectOffsetOnAxis(ap=idx_g[:, q:q + 1], axis=0)).then_inc(g_done[q], 16)

            def scatter(i, r, n, first=False):
                pool.wait_ge(y_ok, i + 1)
                carry(n)
                if not first:
                    pool.wait_ge(acc_st, 16 * i)
                carry(n + 1)
                nc.gpsimd.indirect_dma_start(out, bass.IndirectOffsetOnAxis(ap=idx_s[:, r:r + 1], axis=0),
                                             y[:, r, :], None, compute_op=ALU.add).then_inc(acc_st, 16)

            for q in range(AHEAD):
                gather(q, q, q + 1)
            first_n = AHEAD + 1
            for q in range(AHEAD):
                gather(q + AHEAD, q, first_n + 3 * q)
                scatter(q, q % WAITING, first_n + 3 * q + 1, q == 0)
            with pool.Fori(1, TILES // AHEAD - 1) as j:
                for q in range(AHEAD):
                    i = AHEAD * j + q
                    gather(i + AHEAD, q, 3 * i + first_n)
                    scatter(i, q % WAITING, 3 * i + first_n + 1)
            for q in range(AHEAD):
                i = TILES - AHEAD + q
                scatter(i, q % WAITING, 3 * (TILES - AHEAD) + first_n + 2 * q)

        @block.scalar
        def _(act_e):
            def gate_tanh(i, p):
                act_e.wait_ge(gu_mm, i + 1)
                nc.scalar.activation(th[:, p, :], ps[:, GU + p, 0:F], ACT.Tanh, scale=0.5).then_inc(th_ok, 1)

            def h_rounded(i, p, first=False):
                act_e.wait_ge(h_ok, i + 1)
                if not first:
                    act_e.wait_ge(ht_mm, i - 1)
                nc.scalar.copy(hs[:, p, 0:F], h[:, p, :]).then_inc(hh_ok, 1)

            def hT_out(i, p, first=False):
                act_e.wait_ge(ht_mm, i + 1)
                if not first:
                    act_e.wait_ge(y_mm, i - 1)
                nc.scalar.copy(hT[:, p, :], ps16[:, HT + p, 0:2 * F]).then_inc(ht_ok, 1)

            def y_out(i, r):
                act_e.wait_ge(y_mm, i + 1)
                nc.scalar.activation(y[:, r, :], ps[:, Y + r % 2, :], ACT.Copy, scale=gcol[:, r:r + 1]).then_inc(y_ok, 1)

            def step(i, r, first=False, more=True, before=True):
                p = r % 2
                if more:
                    gate_tanh(i + 1, 1 - p)
                hT_out(i, p, first)
                if more:
                    h_rounded(i + 1, 1 - p, first and r == 0)
                if before:
                    y_out(i - 1, (r - 1) % WAITING)

            for n in range(LATE):
                q = n % 2
                act_e.wait_ge(late_ld[q], 80 * (n // 2 + 1))
                nc.scalar.copy(late13[n][:, :, 0, :], l13[:, q, :].rearrange("p (k f) -> p k f", k=KD)).then_inc(late_hi, 1)
                nc.scalar.copy(late2[n][:, :, 0, :], l2[:, q, :].rearrange("p (a d) -> p a d", a=2)).then_inc(late_hi, 1)
            gate_tanh(0, 0)
            h_rounded(0, 0, True)
            for r in range(WAITING):
                step(r, r, first=r < 2, before=r > 0)
            with act_e.Fori(1, TILES // WAITING - 1) as j:
                for r in range(WAITING):
                    step(WAITING * j + r, r)
            for r in range(WAITING):
                step(TILES - WAITING + r, r, more=r < WAITING - 1)
            y_out(TILES - 1, WAITING - 1)

        @block.vector
        def _(dve):
            count = [0]

            def link(i):
                count[0] += 1
                i.then_inc(s_plan, 1)
                dve.wait_ge(s_plan, count[0])

            link(nc.vector.tensor_scalar(need[:, :], counts[:, :], 1.0 / P, (P - 1.0) / P - 0.5 + 0.5 / P, ALU.mult, ALU.add))
            link(nc.vector.tensor_scalar(need[:, :], need[:, :], MAGIC, MAGIC, ALU.add, ALU.subtract))
            link(nc.vector.tensor_scalar(need[:, :], need[:, :], 1.0, None, ALU.max))
            link(nc.vector.memset(row1[:, :], 1.0))
            link(nc.vector.tensor_tensor_scan(first[:, :], row1[:, :], need[:, :], 0.0, ALU.mult, ALU.add))
            link(nc.vector.tensor_tensor(first[:, :], first[:, :], need[:, :], ALU.subtract))
            link(nc.vector.tensor_copy(first_i[:, :], first[:, :]))
            dve.wait_ge(s_in, 48)
            for c in range(2):
                link(nc.vector.tensor_scalar(le[:, c, :], first[:, :], tile_no[:, c:c + 1], None, ALU.is_le))
            link(nc.vector.tensor_reduce(own[:, 0, :], le[:, :, :], AX.X, ALU.add))
            for c in range(2):
                link(nc.vector.tensor_tensor(le[:, c, :], le[:, c, :], first[:, :], ALU.mult))
            link(nc.vector.tensor_reduce(own[:, 1, :], le[:, :, :], AX.X, ALU.max))
            link(nc.vector.tensor_scalar(own[:, 2, :], own[:, 0, :], -1.0, float(BLOCKS), ALU.add, ALU.mult))
            link(nc.vector.tensor_tensor(own[:, 2, :], own[:, 2, :], own[:, 1, :], ALU.subtract))
            link(nc.vector.tensor_tensor(own[:, 2, :], own[:, 2, :], tile_no[:, :], ALU.add))
            nc.vector.tensor_copy(block_i[:, :], own[:, 2, :]).then_inc(s_blk, 1)
            link(nc.vector.tensor_scalar(own[:, 1, :], own[:, 0, :], float(B * EB), None, ALU.min))
            link(nc.vector.tensor_scalar(own[:, 3, :], own[:, 1, :], 1.0 / RING, 0.5 / RING - 0.5, ALU.mult, ALU.add))
            link(nc.vector.tensor_scalar(own[:, 3, :], own[:, 3, :], MAGIC, MAGIC, ALU.add, ALU.subtract))
            link(nc.vector.tensor_scalar(own[:, 3, :], own[:, 3, :], -float(RING), None, ALU.mult))
            link(nc.vector.tensor_tensor(own[:, 3, :], own[:, 3, :], own[:, 1, :], ALU.add))
            link(nc.vector.tensor_scalar(own[:, 0, :], own[:, 0, :], -float(B * EB), 0.0, ALU.add, ALU.max))
            link(nc.vector.tensor_tensor(own[:, 3, :], own[:, 3, :], own[:, 0, :], ALU.add))
            link(nc.vector.tensor_scalar(own[:, 0, :], own[:, 0, :], 1.0, RING - 1.0, ALU.min, ALU.mult))
            link(nc.vector.tensor_tensor(own[:, 3, :], own[:, 3, :], own[:, 0, :], ALU.add))
            link(nc.vector.tensor_scalar(own[:, 3, :], own[:, 3, :], float(PLACE), None, ALU.mult))
            link(nc.vector.tensor_scalar(own[:, 1, :], own[:, 1, :], float(LOADED), None, ALU.mult))
            link(nc.vector.tensor_tensor(own[:, 1, :], own[:, 1, :], own[:, 3, :], ALU.add))
            nc.vector.memset(listf[:, :, :], 0.0)
            link(nc.vector.memset(tokens[:, :], 0))
            for n in range(LATE):
                q = n % 2
                dve.wait_ge(late_hi, 2 * n + 1)
                nc.vector.tensor_tensor(late13[n][:, :, 1, :], l13[:, q, :].rearrange("p (k f) -> p k f", k=KD), late13[n][:, :, 0, :], ALU.subtract)
                dve.wait_ge(late_hi, 2 * n + 2)
                nc.vector.tensor_tensor(late2[n][:, :, 1, :], l2[:, q, :].rearrange("p (a d) -> p a d", a=2), late2[n][:, :, 0, :],
                                        ALU.subtract).then_inc(late_lo, 1)
            dve.wait_ge(s_list, 32)
            for c in range(2):
                n = (P, TILES - P)[c]
                i = nc.vector.tensor_copy(listf[0:n, c, :], lists[0:n, c, :, 0])
            i.then_inc(s_lt, 1)
            dve.wait_ge(s_tr, 1)
            nc.vector.tensor_copy(tokens[:, 0:TILES], ps[:, 0, 0:TILES])
            nc.vector.tensor_copy(gates[:, 0:TILES], ps[:, 1, 0:TILES])
            nc.vector.tensor_copy(weight_no[:, :], ps[0:1, 3, 0:COLS]).then_inc(s_ready, 1)
            dve.wait_ge(s_ready, 1)

            def index_gather(i, q, first=False):
                if not first:
                    dve.wait_ge(g_done[q], 16 // AHEAD * (i - q))
                nc.vector.tensor_copy(idx_g[:, q:q + 1], tokens[:, bass.ds(i, 1)]).then_inc(idx_ok, 1)

            def x_out(i, p):
                dve.wait_ge(xt_mm, i + 1)
                nc.vector.tensor_copy(xT[:, p, :], ps16[:, XT + p, :]).then_inc(xt_ok, 1)

            def hidden(i, p):
                dve.wait_ge(th_ok, i + 1)
                nc.vector.scalar_tensor_tensor(out=h1[:, p, :], in0=th[:, p, :], scalar=1.0, in1=ps[:, GU + p, 0:F],
                                               op0=ALU.add, op1=ALU.mult).then_inc(h1_ok, 1)
                dve.wait_ge(h1_ok, i + 1)
                nc.vector.scalar_tensor_tensor(out=h[:, p, :], in0=h1[:, p, :], scalar=0.5, in1=ps[:, GU + p, F:2 * F],
                                               op0=ALU.mult, op1=ALU.mult).then_inc(h_ok, 1)

            def h_remainder(i, r, first=False):
                p = r % 2
                if not first:
                    dve.wait_ge(acc_st, 16 * (i - WAITING + 1))
                    nc.vector.memset(idle_v[:, :], 0.0)
                nc.vector.tensor_copy(idx_s[:, r:r + 1], tokens[:, bass.ds(i, 1)])
                nc.vector.tensor_copy(gcol[:, r:r + 1], gates[:, bass.ds(i, 1)])
                dve.wait_ge(hh_ok, i + 1)
                nc.vector.tensor_tensor(hs[:, p, F:2 * P], h[:, p, P:F], hs[:, p, P:F], ALU.subtract)
                nc.vector.tensor_tensor(hs[:, p, 2 * P:2 * F], h[:, p, 0:P], hs[:, p, 0:P], ALU.subtract).then_inc(hl_ok, 1)

            def step(i, q, first=False, gathers=True, more=2):
                if gathers:
                    index_gather(i + AHEAD, q)
                if more > 1:
                    x_out(i + 2, q % 2)
                if more > 0:
                    hidden(i + 1, (q + 1) % 2)
                    h_remainder(i + 1, (q + 1) % WAITING, first)

            for q in range(AHEAD):
                index_gather(q, q, True)
            for q in range(2):
                x_out(q, q)
            hidden(0, 0)
            h_remainder(0, 0, True)
            for q in range(AHEAD):
                step(q, q, first=q + 1 < WAITING)
            with dve.Fori(1, TILES // AHEAD - 1) as j:
                for q in range(AHEAD):
                    step(AHEAD * j + q, q)
            for q in range(AHEAD):
                step(TILES - AHEAD + q, q, gathers=False, more=AHEAD - 1 - q)

        @block.tensor
        def _(pe):
            pe.wait_ge(s_in, 48)
            pe.wait_ge(s_lt, 1)
            for c in range(2):
                n = (P, TILES - P)[c]
                nc.tensor.transpose(ps[:, 0, c * P:c * P + n], listf[0:n, c, :], eye32[0:n, 0:n])
                nc.tensor.transpose(ps[:, 1, c * P:c * P + n], lists[0:n, c, :, 1].bitcast(F32), eye32[0:n, 0:n])
                m = nc.tensor.transpose(ps[0:1, 3, c * P:(c + 1) * P], own[:, 1, c:c + 1], eye32[:, :])
            m.then_inc(s_tr, 1)
            pe.wait_ge(s_ready, 1)
            pe.wait_ge(late_lo, LATE)

            def x_in(i, q, first=False):
                p = q % 2
                pe.wait_ge(g_done[q], 16 // AHEAD * (i - q) + 16)
                if not first:
                    pe.wait_ge(xt_ok, i - 1)
                for k in range(2 * KD):
                    n = nc.tensor.transpose(ps16[:, XT + p, k * P:(k + 1) * P], xg[:, q, k * P:(k + 1) * P], eye16[:, :])
                n.then_inc(xt_mm, 1)

            def weights(i):
                v = pe.value_load(weight_no[0:1, bass.ds(i, 1)], min_val=LOADED, max_val=PLACE * (RING + LATE))
                return (v % PLACE).with_bounds(min_val=LOADED, max_val=LOADED * B * EB), ((v >> 12) * SLOT).with_bounds(min_val=0, max_val=(RING - 1 + LATE) * SLOT)

            def before_up(i, loaded):
                pe.wait_ge(w_ld, loaded)
                pe.wait_ge(xt_ok, i + 1)

            def up(i, p, at, first=False):
                if not first:
                    pe.wait_ge(h_ok, i - 1)
                o = ps[:, GU + p, 0:2 * F]
                for k in range(KD):
                    hi, lo = xT[:, p, k * P:(k + 1) * P], xT[:, p, (KD + k) * P:(KD + k + 1) * P]
                    w_hi = wbuf[:, bass.ds(at + k * 4 * F, 2 * F)]
                    w_lo = wbuf[:, bass.ds(at + k * 4 * F + 2 * F, 2 * F)]
                    nc.tensor.matmul(o, hi, w_hi, start=(k == 0), stop=False)
                    nc.tensor.matmul(o, hi, w_lo, start=False, stop=False)
                    n = nc.tensor.matmul(o, lo, w_hi, start=False, stop=(k == KD - 1))
                n.then_inc(gu_mm, 1)

            def turn(i, p, first=False):
                pe.wait_ge(hl_ok, i + 1)
                if not first:
                    pe.wait_ge(ht_ok, i - 1)
                for c in range(0, 2 * F, P):
                    n = nc.tensor.transpose(ps16[:, HT + p, c:c + P], hs[:, p, c:c + P], eye16[:, :])
                n.then_inc(ht_mm, 1)

            def down(i, p, at, first=False):
                pe.wait_ge(ht_ok, i + 1)
                if not first:
                    pe.wait_ge(y_ok, i - 1)
                w = [wbuf[:, bass.ds(at + WC + a * D, D)] for a in range(3)]
                w_end_lo = wbuf[0:F - P, bass.ds(at + WC + 3 * D, D)]
                hi, ends, lo = (hT[:, p, c:c + P] for c in range(0, 2 * F, P))
                for n, (l, r) in enumerate(((hi, w[0]), (hi, w[1]), (lo, w[0]), (ends, w[2]), (ends[0:F - P], w_end_lo))):
                    m = nc.tensor.matmul(ps[:, Y + p, :], l, r, start=(n == 0), stop=(n == 4))
                m.then_inc(y_mm, 1)

            def step(i, q, at_before, at, first=False, more=2):
                at_next = None
                if more > 0:
                    loaded, at_next = weights(i + 1)
                    before_up(i + 1, loaded)
                if more > 1:
                    x_in(i + 2, (q + 2) % AHEAD)
                if more > 0:
                    up(i + 1, (q + 1) % 2, at_next, first and q == 0)
                turn(i, q % 2, first and q < 2)
                if not (first and q == 0):
                    down(i - 1, (q - 1) % 2, at_before, first and q < 3)
                return at, at_next

            x_in(0, 0, True)
            x_in(1, 1, True)
            loaded, at_0 = weights(0)
            before_up(0, loaded)
            up(0, 0, at_0, True)
            at = None, at_0
            for q in range(AHEAD):
                at = step(q, q, *at, first=True)
            with pe.Fori(0, (TILES // AHEAD - 2) // 2) as j:
                i = 2 * AHEAD * j + AHEAD
                at = weights(i - 1)[1], weights(i)[1]
                for q in range(2 * AHEAD):
                    at = step(i + q, q % AHEAD, *at)
            at = weights(TILES - AHEAD - 1)[1], weights(TILES - AHEAD)[1]
            for q in range(AHEAD):
                at = step(TILES - AHEAD + q, q, *at, more=AHEAD - 1 - q)
            down(TILES - 1, (AHEAD - 1) % 2, at[0])


def lay_out(inputs):
    g = {k: np.asarray(v) for k, v in inputs.items()}
    rows = lambda v: np.ascontiguousarray(np.broadcast_to(v[None, :], (P, D)))
    cols = lambda v: np.ascontiguousarray(v.reshape(KD, P).T)
    a = {
        "x_in": g["x"], "fside": g["fside_BxS2xS2_0"], "ctx_w": g["ctx_1024"],
        "wq": g["L0_attn_wq"], "bq": cols(g["L0_attn_bq"]), "wk": g["L0_attn_wk"], "bk": cols(g["L0_attn_bk"]),
        "wv": g["L0_attn_wv"], "bv": cols(g["L0_attn_bv"]), "wo": g["L0_attn_wo"], "bo": rows(g["L0_attn_bo"]),
        "wg": np.ascontiguousarray(g["L0_ffn_wg"].T), "w1": g["L0_ffn_w1"], "v1": g["L0_ffn_v1"], "w2": g["L0_ffn_w2"],
    }
    a.update(shape_constants())
    return a


def kernel(**inputs):
    import concourse.bacc as bacc
    from concourse.bass_utils import run_bass_kernel_spmd

    nc = bacc.Bacc("TRN2", target_bir_lowering=False, num_devices=1)
    arrays = lay_out(inputs)
    args = [nc.dram_tensor(name, a.shape, mybir.dt.from_np(a.dtype), kind="ExternalInput").ap() for name, a in arrays.items()]
    args.append(nc.dram_tensor("out", [TOK + P, D], F32, kind="ExternalOutput").ap())
    decoder_kernel(nc, *args)
    r = run_bass_kernel_spmd(nc, [arrays], core_ids=[0])
    return r.results[0]["out"][0:TOK].reshape(B, S, D)
```
